# Optimizing a Trainium2 kernel written in Bass

```python
import numpy as np
import jax
import jax.numpy as jnp

def _softmax(x, axis=-1):
    return jax.nn.softmax(x, axis=axis)

def _gelu(x):
    return jax.nn.gelu(x, approximate=True)

def _silu(x):
    return jax.nn.silu(x)

def _sigmoid(x):
    return jax.nn.sigmoid(x)

def _layernorm(x, axis=-1, eps=1e-05):
    m = jnp.mean(x, axis=axis, keepdims=True)
    v = jnp.var(x, axis=axis, keepdims=True)
    return (x - m) / jnp.sqrt(v + eps)

def _scatter_add(tgt, idx, src, axis=0):
    return tgt.at[idx].add(src)

def _segment_sum(src, seg, n):
    return jax.ops.segment_sum(src, seg, n)
kernel_name = 'mk_decoder_postln_d2_seqx_r4_d17843'

def setup_inputs(seed: int=0):
    np.random.seed(seed)
    _w = jnp.asarray

    def _rec_inputs():
        import jax
        import jax.numpy as jnp
        _rk = jax.random.key(seed)
        x = -0.0003929 + 0.9999 * jax.random.normal(jax.random.fold_in(_rk, 1), (4, 512, 256), jnp.float32)
        _lenS = 512 - jax.random.randint(jax.random.fold_in(_rk, 7), (4,), 0, max(1, 512 // 4) + 1, jnp.int32)
        _lenS2 = 1024 - jax.random.randint(jax.random.fold_in(_rk, 8), (4,), 0, max(1, 1024 // 4) + 1, jnp.int32)
        _ctx_1024P = jax.random.normal(jax.random.fold_in(_rk, 11), (4, 16, 256), jnp.float32)
        _ctx_1024c = jax.random.dirichlet(jax.random.fold_in(_rk, 511), 0.3 * jnp.ones((16,), jnp.float32), (4, 1024))
        _ctx_1024t = jnp.einsum('bsk,bkd->bsd', _ctx_1024c, _ctx_1024P)
        _ctx_1024t = _ctx_1024t * jax.lax.rsqrt(jnp.mean(jnp.square(_ctx_1024t)) + 1e-12) * 0.953939
        ctx_1024 = -0.000514642 + 1.00011 * (_ctx_1024t + 0.3 * jax.random.normal(jax.random.fold_in(_rk, 611), (4, 1024, 256), jnp.float32))
        itok_BxS_0_511 = jax.random.randint(jax.random.fold_in(_rk, 12), (4, 512), 0, 128, jnp.int32)
        _validS = jnp.arange(512)[None, :] < _lenS[:, None]
        _validS2 = jnp.arange(1024)[None, :] < _lenS2[:, None]
        _causal = jnp.tril(jnp.ones((512, 512), dtype=bool))
        mask_SxS2_fk1 = jnp.where(jnp.broadcast_to(_validS2[0:1, :], (512, 1024)), 1.0, 0.0).astype(jnp.float32)
        return (x, ctx_1024, itok_BxS_0_511, mask_SxS2_fk1)
    x, ctx_1024, itok_BxS_0_511, mask_SxS2_fk1 = _rec_inputs()

    def _L0_attn_setup():
        import jax, jax.numpy as jnp
        import numpy as np
        B, S, D_IN, D_OUT, H, WIN = (1, 1024, 256, 256, 16, 128)
        HD = D_OUT // H
        key = jax.random.key(seed)
        ks = jax.random.split(key, 6)
        sc_in = 1.0 / np.sqrt(D_IN)
        sc_out = 1.0 / np.sqrt(D_OUT)
        return {'x': jax.random.normal(ks[0], (B, S, D_IN), dtype=jnp.float32), 'Wq': jax.random.uniform(ks[1], (D_IN, D_OUT), jnp.float32, -sc_in, sc_in), 'Wk': jax.random.uniform(ks[2], (D_IN, D_OUT), jnp.float32, -sc_in, sc_in), 'Wv': jax.random.uniform(ks[3], (D_IN, D_OUT), jnp.float32, -sc_in, sc_in), 'Wo': jax.random.uniform(ks[4], (D_OUT, D_OUT), jnp.float32, -sc_out, sc_out), 'bo': jax.random.uniform(ks[5], (D_OUT,), jnp.float32, -sc_out, sc_out)}
    _L0_attn_all = _L0_attn_setup()
    _L0_attn_in = {k: v for k, v in _L0_attn_all.items() if k in ('Wq', 'Wk', 'Wv', 'Wo', 'bo')}
    del _L0_attn_all

    def _L0_xattn_setup():
        import jax, jax.numpy as jnp
        import numpy as np
        Q_DIM = 256
        KV_DIM = 256
        D_ATTN = 256
        N_HEADS = 16
        HDIM = D_ATTN // N_HEADS
        LOOKBACK = 3
        KW = LOOKBACK + 1
        SCALE = HDIM ** (-0.5)
        B, LQ, LKV = (4, 1024, 128)

        def _split_heads(x):
            b, l, _ = x.shape
            return x.reshape(b, l, N_HEADS, HDIM).transpose(0, 2, 1, 3)
        key = jax.random.key(seed)
        ks = jax.random.split(key, 6)
        q = jax.random.normal(ks[0], (B, LQ, Q_DIM), dtype=jnp.float32)
        kv_src = jax.random.normal(ks[1], (B, LKV, KV_DIM), dtype=jnp.float32)
        seg_id = jnp.sort(jax.random.randint(ks[2], (B, LQ), 0, LKV), axis=-1)
        Wq = jax.random.normal(ks[3], (D_ATTN, Q_DIM), dtype=jnp.float32) * Q_DIM ** (-0.5)
        Wkv = jax.random.normal(ks[4], (2 * D_ATTN, KV_DIM), dtype=jnp.float32) * KV_DIM ** (-0.5)
        Wo = jax.random.normal(ks[5], (Q_DIM, D_ATTN), dtype=jnp.float32) * D_ATTN ** (-0.5)
        return {'q': q, 'kv_src': kv_src, 'seg_id': seg_id, 'Wq': Wq, 'Wkv': Wkv, 'Wo': Wo}
    _L0_xattn_all = _L0_xattn_setup()
    _L0_xattn_in = {k: v for k, v in _L0_xattn_all.items() if k in ('Wq', 'Wkv', 'Wo')}
    del _L0_xattn_all

    def _L0_ffn_setup():
        import jax, jax.numpy as jnp
        import numpy as np
        import math
        D_IN = 256
        FEATURES = (1024, 1024, 256)
        BATCH, SEQ = (8, 512)

        def _conn_dense(kernel_bool, x):
            w = jnp.where(kernel_bool, jnp.float32(1.0), jnp.float32(-1.0))
            return x @ w
        key = jax.random.key(seed)
        kx, kk0, kk1, kk2 = jax.random.split(key, 4)
        x = jax.random.normal(kx, (BATCH, SEQ, D_IN), dtype=jnp.float32)
        k0 = jax.random.randint(kk0, (2 * D_IN, FEATURES[0]), 0, 2).astype(jnp.bool_)
        k1 = jax.random.randint(kk1, (FEATURES[0], FEATURES[1]), 0, 2).astype(jnp.bool_)
        k2 = jax.random.randint(kk2, (FEATURES[1], FEATURES[2]), 0, 2).astype(jnp.bool_)
        s0 = jnp.asarray(1.0 / math.sqrt(2 * D_IN), dtype=jnp.float32)
        s1 = jnp.asarray(1.0 / math.sqrt(FEATURES[0]), dtype=jnp.float32)
        s2 = jnp.asarray(1.0 / math.sqrt(FEATURES[1]), dtype=jnp.float32)
        return {'x': x, 'k0': k0, 'k1': k1, 'k2': k2, 's0': s0, 's1': s1, 's2': s2}
    _L0_ffn_all = _L0_ffn_setup()
    _L0_ffn_in = {k: v for k, v in _L0_ffn_all.items() if k in ('k0', 'k1', 'k2', 's0', 's1', 's2')}
    del _L0_ffn_all

    def _L1_attn_setup():
        import jax, jax.numpy as jnp
        import numpy as np
        D_MODEL, N_HEADS, D_HEAD = (256, 16, 64)
        QKV = N_HEADS * D_HEAD
        EPS = 1e-05

        def _layernorm(x, gamma, beta):
            mu = jnp.mean(x, axis=-1, keepdims=True)
            var = jnp.mean((x - mu) ** 2, axis=-1, keepdims=True)
            return (x - mu) * jax.lax.rsqrt(var + EPS) * gamma + beta
        key = jax.random.key(seed)
        ks = jax.random.split(key, 5)
        B, T = (1, 512)
        s_in = 1.0 / np.sqrt(D_MODEL)
        s_qkv = 1.0 / np.sqrt(QKV)
        return {'x': jax.random.normal(ks[0], (B, T, D_MODEL), dtype=jnp.float32), 'Wq': jax.random.normal(ks[1], (QKV, D_MODEL), dtype=jnp.float32) * s_in, 'Wk': jax.random.normal(ks[2], (QKV, D_MODEL), dtype=jnp.float32) * s_in, 'Wv': jax.random.normal(ks[3], (QKV, D_MODEL), dtype=jnp.float32) * s_in, 'Wo': jax.random.normal(ks[4], (D_MODEL, QKV), dtype=jnp.float32) * s_qkv, 'q_gamma': jnp.ones((D_HEAD,), dtype=jnp.float32), 'q_beta': jnp.zeros((D_HEAD,), dtype=jnp.float32), 'k_gamma': jnp.ones((D_HEAD,), dtype=jnp.float32), 'k_beta': jnp.zeros((D_HEAD,), dtype=jnp.float32)}
    _L1_attn_all = _L1_attn_setup()
    _L1_attn_in = {k: v for k, v in _L1_attn_all.items() if k in ('Wq', 'Wk', 'Wv', 'Wo', 'q_gamma', 'q_beta', 'k_gamma', 'k_beta')}
    del _L1_attn_all

    def _L1_xattn_setup():
        import jax, jax.numpy as jnp
        import numpy as np
        D_MODEL = 256
        NUM_HEADS = 16
        D_K = D_MODEL // NUM_HEADS
        B, S = (2, 512)
        NEG = -1000000000.0

        def _split_heads(x):
            b, s, _ = x.shape
            return x.reshape(b, s, NUM_HEADS, D_K).transpose(0, 2, 1, 3)
        key = jax.random.key(seed)
        ks = jax.random.split(key, 12)
        sc = 1.0 / np.sqrt(D_MODEL)
        inp = {'Q': jax.random.normal(ks[0], (B, S, D_MODEL), jnp.float32), 'K': jax.random.normal(ks[1], (B, S, D_MODEL), jnp.float32), 'V': jax.random.normal(ks[2], (B, S, D_MODEL), jnp.float32), 'mask': jnp.triu(jnp.ones((S, S), jnp.float32), k=1), 'Wq': jax.random.normal(ks[3], (D_MODEL, D_MODEL), jnp.float32) * sc, 'bq': jnp.zeros((D_MODEL,), jnp.float32), 'Wk': jax.random.normal(ks[4], (D_MODEL, D_MODEL), jnp.float32) * sc, 'bk': jnp.zeros((D_MODEL,), jnp.float32), 'Wv': jax.random.normal(ks[5], (D_MODEL, D_MODEL), jnp.float32) * sc, 'bv': jnp.zeros((D_MODEL,), jnp.float32), 'Wo': jax.random.normal(ks[6], (D_MODEL, D_MODEL), jnp.float32) * sc, 'bo': jnp.zeros((D_MODEL,), jnp.float32)}
        return inp
    _L1_xattn_all = _L1_xattn_setup()
    _L1_xattn_in = {k: v for k, v in _L1_xattn_all.items() if k in ('Wq', 'bq', 'Wk', 'bk', 'Wv', 'bv', 'Wo', 'bo')}
    del _L1_xattn_all

    def _L1_ffn_setup():
        import jax, jax.numpy as jnp
        import numpy as np
        B, S, H, E, K = (2, 256, 256, 8, 2)
        D = 2 * H
        key = jax.random.key(seed)
        ks = jax.random.split(key, 7)
        x = jax.random.normal(ks[0], (B, S, H), dtype=jnp.float32)
        Wr = jax.random.normal(ks[1], (H, E), dtype=jnp.float32) / np.sqrt(H)
        br = jnp.zeros((E,), dtype=jnp.float32)
        W1 = jax.random.normal(ks[2], (E, H, D), dtype=jnp.float32) / np.sqrt(H)
        b1 = jnp.zeros((E, D), dtype=jnp.float32)
        W2 = jax.random.normal(ks[3], (E, D, H), dtype=jnp.float32) / np.sqrt(D)
        b2 = jnp.zeros((E, H), dtype=jnp.float32)
        return {'x': x, 'Wr': Wr, 'br': br, 'W1': W1, 'b1': b1, 'W2': W2, 'b2': b2}
    _L1_ffn_all = _L1_ffn_setup()
    _L1_ffn_in = {k: v for k, v in _L1_ffn_all.items() if k in ('Wr', 'br', 'W1', 'b1', 'W2', 'b2')}
    del _L1_ffn_all
    return {'x': x, 'ctx_1024': ctx_1024, 'itok_BxS_0_511': itok_BxS_0_511, 'mask_SxS2_fk1': mask_SxS2_fk1, 'L0_attn_Wq': _L0_attn_in['Wq'], 'L0_attn_Wk': _L0_attn_in['Wk'], 'L0_attn_Wv': _L0_attn_in['Wv'], 'L0_attn_Wo': _L0_attn_in['Wo'], 'L0_attn_bo': _L0_attn_in['bo'], 'L0_xattn_Wq': _L0_xattn_in['Wq'], 'L0_xattn_Wkv': _L0_xattn_in['Wkv'], 'L0_xattn_Wo': _L0_xattn_in['Wo'], 'L0_ffn_k0': _L0_ffn_in['k0'], 'L0_ffn_k1': _L0_ffn_in['k1'], 'L0_ffn_k2': _L0_ffn_in['k2'], 'L0_ffn_s0': _L0_ffn_in['s0'], 'L0_ffn_s1': _L0_ffn_in['s1'], 'L0_ffn_s2': _L0_ffn_in['s2'], 'L1_attn_Wq': _L1_attn_in['Wq'], 'L1_attn_Wk': _L1_attn_in['Wk'], 'L1_attn_Wv': _L1_attn_in['Wv'], 'L1_attn_Wo': _L1_attn_in['Wo'], 'L1_attn_q_gamma': _L1_attn_in['q_gamma'], 'L1_attn_q_beta': _L1_attn_in['q_beta'], 'L1_attn_k_gamma': _L1_attn_in['k_gamma'], 'L1_attn_k_beta': _L1_attn_in['k_beta'], 'L1_xattn_Wq': _L1_xattn_in['Wq'], 'L1_xattn_bq': _L1_xattn_in['bq'], 'L1_xattn_Wk': _L1_xattn_in['Wk'], 'L1_xattn_bk': _L1_xattn_in['bk'], 'L1_xattn_Wv': _L1_xattn_in['Wv'], 'L1_xattn_bv': _L1_xattn_in['bv'], 'L1_xattn_Wo': _L1_xattn_in['Wo'], 'L1_xattn_bo': _L1_xattn_in['bo'], 'L1_ffn_Wr': _L1_ffn_in['Wr'], 'L1_ffn_br': _L1_ffn_in['br'], 'L1_ffn_W1': _L1_ffn_in['W1'], 'L1_ffn_b1': _L1_ffn_in['b1'], 'L1_ffn_W2': _L1_ffn_in['W2'], 'L1_ffn_b2': _L1_ffn_in['b2']}

def reference(x, ctx_1024, itok_BxS_0_511, mask_SxS2_fk1, L0_attn_Wq, L0_attn_Wk, L0_attn_Wv, L0_attn_Wo, L0_attn_bo, L0_xattn_Wq, L0_xattn_Wkv, L0_xattn_Wo, L0_ffn_k0, L0_ffn_k1, L0_ffn_k2, L0_ffn_s0, L0_ffn_s1, L0_ffn_s2, L1_attn_Wq, L1_attn_Wk, L1_attn_Wv, L1_attn_Wo, L1_attn_q_gamma, L1_attn_q_beta, L1_attn_k_gamma, L1_attn_k_beta, L1_xattn_Wq, L1_xattn_bq, L1_xattn_Wk, L1_xattn_bk, L1_xattn_Wv, L1_xattn_bv, L1_xattn_Wo, L1_xattn_bo, L1_ffn_Wr, L1_ffn_br, L1_ffn_W1, L1_ffn_b1, L1_ffn_W2, L1_ffn_b2):
    import jax
    import jax.numpy as jnp

    def _L0_attn_ref(x, Wq, Wk, Wv, Wo, bo):
        import jax, jax.numpy as jnp
        import numpy as np
        B, S, D_IN, D_OUT, H, WIN = (1, 1024, 256, 256, 16, 128)
        HD = D_OUT // H
        b, s, _ = x.shape
        q = (x @ Wq).reshape(b, s, H, HD).transpose(0, 2, 1, 3)
        k = (x @ Wk).reshape(b, s, H, HD).transpose(0, 2, 1, 3)
        v = (x @ Wv).reshape(b, s, H, HD).transpose(0, 2, 1, 3)
        scores = jnp.einsum('bhqd,bhkd->bhqk', q, k)
        pos = jnp.arange(s)
        diff = pos[:, None] - pos[None, :]
        mask = (diff < 0) | (diff >= WIN)
        scores = jnp.where(mask, -jnp.inf, scores)
        attn = jax.nn.softmax(scores / np.sqrt(HD), axis=-1)
        ctx = jnp.einsum('bhqk,bhkd->bhqd', attn, v)
        ctx = ctx.transpose(0, 2, 1, 3).reshape(b, s, D_OUT)
        return ctx @ Wo + bo

    def _L0_xattn_ref(q, kv_src, seg_id, Wq, Wkv, Wo):
        import jax, jax.numpy as jnp
        import numpy as np
        Q_DIM = 256
        KV_DIM = 256
        D_ATTN = 256
        N_HEADS = 16
        HDIM = D_ATTN // N_HEADS
        LOOKBACK = 3
        KW = LOOKBACK + 1
        SCALE = HDIM ** (-0.5)
        B, LQ, LKV = (4, 1024, 128)

        def _split_heads(x):
            b, l, _ = x.shape
            return x.reshape(b, l, N_HEADS, HDIM).transpose(0, 2, 1, 3)
        b, lq, _ = q.shape
        lkv = kv_src.shape[1]
        qh = _split_heads(q @ Wq.T)
        kv = kv_src @ Wkv.T
        k, v = jnp.split(kv, 2, axis=-1)
        kh = _split_heads(k)
        vh = _split_heads(v)
        offsets = jnp.arange(KW)
        gather = seg_id[:, :, None] - offsets
        neg_mask = gather < 0
        gc = jnp.clip(gather, 0, lkv - 1)
        b_idx = jnp.arange(b)[:, None, None]
        k_sel = kh[b_idx, :, gc].transpose(0, 3, 1, 2, 4)
        v_sel = vh[b_idx, :, gc].transpose(0, 3, 1, 2, 4)
        scores = jnp.einsum('bhqd,bhqkd->bhqk', qh, k_sel) * SCALE
        neg_inf = jnp.finfo(scores.dtype).min
        scores = jnp.where(neg_mask[:, None, :, :], neg_inf, scores)
        probs = jax.nn.softmax(scores, axis=-1)
        out = jnp.einsum('bhqk,bhqkd->bhqd', probs, v_sel)
        out = out.transpose(0, 2, 1, 3).reshape(b, lq, D_ATTN)
        return out @ Wo.T

    def _L0_ffn_ref(x, k0, k1, k2, s0, s1, s2):
        import jax, jax.numpy as jnp
        import numpy as np
        import math
        D_IN = 256
        FEATURES = (1024, 1024, 256)
        BATCH, SEQ = (8, 512)

        def _conn_dense(kernel_bool, x):
            w = jnp.where(kernel_bool, jnp.float32(1.0), jnp.float32(-1.0))
            return x @ w
        h = jnp.concatenate([x, -x], axis=-1)
        h = s0 * _conn_dense(k0, h)
        h = jax.nn.relu(h) * 2
        h = s1 * _conn_dense(k1, h)
        h = jax.nn.relu(h) * 2
        h = s2 * _conn_dense(k2, h)
        return h

    def _L1_attn_ref(x, Wq, Wk, Wv, Wo, q_gamma, q_beta, k_gamma, k_beta):
        import jax, jax.numpy as jnp
        import numpy as np
        D_MODEL, N_HEADS, D_HEAD = (256, 16, 64)
        QKV = N_HEADS * D_HEAD
        EPS = 1e-05

        def _layernorm(x, gamma, beta):
            mu = jnp.mean(x, axis=-1, keepdims=True)
            var = jnp.mean((x - mu) ** 2, axis=-1, keepdims=True)
            return (x - mu) * jax.lax.rsqrt(var + EPS) * gamma + beta
        B, T, _ = x.shape

        def split_heads(y):
            return y.reshape(B, T, N_HEADS, D_HEAD).transpose(0, 2, 1, 3)
        q = split_heads(x @ Wq.T)
        k = split_heads(x @ Wk.T)
        v = split_heads(x @ Wv.T)
        q = _layernorm(q, q_gamma, q_beta)
        k = _layernorm(k, k_gamma, k_beta)
        kv = k[..., :, None] * v[..., None, :]
        S = jnp.cumsum(kv, axis=2)
        o = jnp.einsum('bhtd,bhtde->bhte', q, S)
        o = o.transpose(0, 2, 1, 3).reshape(B, T, QKV)
        return o @ Wo.T

    def _L1_xattn_ref(Q, K, V, mask, Wq, bq, Wk, bk, Wv, bv, Wo, bo):
        import jax, jax.numpy as jnp
        import numpy as np
        D_MODEL = 256
        NUM_HEADS = 16
        D_K = D_MODEL // NUM_HEADS
        B, S = (2, 512)
        NEG = -1000000000.0

        def _split_heads(x):
            b, s, _ = x.shape
            return x.reshape(b, s, NUM_HEADS, D_K).transpose(0, 2, 1, 3)
        q = _split_heads(Q @ Wq.T + bq)
        k = _split_heads(K @ Wk.T + bk)
        v = _split_heads(V @ Wv.T + bv)
        scores = jnp.einsum('bhqd,bhkd->bhqk', q, k) / np.sqrt(D_K)
        scores = scores + mask * NEG
        probs = jax.nn.softmax(scores, axis=-1)
        attn = jnp.einsum('bhqk,bhkd->bhqd', probs, v)
        attn = attn.transpose(0, 2, 1, 3).reshape(Q.shape[0], Q.shape[1], D_MODEL)
        return attn @ Wo.T + bo

    def _L1_ffn_ref(x, Wr, br, W1, b1, W2, b2):
        import jax, jax.numpy as jnp
        import numpy as np
        B, S, H, E, K = (2, 256, 256, 8, 2)
        D = 2 * H
        logits = jnp.einsum('bsh,he->bse', x, Wr) + br
        probs = jax.nn.softmax(logits, axis=-1)
        top_p, top_i = jax.lax.top_k(probs, K)
        cw = jnp.sum(jax.nn.one_hot(top_i, E, dtype=x.dtype) * top_p[..., None], axis=-2)
        h = jax.nn.relu(jnp.einsum('bsh,ehd->bsed', x, W1) + b1)
        y = jnp.einsum('bsed,edh->bseh', h, W2) + b2
        out = jnp.einsum('bseh,bse->bsh', y, cw)
        return out
    x = _layernorm(x + _L0_attn_ref(x, L0_attn_Wq, L0_attn_Wk, L0_attn_Wv, L0_attn_Wo, L0_attn_bo), axis=-1)
    x = _layernorm(x + _L0_xattn_ref(x, ctx_1024, itok_BxS_0_511, L0_xattn_Wq, L0_xattn_Wkv, L0_xattn_Wo), axis=-1)
    x = _layernorm(x + _L0_ffn_ref(x, L0_ffn_k0, L0_ffn_k1, L0_ffn_k2, L0_ffn_s0, L0_ffn_s1, L0_ffn_s2), axis=-1)
    x = _layernorm(x + _L1_attn_ref(x, L1_attn_Wq, L1_attn_Wk, L1_attn_Wv, L1_attn_Wo, L1_attn_q_gamma, L1_attn_q_beta, L1_attn_k_gamma, L1_attn_k_beta), axis=-1)
    x = _layernorm(x + _L1_xattn_ref(x, ctx_1024, ctx_1024, mask_SxS2_fk1, L1_xattn_Wq, L1_xattn_bq, L1_xattn_Wk, L1_xattn_bk, L1_xattn_Wv, L1_xattn_bv, L1_xattn_Wo, L1_xattn_bo), axis=-1)
    x = _layernorm(x + _L1_ffn_ref(x, L1_ffn_Wr, L1_ffn_br, L1_ffn_W1, L1_ffn_b1, L1_ffn_W2, L1_ffn_b2), axis=-1)
    return x

_drawn_inputs = setup_inputs


def setup_inputs(seed=0):
    import zlib

    import numpy as np

    out = dict(_drawn_inputs(seed))
    spreads = {'L1_attn_q_gamma': (1.0, 0.2),
     'L1_attn_q_beta': (0.0, 0.1),
     'L1_attn_k_gamma': (1.0, 0.2),
     'L1_attn_k_beta': (0.0, 0.1),
     'L1_xattn_bq': (0.0, 0.276),
     'L1_xattn_bk': (0.0, 0.8),
     'L1_xattn_bv': (0.0, 0.1),
     'L1_xattn_bo': (0.0, 0.1),
     'L1_ffn_br': (0.0, 0.1),
     'L1_ffn_b1': (0.0, 0.293),
     'L1_ffn_b2': (0.0, 0.1)}
    factors = {'L0_attn_Wq': 2.899}
    for name, (base, spread) in spreads.items():
        noise = np.random.default_rng([zlib.crc32(name.encode()), seed]).standard_normal(out[name].shape)
        drawn = base * np.exp(spread * noise) if base else spread * noise
        out[name] = jnp.asarray(drawn.astype(out[name].dtype))
    for name, factor in factors.items():
        out[name] = (out[name] * factor).astype(out[name].dtype)
    return out
```

```python
from contextlib import ExitStack

import numpy as np

import concourse.bass as bass
from concourse import mybir

F32 = mybir.dt.float32
F32R = mybir.dt.float32r
I32 = mybir.dt.int32
U8 = mybir.dt.uint8
ALU = mybir.AluOpType
ACT = mybir.ActivationFunctionType
AX = mybir.AxisListType

P = 128
B, S, D = 4, 512, 256
SC = 1024
T, KD, CT = S // P, D // P, SC // P
H, HD = 16, D // 16
PADW = 32
G = H * PADW // P
WIN = 128
NOFF = 4
LH = 64
LD = H * LH
LM = LD // P
F = 1024
FM = F // P
E, ED = 8, 512
EM = ED // P
EPS = 1e-5
NEG = -1.0e9
LOWEST = float(np.finfo(np.float32).min)
FAR = -1.0e30


class Stage:

    def __init__(self, nc, name):
        self.nc, self.name, self.ctx, self.sems = nc, name, ExitStack(), []

    def __enter__(self):
        return self

    def sem(self, name):
        s = self.ctx.enter_context(self.nc.semaphore(f"{self.name}_{name}"))
        self.sems.append(s)
        return s

    def sb(self, name, shape, dt=F32):
        return self.ctx.enter_context(self.nc.sbuf_tensor(f"{self.name}_{name}", shape, dt))

    def __exit__(self, *exc):
        if exc[0] is None:
            nums = [s.num for s in self.sems]
            if nums:
                self.nc.all_engine_barrier(sems_to_clear=range(min(nums), max(nums) + 1))
        return self.ctx.__exit__(*exc)


class Chain:

    def __init__(self, eng, sem):
        self.eng, self.sem, self.n = eng, sem, 0

    def __call__(self, ins):
        self.n += 1
        ins.then_inc(self.sem, 1)
        self.eng.wait_ge(self.sem, self.n)


class Buffers:
    pass


def decoder(nc, a, out, n_batches=B, last_stage=99):
    top = ExitStack()

    def sb(name, shape, dt=F32):
        return top.enter_context(nc.sbuf_tensor(name, shape, dt))

    L = Buffers()
    L.kv_table = nc.dram_tensor("kv_table", [SC, 2 * D], F32).ap()

    L.PS = top.enter_context(nc.psum_tensor("PS", [P, 8 * 512], F32))

    L.ident = sb("ident", [P, P])
    L.ones = sb("ones", [1, P])
    L.eps = sb("eps", [P, 1])
    L.window = sb("window", [P, 2 * P])
    L.causal = sb("causal", [P, S])
    L.head_mean = sb("head_mean", [P, P])
    L.a0q = sb("a0q", [P, KD, G * P])
    L.a0k = sb("a0k", [P, KD, G * P])
    L.a0v = sb("a0v", [P, KD, D])
    L.a0o = sb("a0o", [P, KD, D])
    L.a0bo = sb("a0bo", [1, D])
    L.x0q = sb("x0q", [P, KD, D])
    L.x0kv = sb("x0kv", [P, KD, 2 * D])
    L.x0o = sb("x0o", [P, KD, D])
    L.k0_words, L.k1_words, L.k2_words = (sb(n, [P, r, c // 4], I32) for n, r, c in (("k0", 2 * KD, F), ("k1", FM, F), ("k2", FM, D)))
    L.k0, L.k1, L.k2 = (w[:, :, :].bitcast(U8) for w in (L.k0_words, L.k1_words, L.k2_words))
    L.scales = sb("scales", [P, 4])
    L.a1q = sb("a1q", [P, KD, LD])
    L.a1k = sb("a1k", [P, KD, LD])
    L.a1v = sb("a1v", [P, KD, LD])
    L.a1o = sb("a1o", [P, LM, D])
    L.gains = sb("gains", [P, 4])
    L.x1q = sb("x1q", [P, KD, G * P])
    L.x1k = sb("x1k", [P, KD, G * P])
    L.x1v = sb("x1v", [P, KD, D])
    L.x1o = sb("x1o", [P, KD, D])
    L.x1bqk = sb("x1bqk", [P, 2, G])
    L.x1bv = sb("x1bv", [1, D])
    L.x1bo = sb("x1bo", [1, D])
    L.wr = sb("wr", [P, KD, E])
    L.br = sb("br", [1, E])
    L.b1 = sb("b1", [P, E * EM])
    L.b2 = sb("b2", [E, D])
    L.x_tok = sb("x_tok", [P, T, D])
    L.x_T = sb("x_T", [P, KD, S])
    L.ctx_T = sb("ctx_T", [P, KD, SC])
    L.mixed = sb("mixed", [P, T, D])

    setup(nc, a, L)

    with nc.Fori(0, n_batches) as b:
        load_batch(nc, a, b, L)
        with Stage(nc, "gat") as gs:
            context_table(nc, a, b, gs, L)
            window_attention(nc, gs, L)
            if last_stage >= 1:
                project_norm(nc, "a0p", L, L.a0o, L.a0bo)
            if last_stage >= 3:
                gather_attention(nc, gs, L)
        if last_stage >= 3:
            project_norm(nc, "x0p", L, L.x0o, None)
        if last_stage >= 4:
            sign_ffn(nc, L)
        if last_stage >= 5:
            linear_attention(nc, L)
        if last_stage >= 6:
            cross_attention(nc, a, L)
            project_norm(nc, "x1p", L, L.x1o, L.x1bo)
        if last_stage >= 7:
            experts(nc, a, L)
        store_batch(nc, b, out, L.x_tok)
    top.close()


def setup(nc, a, L):
    with Stage(nc, "set") as st:
        loads = [0]
        loaded, memset, piece = st.sem("loaded"), st.sem("memset"), st.sem("const")
        turned, copied_v, copied_s = st.sem("turned"), st.sem("copied_v"), st.sem("copied_s")
        vec = st.sem("vec")
        raw = {}
        for n, rows in (("L0_xattn_Wq", 2), ("L0_xattn_Wkv", 4), ("L0_xattn_Wo", 2), ("L1_attn_Wq", 8),
                        ("L1_attn_Wk", 8), ("L1_attn_Wv", 8), ("L1_xattn_Wq", 2), ("L1_xattn_Wk", 2),
                        ("L1_xattn_Wv", 2), ("L1_xattn_Wo", 2)):
            raw[n] = st.sb(n, [P, rows, D])
        raw["L1_attn_Wo"] = st.sb("L1_attn_Wo", [P, KD, LD])
        plain_q, plain_k = st.sb("plain_q", [P, KD, D]), st.sb("plain_k", [P, KD, D])
        mean = st.sb("mean", [P, KD * H])
        b1_rows = st.sb("b1_rows", [E * EM, P])

        jobs = []
        for n, dst, padded in (("L0_xattn_Wq", L.x0q, 0), ("L0_xattn_Wkv", L.x0kv, 0),
                               ("L0_xattn_Wo", L.x0o, 0), ("L1_attn_Wq", L.a1q, 0), ("L1_attn_Wk", L.a1k, 0),
                               ("L1_attn_Wv", L.a1v, 0), ("L1_xattn_Wq", L.x1q, 1), ("L1_xattn_Wk", L.x1k, 1),
                               ("L1_xattn_Wv", L.x1v, 0), ("L1_xattn_Wo", L.x1o, 0)):
            for r in range(raw[n].shape[1]):
                pair = [raw[n][:, r, k * P:(k + 1) * P] for k in range(KD)]
                if padded:
                    to = dst[:, :, 2 * r * P:2 * (r + 1) * P].rearrange("p k (h w) -> p k h w", w=PADW)[:, :, :, 0:HD]
                else:
                    to = dst[:, :, r * P:(r + 1) * P]
                jobs.append((pair, to, padded))
        for r in range(KD):
            for c in range(0, LM, 2):
                pair = [raw["L1_attn_Wo"][:, r, (c + k) * P:(c + k + 1) * P] for k in range(2)]
                jobs.append((pair, L.a1o[:, c:c + 2, r * P:(r + 1) * P], 0))

        direct = [(raw[n][:, :, :], a[n].rearrange("(r p) n -> p r n", p=P)) for n in raw]
        direct += [
            (plain_q[:, :, :], a["L0_attn_Wq"].rearrange("(k p) n -> p k n", p=P)),
            (plain_k[:, :, :], a["L0_attn_Wk"].rearrange("(k p) n -> p k n", p=P)),
            (L.a0v[:, :, :], a["L0_attn_Wv"].rearrange("(k p) n -> p k n", p=P)),
            (L.a0o[:, :, :], a["L0_attn_Wo"].rearrange("(k p) n -> p k n", p=P)),
            (L.a0bo[:, :], a["L0_attn_bo"].rearrange("(a n) -> a n", a=1)),
            (L.k0_words[:, :, :], a["L0_ffn_k0"].rearrange("(k p) n -> p k n", p=P)),
            (L.k1_words[:, :, :], a["L0_ffn_k1"].rearrange("(k p) n -> p k n", p=P)),
            (L.k2_words[:, :, :], a["L0_ffn_k2"].rearrange("(k p) n -> p k n", p=P)),
            (L.x1bv[:, :], a["L1_xattn_bv"].rearrange("(a n) -> a n", a=1)),
            (L.x1bo[:, :], a["L1_xattn_bo"].rearrange("(a n) -> a n", a=1)),
            (L.wr[:, :, :], a["L1_ffn_Wr"].rearrange("(k p) n -> p k n", p=P)),
            (L.br[:, :], a["L1_ffn_br"].rearrange("(a n) -> a n", a=1)),
            (b1_rows[:, :], a["L1_ffn_b1"].rearrange("e (m p) -> (e m) p", p=P)),
            (L.b2[:, :], a["L1_ffn_b2"]),
        ]
        for i in range(3):
            direct.append((L.scales[:, i:i + 1], a[f"L0_ffn_s{i}"].rearrange("(a n) -> a n", a=1).to_broadcast((P, 1))))
        for i, n in enumerate(("q_gamma", "q_beta", "k_gamma", "k_beta")):
            for j in range(2):
                direct.append((L.gains[j * LH:(j + 1) * LH, i:i + 1], a[f"L1_attn_{n}"].rearrange("(n a) -> n a", a=1)))
        biases = []
        for i, n in enumerate(("L1_xattn_bq", "L1_xattn_bk")):
            for j in range(P // PADW):
                src = a[n].rearrange("(g j d) -> j d g", j=P // PADW, d=HD)[j]
                biases.append((L.x1bqk[j * PADW:j * PADW + HD, i, :], src))

        small = nc.allow_non_contiguous_dma("biases and gains, a few hundred words each")
        with small, nc.Block("setup") as block:
            @block.sync
            def _(sp):
                for dst, src in direct[:len(direct) // 2]:
                    sp.dma_start(dst, src).then_inc(loaded, 16)
                sp.wait_ge(memset, 6)
                for dst, src in biases:
                    sp.dma_start(dst, src).then_inc(loaded, 16)
                sp.wait_ge(loaded, 16 * (len(direct) + len(biases)))

            @block.gpsimd
            def _(pool):
                nc.gpsimd.memset(L.ident[:, :], 0.0).then_inc(piece, 1)
                nc.gpsimd.memset(L.window[:, :], 0.0).then_inc(piece, 1)
                nc.gpsimd.memset(L.causal[:, :], 1.0).then_inc(piece, 1)
                nc.gpsimd.memset(L.ones[:, :], 1.0).then_inc(piece, 1)
                nc.gpsimd.memset(L.eps[:, :], EPS).then_inc(piece, 1)
                pool.wait_ge(piece, 5)
                nc.gpsimd.affine_select(out=L.ident[:, :], in_=L.ident[:, :], compare_op=ALU.not_equal, fill=1.0,
                                        base=0, pattern=[[-1, P]], channel_multiplier=1).then_inc(piece, 1)
                nc.gpsimd.affine_select(out=L.window[:, :], in_=L.window[:, :], compare_op=ALU.is_gt, fill=FAR,
                                        base=0, pattern=[[1, 2 * P]], channel_multiplier=-1).then_inc(piece, 1)
                nc.gpsimd.affine_select(out=L.causal[:, :], in_=L.causal[:, :], compare_op=ALU.is_ge, fill=0.0,
                                        base=0, pattern=[[1, S]], channel_multiplier=-1).then_inc(piece, 1)
                pool.wait_ge(piece, 8)
                nc.gpsimd.affine_select(out=L.window[:, :], in_=L.window[:, :], compare_op=ALU.is_ge, fill=FAR,
                                        base=P, pattern=[[-1, 2 * P]], channel_multiplier=1).then_inc(piece, 1)
                pool.wait_ge(piece, 9)

            @block.tensor
            def _(pe):
                pe.wait_ge(loaded, 16 * (len(direct) + len(biases)))
                pe.wait_ge(piece, 8)
                for n, (pair, _, _) in enumerate(jobs):
                    if n >= 4:
                        pe.wait_ge(copied_v if n % 2 == 0 else copied_s, (n - 4) // 2 + 1)
                    for k, src in enumerate(pair):
                        last = nc.tensor.transpose(bank_of(L, n % 4)[:, k * P:(k + 1) * P], src, L.ident[:, :])
                    last.then_inc(turned, 1)
                nc.tensor.transpose(bank_of(L, 4, E * EM), b1_rows[:, :], L.ident[0:E * EM, 0:E * EM]).then_inc(turned, 1)

            @block.scalar
            def _(act):
                for dst, src in direct[len(direct) // 2:]:
                    act.dma_start(dst, src).then_inc(loaded, 16)
                act.wait_ge(memset, 6)
                for n, (_, to, padded) in enumerate(jobs):
                    if n % 2:
                        act.wait_ge(turned, n + 1)
                        src = bank_of(L, n % 4)[:, 0:2 * P].rearrange("p (k n) -> p k n", k=2)
                        if padded:
                            src = src.rearrange("p k (h d) -> p k h d", d=HD)
                        nc.scalar.copy(to, src).then_inc(copied_s, 1)

            @block.vector
            def _(dve):
                step = Chain(dve, vec)
                for t in (L.a0q, L.a0k, L.x1q, L.x1k, L.x1bqk):
                    nc.vector.memset(t[:, :, :], 0.0).then_inc(memset, 1)
                nc.vector.memset(L.head_mean[:, :], 0.0).then_inc(memset, 1)
                dve.wait_ge(memset, 6)
                for j in range(2):
                    step(nc.vector.memset(L.head_mean[j * LH:(j + 1) * LH, j * LH:(j + 1) * LH], 1.0 / LH))
                dve.wait_ge(loaded, 16 * (len(direct) + len(biases)))
                for dst, src in ((L.a0q, plain_q), (L.a0k, plain_k)):
                    step(nc.vector.tensor_copy(
                        dst[:, :, :].rearrange("p k (h w) -> p k h w", w=PADW)[:, :, :, 0:HD],
                        src[:, :, :].rearrange("p k (h d) -> p k h d", d=HD)))
                step(nc.vector.tensor_scalar(L.scales[:, 0:2], L.scales[:, 0:2], 2.0, None, ALU.mult))
                step(nc.vector.tensor_scalar(L.x1bqk[:, 0, :], L.x1bqk[:, 0, :], HD ** -0.5, None, ALU.mult))
                for n, (_, to, padded) in enumerate(jobs):
                    if n % 2 == 0:
                        dve.wait_ge(turned, n + 1)
                        src = bank_of(L, n % 4)[:, 0:2 * P].rearrange("p (k n) -> p k n", k=2)
                        if padded:
                            src = src.rearrange("p k (h d) -> p k h d", d=HD)
                        nc.vector.tensor_copy(to, src).then_inc(copied_v, 1)
                dve.wait_ge(turned, len(jobs) + 1)
                step(nc.vector.tensor_copy(L.b1[:, :], bank_of(L, 4, E * EM)))
                dve.wait_ge(copied_v, (len(jobs) + 1) // 2)
                dve.wait_ge(copied_s, len(jobs) // 2)
                for w in (L.a1q, L.a1k):
                    heads = w[:, :, :].rearrange("p k (h d) -> p (k h) d", d=LH)
                    step(nc.vector.tensor_reduce(mean[:, :], heads, AX.X, ALU.add))
                    step(nc.vector.tensor_scalar(mean[:, :], mean[:, :], 1.0 / LH, None, ALU.mult))
                    step(nc.vector.tensor_tensor(heads, heads, mean[:, :].rearrange("p (h a) -> p h a", a=1).to_broadcast((P, KD * H, LH)), ALU.subtract))


def bank_of(L, i, n=512):
    return L.PS[:, i * 512:i * 512 + n]


def load_batch(nc, a, b, L):
    with Stage(nc, "load") as st:
        ctx = st.sb("ctx", [P, CT, D])
        x_in, ctx_in, turned, cv, cs = (st.sem(n) for n in ("x_in", "ctx_in", "turned", "copied_v", "copied_s"))
        jobs = [([L.x_tok[:, t, k * P:(k + 1) * P] for k in range(KD)], L.x_T[:, :, t * P:(t + 1) * P]) for t in range(T)]
        jobs += [([ctx[:, t, k * P:(k + 1) * P] for k in range(KD)], L.ctx_T[:, :, t * P:(t + 1) * P]) for t in range(CT)]
        with nc.Block("load_batch") as block:
            @block.sync
            def _(sp):
                sp.dma_start(L.x_tok[:, :, :], a["x"][bass.ds(b, 1), :, :].rearrange("a (t p) d -> p (a t) d", p=P)).then_inc(x_in, 16)

            @block.tensor
            def _(pe):
                pe.wait_ge(x_in, 16)
                for n, (pair, _) in enumerate(jobs):
                    if n == T:
                        pe.wait_ge(ctx_in, 16)
                    if n >= 4:
                        pe.wait_ge(cs if n % 2 else cv, (n - 4) // 2 + 1)
                    for k, src in enumerate(pair):
                        last = nc.tensor.transpose(bank_of(L, n % 4)[:, k * P:(k + 1) * P], src, L.ident[:, :])
                    last.then_inc(turned, 1)

            @block.scalar
            def _(act):
                act.dma_start(ctx[:, :, :], a["ctx_1024"][bass.ds(b, 1), :, :].rearrange("a (t p) d -> p (a t) d", p=P)).then_inc(ctx_in, 16)
                for n, (_, to) in enumerate(jobs):
                    if n % 2:
                        act.wait_ge(turned, n + 1)
                        nc.scalar.copy(to, bank_of(L, n % 4, 2 * P).rearrange("p (k n) -> p k n", k=2)).then_inc(cs, 1)

            @block.vector
            def _(dve):
                for n, (_, to) in enumerate(jobs):
                    if n % 2 == 0:
                        dve.wait_ge(turned, n + 1)
                        nc.vector.tensor_copy(to, bank_of(L, n % 4, 2 * P).rearrange("p (k n) -> p k n", k=2)).then_inc(cv, 1)


def store_batch(nc, b, out, x_tok):
    with Stage(nc, "store") as st:
        stored = st.sem("stored")
        with nc.Block("store_batch") as block:
            @block.sync
            def _(sp):
                sp.dma_start(out[bass.ds(b, 1), :, :].rearrange("a (t p) d -> p (a t) d", p=P), x_tok[:, :, :]).then_inc(stored, 16)
                sp.wait_ge(stored, 16)


def context_table(nc, a, b, gs, L):
    gs.selected = gs.sb("selected", [P, T, NOFF, 2 * D])
    gs.rows = gs.sb("rows", [P, NOFF, T], I32)
    gs.keep = gs.sb("keep", [P, T, NOFF])
    gs.lowest = gs.sb("lowest", [P, T, NOFF])
    gs.rows_done = gs.sem("rows_done")
    gs.gathered = [[gs.sem(f"gathered{t}_{o}") for o in range(NOFF)] for t in range(T)]
    with Stage(nc, "tab") as st:
        kv = st.sb("kv", [P, CT, 2 * D])
        tok = st.sb("tok", [P, T], I32)
        tokf = st.sb("tokf", [P, T])
        shifted = st.sb("shifted", [P, T, NOFF])
        tok_in, made, cv, cs, written, vec = (st.sem(n) for n in ("tok_in", "made", "copied_v", "copied_s", "written", "vec"))
        with nc.Block("table") as block:
            @block.sync
            def _(sp):
                with nc.allow_non_contiguous_dma("token numbers, 2 KB"):
                    sp.dma_start(tok[:, :], a["itok_BxS_0_511"][bass.ds(b, 1), :].rearrange("a (t p) -> p (a t)", p=P)).then_inc(tok_in, 16)
                for n in range(CT):
                    sp.wait_ge(cs if n % 2 else cv, n // 2 + 1)
                    sp.dma_start(L.kv_table[n * P:(n + 1) * P, :], kv[:, n, :]).then_inc(written, 16)
                sp.wait_ge(written, 16 * CT)

            @block.tensor
            def _(pe):
                for n in range(CT):
                    if n >= 4:
                        pe.wait_ge(cs if n % 2 else cv, (n - 4) // 2 + 1)
                    for k in range(KD):
                        last = nc.tensor.matmul(bank_of(L, n % 4), L.ctx_T[:, k, n * P:(n + 1) * P], L.x0kv[:, k, :],
                                                start=(k == 0), stop=(k == KD - 1))
                    last.then_inc(made, 1)

            @block.scalar
            def _(act):
                for n in range(1, CT, 2):
                    act.wait_ge(made, n + 1)
                    nc.scalar.copy(kv[:, n, :], bank_of(L, n % 4)).then_inc(cs, 1)

            @block.vector
            def _(dve):
                step = Chain(dve, vec)
                for n in range(0, CT, 2):
                    dve.wait_ge(made, n + 1)
                    nc.vector.tensor_copy(kv[:, n, :], bank_of(L, n % 4)).then_inc(cv, 1)
                dve.wait_ge(tok_in, 16)
                step(nc.vector.tensor_copy(tokf[:, :], tok[:, :]))
                for o in range(NOFF):
                    step(nc.vector.tensor_scalar(shifted[:, :, o], tokf[:, :], float(-o), None, ALU.add))
                step(nc.vector.tensor_scalar(gs.keep[:, :, :], shifted[:, :, :], 0.0, None, ALU.is_ge))
                step(nc.vector.tensor_scalar(gs.lowest[:, :, :], shifted[:, :, :], 0.0, LOWEST, ALU.is_lt, ALU.mult))
                nc.vector.tensor_scalar(gs.rows[:, :, :].rearrange("p o t -> p t o"), shifted[:, :, :], 0.0, float(SC - 1),
                                        ALU.max, ALU.min).then_inc(gs.rows_done, 1)


def window_attention(nc, gs, L):
    NU = T * 2 * G
    units = [(t, gp, j) for t in range(T) for gp in range(G // 2) for j in range(4)]
    with Stage(nc, "win") as st:
        qT, kT = st.sb("qT", [P, G, S]), st.sb("kT", [P, G, S])
        v = st.sb("v", [P, T, D])
        sc = st.sb("sc", [P, 2, 2, 2 * P])
        pr = st.sb("pr", [P, 3, 2, 2 * P])
        pT = st.sb("pT", [P, 2, 4, P])
        mx = st.sb("mx", [P, NU, 2])
        nmx = st.sb("nmx", [P, NU, 2])
        den = st.sb("den", [P, T, H])
        rden = st.sb("rden", [P, T, H])
        names = ("made", "qkv_v", "qkv_s", "scored", "masked", "bias", "exped", "turned", "pT_v", "pT_s", "summed", "normed", "vec")
        made, qkv_v, qkv_s, scored, masked, bias, exped, turned, pT_v, pT_s, summed, normed, vec = (st.sem(n) for n in names)
        proj = [("q", g) for g in range(G)] + [("k", g) for g in range(G)] + [("v", t) for t in range(T)]

        def width(t):
            return P if t == 0 else 2 * P

        with nc.Block("window") as block:
            def evac(copy, eng, u, done):
                nb = width(units[u][0]) // P
                eng.wait_ge(turned, u + 1)
                if u >= 2:
                    eng.wait_ge(summed, u - 1)
                copy(pT[:, u % 2, 0:2 * nb, :], bank_of(L, 4 + u % 2, 2 * nb * P).rearrange("p (c n) -> p c n", n=P)).then_inc(done, 1)

            @block.gpsimd
            def _(pool):
                pool.wait_ge(gs.rows_done, 1)
                for t in range(T):
                    for o in range(NOFF):
                        nc.gpsimd.indirect_dma_start(
                            out=gs.selected[:, t, o, :], out_offset=None, in_=L.kv_table,
                            in_offset=bass.IndirectOffsetOnAxis(ap=gs.rows[:, o, t:t + 1], axis=0)).then_inc(gs.gathered[t][o], 16)

            @block.tensor
            def _(pe):
                for n, (what, i) in enumerate(proj):
                    if n >= 4:
                        pe.wait_ge(qkv_s if n % 2 else qkv_v, (n - 4) // 2 + 1)
                    for k in range(KD):
                        if what == "v":
                            lhs, rhs, o = L.x_T[:, k, i * P:(i + 1) * P], L.a0v[:, k, :], bank_of(L, n % 4, D)
                        else:
                            w = L.a0q if what == "q" else L.a0k
                            lhs, rhs, o = w[:, k, i * P:(i + 1) * P], L.x_T[:, k, :], bank_of(L, n % 4)
                        last = nc.tensor.matmul(o, lhs, rhs, start=(k == 0), stop=(k == KD - 1))
                    last.then_inc(made, 1)
                pe.wait_ge(qkv_v, len(proj) // 2)
                pe.wait_ge(qkv_s, len(proj) // 2)

                def scores(u):
                    t, gp, j = units[u]
                    if u >= 4:
                        pe.wait_ge(masked, 2 * (u - 3))
                    rows = slice(j * PADW, (j + 1) * PADW)
                    for i in range(2):
                        g = 2 * gp + i
                        last = nc.tensor.matmul(bank_of(L, u % 4)[:, i * 2 * P:i * 2 * P + width(t)],
                                                qT[rows, g, t * P:(t + 1) * P],
                                                kT[rows, g, (t + 1) * P - width(t):(t + 1) * P], start=True, stop=True)
                    last.then_inc(scored, 1)

                def turn(u):
                    t, gp, j = units[u]
                    pe.wait_ge(exped, 2 * (u + 1))
                    if u >= 2:
                        pe.wait_ge(pT_s if u % 2 else pT_v, (u - 2) // 2 + 1)
                    nb = width(t) // P
                    for i in range(2):
                        for c in range(nb):
                            last = nc.tensor.transpose(bank_of(L, 4 + u % 2)[:, (nb * i + c) * P:(nb * i + c + 1) * P],
                                                       pr[:, u % 3, i, c * P:(c + 1) * P], L.ident[:, :])
                    last.then_inc(turned, 1)

                def mix(u):
                    t, gp, j = units[u]
                    pe.wait_ge(pT_s if u % 2 else pT_v, u // 2 + 1)
                    if gp == 0 and j == 0 and t >= 2:
                        pe.wait_ge(normed, t - 1)
                    nb = width(t) // P
                    for i in range(2):
                        h = 4 * (2 * gp + i) + j
                        for c in range(nb):
                            last = nc.tensor.matmul(bank_of(L, 6 + t % 2)[:, h * HD:(h + 1) * HD], pT[:, u % 2, nb * i + c, :],
                                                    v[:, t - nb + 1 + c, h * HD:(h + 1) * HD], start=(c == 0), stop=(c == nb - 1))
                    last.then_inc(summed, 1)

                for n in range(NU + 3):
                    if n < NU:
                        scores(n)
                    if 2 <= n < NU + 2:
                        turn(n - 2)
                    if n >= 3:
                        mix(n - 3)

            @block.scalar
            def _(act):
                for n, (what, i) in enumerate(proj):
                    if n % 2:
                        act.wait_ge(made, n + 1)
                        if what == "v":
                            nc.scalar.copy(v[:, i, :], bank_of(L, n % 4, D)).then_inc(qkv_s, 1)
                        elif what == "q":
                            nc.scalar.mul(qT[:, i, :], bank_of(L, n % 4), HD ** -0.5).then_inc(qkv_s, 1)
                        else:
                            nc.scalar.copy(kT[:, i, :], bank_of(L, n % 4)).then_inc(qkv_s, 1)
                for n in range(NU + 1):
                    if n < NU:
                        t, gp, j = units[n]
                        act.wait_ge(bias, n + 1)
                        if n >= 3:
                            act.wait_ge(turned, n - 2)
                        for i in range(2):
                            h = 4 * (2 * gp + i) + j
                            nc.scalar.activation(pr[:, n % 3, i, 0:width(t)], sc[:, n % 2, i, 0:width(t)], ACT.Exp,
                                                 bias=nmx[:, n, i:i + 1], accum_out=den[:, t, h:h + 1]).then_inc(exped, 1)
                    if n >= 1 and (n - 1) % 2:
                        evac(nc.scalar.copy, act, n - 1, pT_s)

            @block.vector
            def _(dve):
                step = Chain(dve, vec)
                for n, (what, i) in enumerate(proj):
                    if n % 2 == 0:
                        dve.wait_ge(made, n + 1)
                        if what == "v":
                            nc.vector.tensor_copy(v[:, i, :], bank_of(L, n % 4, D)).then_inc(qkv_v, 1)
                        elif what == "q":
                            nc.vector.tensor_scalar(qT[:, i, :], bank_of(L, n % 4), HD ** -0.5, None, ALU.mult).then_inc(qkv_v, 1)
                        else:
                            nc.vector.tensor_copy(kT[:, i, :], bank_of(L, n % 4)).then_inc(qkv_v, 1)

                def norm(t):
                    dve.wait_ge(summed, 8 * (t + 1))
                    step(nc.vector.reciprocal(rden[:, t, :], den[:, t, :]))
                    nc.vector.tensor_tensor(
                        L.mixed[:, t, :].rearrange("p (h d) -> p h d", d=HD),
                        bank_of(L, 6 + t % 2, D).rearrange("p (h d) -> p h d", d=HD),
                        rden[:, t, :].rearrange("p (h a) -> p h a", a=1).to_broadcast((P, H, HD)), ALU.mult).then_inc(normed, 1)

                for n in range(NU + 2):
                    if n < NU:
                        t = units[n][0]
                        w = width(t)
                        dve.wait_ge(scored, n + 1)
                        if n >= 2:
                            dve.wait_ge(exped, 2 * (n - 1))
                        for i in range(2):
                            nc.vector.tensor_tensor_reduce(
                                out=sc[:, n % 2, i, 0:w], in0=bank_of(L, n % 4)[:, i * 2 * P:i * 2 * P + w],
                                in1=L.window[:, 2 * P - w:2 * P], scale=1.0, scalar=LOWEST, op0=ALU.add, op1=ALU.max,
                                accum_out=mx[:, n, i:i + 1]).then_inc(masked, 1)
                        dve.wait_ge(masked, 2 * (n + 1))
                        nc.vector.tensor_scalar(nmx[:, n, :], mx[:, n, :], -1.0, None, ALU.mult).then_inc(bias, 1)
                    if n >= 2 and (n - 2) % 2 == 0:
                        evac(nc.vector.tensor_copy, dve, n - 2, pT_v)
                    if n >= 8 + 4 and (n - 4) % 8 == 0 and (n - 4) // 8 <= T - 1:
                        norm((n - 4) // 8 - 1)
                norm(T - 1)


def project_norm(nc, name, L, weight, bias):
    with Stage(nc, name) as st:
        mT = st.sb("mT", [P, T, KD, P])
        res = st.sb("res", [P, T, D])
        turned, mT_done, made = st.sem("turned"), st.sem("mT_done"), st.sem("made")
        tail = NormTail(nc, st, L, res, turned_banks=(6, 7))
        with nc.Block(name) as block:
            @block.tensor
            def _(pe):
                for t in range(T):
                    for k in range(KD):
                        last = nc.tensor.transpose(bank_of(L, t)[:, k * P:(k + 1) * P], L.mixed[:, t, k * P:(k + 1) * P], L.ident[:, :])
                    last.then_inc(turned, 1)
                for t in range(T):
                    pe.wait_ge(mT_done, t + 1)
                    o = bank_of(L, 4 + t % 2, D)
                    if t >= 2:
                        pe.wait_ge(tail.added, t - 1)
                    if bias is not None:
                        nc.tensor.matmul(o, L.ones[:, :], bias[:, :], start=True, stop=False)
                    for k in range(KD):
                        last = nc.tensor.matmul(o, mT[:, t, k, :], weight[:, k, :], start=(k == 0 and bias is None), stop=(k == KD - 1))
                    last.then_inc(made, 1)
                tail.turn(pe)

            @block.scalar
            def _(act):
                for t in range(T):
                    act.wait_ge(turned, t + 1)
                    nc.scalar.copy(mT[:, t, :, :], bank_of(L, t, KD * P).rearrange("p (k n) -> p k n", k=KD)).then_inc(mT_done, 1)
                tail.finish(act)

            @block.vector
            def _(dve):
                step = Chain(dve, tail.vec)
                for t in range(T):
                    dve.wait_ge(made, t + 1)
                    nc.vector.tensor_tensor(res[:, t, :], bank_of(L, 4 + t % 2, D), L.x_tok[:, t, :], ALU.add).then_inc(tail.added, 1)
                    dve.wait_ge(tail.added, t + 1)
                    tail.stats_of(step, t)
                    if t >= 1:
                        tail.norm(dve, t - 1)
                tail.norm(dve, T - 1)


class NormTail:

    def __init__(self, nc, st, L, res, turned_banks, turn_x=True):
        self.nc, self.L, self.res, self.banks = nc, L, res, turned_banks
        self.stats, self.mv = st.sb("stats", [P, T, 6]), st.sb("mv", [P, T, 2])
        self.std, self.rstd = st.sb("std", [P, T]), st.sb("rstd", [P, T])
        self.added, self.var_done, self.std_done, self.rstd_done, self.new_x, self.x_turned, self.xT_done, self.vec = (
            st.sem(n) for n in ("added", "var_done", "std_done", "rstd_done", "new_x", "x_turned", "xT_done", "vec"))

    def stats_of(self, step, t):
        step(self.nc.vector.bn_stats(self.stats[:, t, :], self.res[:, t, :]))
        self.nc.vector.bn_aggr(self.mv[:, t, :], self.stats[:, t, :]).then_inc(self.var_done, 1)

    def norm(self, dve, t):
        dve.wait_ge(self.std_done, t + 1)
        self.nc.vector.reciprocal(self.rstd[:, t:t + 1], self.std[:, t:t + 1]).then_inc(self.rstd_done, 1)
        dve.wait_ge(self.rstd_done, t + 1)
        self.nc.vector.tensor_scalar(self.L.x_tok[:, t, :], self.res[:, t, :], self.mv[:, t, 0:1], self.rstd[:, t:t + 1],
                                     ALU.subtract, ALU.mult).then_inc(self.new_x, 1)

    def turn(self, pe):
        for t in range(T):
            pe.wait_ge(self.new_x, t + 1)
            if t >= 2:
                pe.wait_ge(self.xT_done, t - 1)
            for k in range(KD):
                last = self.nc.tensor.transpose(bank_of(self.L, self.banks[t % 2])[:, k * P:(k + 1) * P],
                                                self.L.x_tok[:, t, k * P:(k + 1) * P], self.L.ident[:, :])
            last.then_inc(self.x_turned, 1)

    def finish(self, act, turned=True):
        def copy_turned(t):
            act.wait_ge(self.x_turned, t + 1)
            self.nc.scalar.copy(self.L.x_T[:, :, t * P:(t + 1) * P],
                                bank_of(self.L, self.banks[t % 2], KD * P).rearrange("p (k n) -> p k n", k=KD)).then_inc(self.xT_done, 1)

        for t in range(T):
            act.wait_ge(self.var_done, t + 1)
            self.nc.scalar.activation(self.std[:, t:t + 1], self.mv[:, t, 1:2], ACT.Sqrt, bias=self.L.eps[:, :]).then_inc(self.std_done, 1)
            if turned and t >= 1:
                copy_turned(t - 1)
        if turned:
            copy_turned(T - 1)


def gather_attention(nc, gs, L):
    with Stage(nc, "gatt") as st:
        q = st.sb("q", [P, 2, D])
        pk, pv = st.sb("pk", [P, 2, NOFF, D]), st.sb("pv", [P, 2, NOFF, D])
        s = st.sb("s", [P, T, NOFF, H])
        m, den, rden = (st.sb(n, [P, T, H]) for n in ("m", "den", "rden"))
        e = st.sb("e", [P, T, NOFF, H])
        made, q_done, centred, exped, weighted, summed, vec = (
            st.sem(n) for n in ("made", "q_done", "centred", "exped", "weighted", "summed", "vec"))

        def heads(ap):
            return ap.rearrange("p o (h d) -> p (o h) d", d=HD)

        with nc.Block("gather_attention") as block:
            @block.tensor
            def _(pe):
                for t in range(T):
                    if t >= 2:
                        pe.wait_ge(q_done, t - 1)
                    for k in range(KD):
                        last = nc.tensor.matmul(bank_of(L, t % 2, D), L.x_T[:, k, t * P:(t + 1) * P], L.x0q[:, k, :],
                                                start=(k == 0), stop=(k == KD - 1))
                    last.then_inc(made, 1)

            @block.scalar
            def _(act):
                for t in range(T):
                    act.wait_ge(made, t + 1)
                    if t >= 2:
                        act.wait_ge(centred, t - 1)
                    nc.scalar.mul(q[:, t % 2, :], bank_of(L, t % 2, D), HD ** -0.5).then_inc(q_done, 1)
                    if t >= 1:
                        act.wait_ge(centred, t)
                        nc.scalar.activation(e[:, t - 1, :, :], s[:, t - 1, :, :], ACT.Exp).then_inc(exped, 1)
                act.wait_ge(centred, T)
                nc.scalar.activation(e[:, T - 1, :, :], s[:, T - 1, :, :], ACT.Exp).then_inc(exped, 1)

            @block.gpsimd
            def _(pool):
                for t in range(T):
                    for o in range(NOFF):
                        pool.wait_ge(gs.gathered[t][o], 16)
                nc.gpsimd.dma_reset()
                for t in range(T):
                    pool.wait_ge(exped, t + 1)
                    if t >= 2:
                        pool.wait_ge(summed, t - 1)
                    nc.gpsimd.tensor_tensor(
                        pv[:, t % 2, :, :].rearrange("p o (h d) -> p o h d", d=HD), gs.selected[:, t, :, D:2 * D].rearrange("p o (h d) -> p o h d", d=HD),
                        e[:, t, :, :].rearrange("p o (h a) -> p o h a", a=1).to_broadcast((P, NOFF, H, HD)), ALU.mult).then_inc(weighted, 1)

            @block.vector
            def _(dve):
                step = Chain(dve, vec)

                def out(t):
                    dve.wait_ge(exped, t + 1)
                    step(nc.vector.tensor_reduce(den[:, t, :], e[:, t, :, :].rearrange("p o h -> p h o"), AX.X, ALU.add))
                    step(nc.vector.reciprocal(rden[:, t, :], den[:, t, :]))
                    dve.wait_ge(weighted, t + 1)
                    nc.vector.tensor_reduce(L.mixed[:, t, :], pv[:, t % 2, :, :].rearrange("p o n -> p n o"), AX.X, ALU.add).then_inc(summed, 1)
                    dve.wait_ge(summed, t + 1)
                    view = L.mixed[:, t, :].rearrange("p (h d) -> p h d", d=HD)
                    step(nc.vector.tensor_tensor(view, view, rden[:, t, :].rearrange("p (h a) -> p h a", a=1).to_broadcast((P, H, HD)), ALU.mult))

                for t in range(T):
                    dve.wait_ge(q_done, t + 1)
                    for o in range(NOFF):
                        dve.wait_ge(gs.gathered[t][o], 16)
                    step(nc.vector.tensor_tensor(pk[:, t % 2, :, :], gs.selected[:, t, :, 0:D],
                                                 q[:, t % 2, :].rearrange("p (a n) -> p a n", a=1).to_broadcast((P, NOFF, D)), ALU.mult))
                    step(nc.vector.tensor_reduce(s[:, t, :, :], heads(pk[:, t % 2, :, :]), AX.X, ALU.add))
                    for mask, op in ((gs.keep, ALU.mult), (gs.lowest, ALU.add)):
                        step(nc.vector.tensor_tensor(s[:, t, :, :], s[:, t, :, :],
                                                     mask[:, t, :].rearrange("p (o a) -> p o a", a=1).to_broadcast((P, NOFF, H)), op))
                    step(nc.vector.tensor_reduce(m[:, t, :], s[:, t, :, :].rearrange("p o h -> p h o"), AX.X, ALU.max))
                    nc.vector.tensor_tensor(s[:, t, :, :], s[:, t, :, :],
                                            m[:, t, :].rearrange("p (a h) -> p a h", a=1).to_broadcast((P, NOFF, H)), ALU.subtract).then_inc(centred, 1)
                    if t >= 1:
                        out(t - 1)
                out(T - 1)



def sign_ffn(nc, L):
    NR = 3
    with Stage(nc, "ffn") as st:
        def pair(name, shape):
            return [st.sb(f"{name}_{w}", shape, F32R) for w in ("hi", "lo")]
        h1, h2 = pair("h1", [P, FM, S]), pair("h2", [P, FM, S])
        x2 = [h[:, 0:KD, :] for h in h2]
        w0 = st.sb("w0", [P, KD, F], F32R)
        w1 = st.sb("w1", [P, NR, FM, P], F32R)
        w2 = st.sb("w2", [P, FM, D], F32R)
        full = st.sb("full", [P, 4, S])
        w0_half = L.mixed[:, 0:2, :].rearrange("p m (k n) -> p m k n", k=KD)
        res = L.mixed
        names = ("w0_done", "w1_done", "w2_done", "x_hi", "x_lo", "made", "relued", "hi_done", "lo_done", "summed")
        w0_done, w1_done, w2_done, x_hi, x_lo, made, relued, hi_done, lo_done, summed = (st.sem(n) for n in names)
        tail = NormTail(nc, st, L, res, turned_banks=(6, 7))
        NT = 2 * FM

        with nc.Block("sign_ffn") as block:
            @block.gpsimd
            def _(pool):
                nc.gpsimd.tensor_copy(x2[0][:, :, :], L.x_T[:, :, :]).then_inc(x_hi, 1)
                for n in range(FM):
                    if n >= NR:
                        pool.wait_ge(made, FM + n - NR + 1)
                    nc.gpsimd.tensor_scalar(w1[:, n % NR, :, :], L.k1[:, :, n * P:(n + 1) * P], 2.0, -1.0, ALU.mult, ALU.add).then_inc(w1_done, 1)
                for k in range(FM):
                    nc.gpsimd.tensor_scalar(w2[:, k, :], L.k2[:, k, :], 2.0, -1.0, ALU.mult, ALU.add).then_inc(w2_done, 1)

            @block.tensor
            def _(pe):
                pe.wait_ge(x_lo, 1)
                for n in range(NT):
                    layer, m = n // FM, n % FM
                    if n >= 4:
                        pe.wait_ge(relued, n - 3)
                    if layer == 0:
                        pe.wait_ge(w0_done, m + 1)
                    else:
                        pe.wait_ge(w1_done, m + 1)
                    ks = KD if layer == 0 else FM
                    for k in range(ks):
                        if layer == 1 and m == 0:
                            pe.wait_ge(lo_done, k + 1)
                        for part in range(2):
                            w = w0[:, k, m * P:(m + 1) * P] if layer == 0 else w1[:, m % NR, k, :]
                            x = (x2 if layer == 0 else h1)[part][:, k, :]
                            last = nc.tensor.matmul(bank_of(L, n % 4), w, x, start=(k == 0 and part == 0), stop=(k == ks - 1 and part == 1))
                    last.then_inc(made, 1)
                pe.wait_ge(lo_done, NT)
                pe.wait_ge(w2_done, FM)
                for t in range(T):
                    if t >= 2:
                        pe.wait_ge(tail.added, t - 1)
                    for k in range(FM):
                        for part in range(2):
                            last = nc.tensor.matmul(bank_of(L, 4 + t % 2, D), h2[part][:, k, t * P:(t + 1) * P], w2[:, k, :],
                                                    start=(k == 0 and part == 0), stop=(k == FM - 1 and part == 1))
                    last.then_inc(summed, 1)
                tail.turn(pe)

            @block.scalar
            def _(act):
                for n in range(NT):
                    act.wait_ge(made, n + 1)
                    if n >= 4:
                        act.wait_ge(lo_done, n - 3)
                    layer = n // FM
                    nc.scalar.activation(full[:, n % 4, :], bank_of(L, n % 4), ACT.Relu,
                                         scale=L.scales[:, layer:layer + 1]).then_inc(relued, 1)
                    act.wait_ge(relued, n + 1)
                    nc.scalar.copy((h1 if n < FM else h2)[0][:, n % FM, :], full[:, n % 4, :]).then_inc(hi_done, 1)
                tail.finish(act)

            @block.vector
            def _(dve):
                step = Chain(dve, tail.vec)
                dve.wait_ge(x_hi, 1)
                nc.vector.tensor_tensor(x2[1][:, :, :], L.x_T[:, :, :], x2[0][:, :, :].bitcast(F32), ALU.subtract).then_inc(x_lo, 1)
                for m in range(FM):
                    w = w0[:, :, m * P:(m + 1) * P]
                    cols = slice(m * P, (m + 1) * P)
                    tmp = w0_half[:, m % 2, :, :]
                    if m >= 2:
                        dve.wait_ge(w0_done, m - 1)
                    step(nc.vector.tensor_tensor(tmp, L.k0[:, 0:KD, cols], L.k0[:, KD:2 * KD, cols], ALU.subtract))
                    nc.vector.tensor_scalar(w, tmp, 2.0, None, ALU.mult).then_inc(w0_done, 1)
                for n in range(NT):
                    dve.wait_ge(hi_done, n + 1)
                    h = h1 if n < FM else h2
                    nc.vector.tensor_tensor(h[1][:, n % FM, :], full[:, n % 4, :], h[0][:, n % FM, :].bitcast(F32), ALU.subtract).then_inc(lo_done, 1)
                for t in range(T):
                    dve.wait_ge(summed, t + 1)
                    nc.vector.scalar_tensor_tensor(out=res[:, t, :], in0=bank_of(L, 4 + t % 2, D), scalar=L.scales[:, 2:3],
                                                   in1=L.x_tok[:, t, :], op0=ALU.mult, op1=ALU.add).then_inc(tail.added, 1)
                    dve.wait_ge(tail.added, t + 1)
                    tail.stats_of(step, t)
                    if t >= 1:
                        tail.norm(dve, t - 1)
                tail.norm(dve, T - 1)


def linear_attention(nc, L):
    NQK = 2 * LM
    NV = 2 * T
    units = [(m, i, j) for m in range(LM) for i in range(T) for j in range(2)]
    NU = len(units)
    with Stage(nc, "lin") as st:
        qk = [st.sb("qT", [P, LM, S]), st.sb("kT", [P, LM, S])]
        v = st.sb("v", [P, T, LD])
        oT = st.sb("oT", [P, LM, S])
        sq, std, normed = (st.sb(n, [P, 2, S]) for n in ("sq", "root", "normed"))
        aT = st.sb("aT", [P, 4, S])
        res = L.mixed
        names = ("made", "squared", "meaned", "rooted", "divided", "scaled", "v_made", "v_v", "v_s", "scored", "copied",
                 "ready_v", "ready_p", "mixed_in", "oT_v", "oT_s", "summed")
        (made, squared, meaned, rooted, divided, scaled, v_made, v_v, v_s, scored, copied,
         ready_v, ready_p, mixed_in, oT_v, oT_s, summed) = (st.sem(n) for n in names)
        tail = NormTail(nc, st, L, res, turned_banks=(2, 3))

        def width(i):
            return S - i * P

        with nc.Block("linear") as block:
            def take_oT(copy, eng, m, done):
                eng.wait_ge(mixed_in, 8 * (m + 1))
                copy(oT[:, m, :], bank_of(L, 6 + m % 2)).then_inc(done, 1)

            @block.tensor
            def _(pe):
                def mean_square(n):
                    pe.wait_ge(squared, n + 1)
                    if n >= 2:
                        pe.wait_ge(rooted, n - 1)
                    nc.tensor.matmul(bank_of(L, 4 + n % 2), L.head_mean[:, :], sq[:, n % 2, :], start=True, stop=True).then_inc(meaned, 1)

                for n in range(NQK):
                    if n >= 4:
                        pe.wait_ge(divided, n - 3)
                    w = L.a1q if n < LM else L.a1k
                    m = n % LM
                    for k in range(KD):
                        last = nc.tensor.matmul(bank_of(L, n % 4), w[:, k, m * P:(m + 1) * P], L.x_T[:, k, :], start=(k == 0), stop=(k == KD - 1))
                    last.then_inc(made, 1)
                    if n >= 1:
                        mean_square(n - 1)
                    if n < NV:
                        if n >= 2:
                            pe.wait_ge(v_s if n % 2 else v_v, (n - 2) // 2 + 1)
                        t, half = n // 2, n % 2
                        for k in range(KD):
                            last = nc.tensor.matmul(bank_of(L, 6 + n % 2), L.x_T[:, k, t * P:(t + 1) * P],
                                                    L.a1v[:, k, half * 512:(half + 1) * 512], start=(k == 0), stop=(k == KD - 1))
                        last.then_inc(v_made, 1)
                mean_square(NQK - 1)
                pe.wait_ge(divided, NQK)
                pe.wait_ge(v_v, NV // 2)
                pe.wait_ge(v_s, NV // 2)

                def scores(u):
                    m, i, j = units[u]
                    if i == 0 and j == 0:
                        pe.wait_ge(scaled, LM + m + 1)
                    if u >= 4:
                        pe.wait_ge(copied if j else ready_v, (u - 4) // 2 + 1)
                    rows = slice(j * LH, (j + 1) * LH)
                    nc.tensor.matmul(bank_of(L, u % 4, width(i)), qk[1][rows, m, i * P:(i + 1) * P], qk[0][rows, m, i * P:S],
                                     start=True, stop=True).then_inc(scored, 1)

                def mix(u):
                    m, i, j = units[u]
                    pe.wait_ge(ready_p if j else ready_v, u // 2 + 1)
                    if i == 0 and j == 0 and m >= 2:
                        pe.wait_ge(oT_s if m % 2 else oT_v, (m - 2) // 2 + 1)
                    h = 2 * m + j
                    nc.tensor.matmul(bank_of(L, 6 + m % 2)[j * LH:(j + 1) * LH, i * P:S], v[:, i, h * LH:(h + 1) * LH],
                                     aT[:, u % 4, 0:width(i)], start=(i == 0), stop=(i == T - 1)).then_inc(mixed_in, 1)

                for n in range(NU + 2):
                    if n < NU:
                        scores(n)
                    if n >= 2:
                        mix(n - 2)
                pe.wait_ge(oT_v, LM // 2)
                pe.wait_ge(oT_s, LM // 2)
                for t in range(T):
                    if t >= 2:
                        pe.wait_ge(tail.added, t - 1)
                    for k in range(LM):
                        last = nc.tensor.matmul(bank_of(L, 4 + t % 2, D), oT[:, k, t * P:(t + 1) * P], L.a1o[:, k, :], start=(k == 0), stop=(k == LM - 1))
                    last.then_inc(summed, 1)
                tail.turn(pe)

            @block.scalar
            def _(act):
                def root(n):
                    act.wait_ge(meaned, n + 1)
                    if n >= 2:
                        act.wait_ge(divided, n - 1)
                    nc.scalar.activation(std[:, n % 2, :], bank_of(L, 4 + n % 2), ACT.Sqrt, bias=L.eps[:, :]).then_inc(rooted, 1)

                for n in range(NQK):
                    act.wait_ge(made, n + 1)
                    if n >= 2:
                        act.wait_ge(meaned, n - 1)
                    nc.scalar.activation(sq[:, n % 2, :], bank_of(L, n % 4), ACT.Square).then_inc(squared, 1)
                    if n >= 1:
                        root(n - 1)
                    if n < NV and n % 2:
                        act.wait_ge(v_made, n + 1)
                        nc.scalar.copy(v[:, n // 2, 512:LD], bank_of(L, 6 + n % 2)).then_inc(v_s, 1)
                root(NQK - 1)
                for u in range(NU):
                    m, i, j = units[u]
                    if j:
                        act.wait_ge(scored, u + 1)
                        if u >= 4:
                            act.wait_ge(mixed_in, u - 3)
                        nc.scalar.copy(aT[:, u % 4, 0:width(i)], bank_of(L, u % 4, width(i))).then_inc(copied, 1)
                        if i == 1 and m >= 1 and (m - 1) % 2:
                            take_oT(nc.scalar.copy, act, m - 1, oT_s)
                take_oT(nc.scalar.copy, act, LM - 1, oT_s)
                tail.finish(act)

            @block.gpsimd
            def _(pool):
                for n in range(NQK):
                    pool.wait_ge(divided, n + 1)
                    i = 0 if n < LM else 2
                    nc.gpsimd.tensor_scalar(qk[n // LM][:, n % LM, :], normed[:, n % 2, :], L.gains[:, i:i + 1], L.gains[:, i + 1:i + 2],
                                            ALU.mult, ALU.add).then_inc(scaled, 1)
                for u in range(1, NU, 2):
                    pool.wait_ge(copied, u // 2 + 1)
                    nc.gpsimd.affine_select(out=aT[:, u % 4, 0:P], in_=aT[:, u % 4, 0:P], compare_op=ALU.is_ge, fill=0.0,
                                            base=0, pattern=[[1, P]], channel_multiplier=-1).then_inc(ready_p, 1)

            @block.vector
            def _(dve):
                step = Chain(dve, tail.vec)

                def divide(n):
                    dve.wait_ge(rooted, n + 1)
                    if n >= 2:
                        dve.wait_ge(scaled, n - 1)
                    step(nc.vector.reciprocal(std[:, n % 2, :], std[:, n % 2, :]))
                    nc.vector.tensor_tensor(normed[:, n % 2, :], bank_of(L, n % 4), std[:, n % 2, :], ALU.mult).then_inc(divided, 1)

                for n in range(NQK):
                    if n < NV and n % 2 == 0:
                        dve.wait_ge(v_made, n + 1)
                        nc.vector.tensor_copy(v[:, n // 2, 0:512], bank_of(L, 6 + n % 2)).then_inc(v_v, 1)
                    if n >= 1:
                        divide(n - 1)
                divide(NQK - 1)
                for u in range(NU):
                    m, i, j = units[u]
                    if j == 0:
                        dve.wait_ge(scored, u + 1)
                        if u >= 4:
                            dve.wait_ge(mixed_in, u - 3)
                        nc.vector.tensor_tensor(aT[:, u % 4, 0:width(i)], bank_of(L, u % 4, width(i)), L.causal[:, 0:width(i)], ALU.mult).then_inc(ready_v, 1)
                        if i == 1 and m >= 1 and (m - 1) % 2 == 0:
                            take_oT(nc.vector.tensor_copy, dve, m - 1, oT_v)
                for t in range(T):
                    dve.wait_ge(summed, t + 1)
                    nc.vector.tensor_tensor(res[:, t, :], bank_of(L, 4 + t % 2, D), L.x_tok[:, t, :], ALU.add).then_inc(tail.added, 1)
                    dve.wait_ge(tail.added, t + 1)
                    tail.stats_of(step, t)
                    if t >= 1:
                        tail.norm(dve, t - 1)
                tail.norm(dve, T - 1)


def cross_attention(nc, a, L):
    NU = T * H
    with Stage(nc, "cross") as st:
        qT, kT = st.sb("qT", [P, G, S]), st.sb("kT", [P, G, SC])
        v = st.sb("v", [P, CT, D])
        mask = st.sb("mask", [P, T, SC])
        sc = st.sb("sc", [P, 2, SC])
        pr = st.sb("pr", [P, 3, SC])
        pT = st.sb("pT", [P, 2, CT, P])
        mx, nmx, den, rden = (st.sb(n, [P, T, H]) for n in ("mx", "nmx", "den", "rden"))
        names = ("mask_in", "mask_done", "made", "qkv_v", "qkv_s", "scored", "masked", "bias", "exped", "turned", "pT_v", "pT_s", "summed", "normed", "vec")
        mask_in, mask_done, made, qkv_v, qkv_s, scored, masked, bias, exped, turned, pT_v, pT_s, summed, normed, vec = (st.sem(n) for n in names)
        proj = [("q", g, 0) for g in range(G)] + [("k", g, c) for g in range(G) for c in range(2)] + [("v", c, 0) for c in range(CT)]

        def take(n, eng, done, vector):
            what, i, c = proj[n]
            eng.wait_ge(made, n + 1)
            if what == "v":
                dst, src, args = v[:, i, :], bank_of(L, n % 4, D), None
            elif what == "q":
                dst, src, args = qT[:, i, :], bank_of(L, n % 4), (HD ** -0.5, L.x1bqk[:, 0, i:i + 1])
            else:
                dst, src, args = kT[:, i, c * 512:(c + 1) * 512], bank_of(L, n % 4), (1.0, L.x1bqk[:, 1, i:i + 1])
            if vector:
                ins = nc.vector.tensor_copy(dst, src) if args is None else nc.vector.tensor_scalar(dst, src, args[0], args[1], ALU.mult, ALU.add)
            else:
                ins = nc.scalar.copy(dst, src) if args is None else nc.scalar.activation(dst, src, ACT.Identity, bias=args[1], scale=args[0])
            ins.then_inc(done, 1)

        def take_turned(copy, eng, n, done):
            u, c = n // 2, n % 2
            eng.wait_ge(turned, n + 1)
            if u >= 2:
                eng.wait_ge(summed, u - 1)
            copy(pT[:, u % 2, 4 * c:4 * c + 4, :], bank_of(L, 4 + c).rearrange("p (c n) -> p c n", n=P)).then_inc(done, 1)

        with nc.Block("cross") as block:
            @block.sync
            def _(sp):
                sp.dma_start(mask[:, :, :], a["mask_SxS2_fk1"].rearrange("(t p) n -> p t n", p=P)).then_inc(mask_in, 16)

            @block.gpsimd
            def _(pool):
                pool.wait_ge(mask_in, 16)
                for t in range(T):
                    nc.gpsimd.tensor_scalar(mask[:, t, :], mask[:, t, :], NEG, None, ALU.mult).then_inc(mask_done, 1)

            @block.tensor
            def _(pe):
                for n, (what, i, c) in enumerate(proj):
                    if n >= 4:
                        pe.wait_ge(qkv_s if n % 2 else qkv_v, (n - 4) // 2 + 1)
                    if what == "v":
                        nc.tensor.matmul(bank_of(L, n % 4, D), L.ones[:, :], L.x1bv[:, :], start=True, stop=False)
                    for k in range(KD):
                        if what == "v":
                            lhs, rhs, o = L.ctx_T[:, k, i * P:(i + 1) * P], L.x1v[:, k, :], bank_of(L, n % 4, D)
                        elif what == "q":
                            lhs, rhs, o = L.x1q[:, k, i * P:(i + 1) * P], L.x_T[:, k, :], bank_of(L, n % 4)
                        else:
                            lhs, rhs, o = L.x1k[:, k, i * P:(i + 1) * P], L.ctx_T[:, k, c * 512:(c + 1) * 512], bank_of(L, n % 4)
                        last = nc.tensor.matmul(o, lhs, rhs, start=(k == 0 and what != "v"), stop=(k == KD - 1))
                    last.then_inc(made, 1)
                pe.wait_ge(qkv_v, len(proj) // 2)
                pe.wait_ge(qkv_s, len(proj) // 2)

                def scores(u):
                    t, h = u // H, u % H
                    g, j = h // 4, h % 4
                    if u >= 2:
                        pe.wait_ge(masked, u - 1)
                    rows = slice(j * PADW, (j + 1) * PADW)
                    for c in range(2):
                        last = nc.tensor.matmul(bank_of(L, 2 * (u % 2) + c), qT[rows, g, t * P:(t + 1) * P], kT[rows, g, c * 512:(c + 1) * 512],
                                                start=True, stop=True)
                    last.then_inc(scored, 1)

                def turn(u):
                    pe.wait_ge(exped, u + 1)
                    for c in range(2):
                        if u >= 1:
                            pe.wait_ge(pT_s if c else pT_v, u)
                        for i in range(4):
                            last = nc.tensor.transpose(bank_of(L, 4 + c)[:, i * P:(i + 1) * P], pr[:, u % 3, (4 * c + i) * P:(4 * c + i + 1) * P], L.ident[:, :])
                        last.then_inc(turned, 1)

                def mix(u):
                    t, h = u // H, u % H
                    pe.wait_ge(pT_v, u + 1)
                    pe.wait_ge(pT_s, u + 1)
                    if h == 0 and t >= 2:
                        pe.wait_ge(normed, t - 1)
                    for c in range(CT):
                        last = nc.tensor.matmul(bank_of(L, 6 + t % 2)[:, h * HD:(h + 1) * HD], pT[:, u % 2, c, :], v[:, c, h * HD:(h + 1) * HD],
                                                start=(c == 0), stop=(c == CT - 1))
                    last.then_inc(summed, 1)

                for n in range(NU + 3):
                    if n < NU:
                        scores(n)
                    if 2 <= n < NU + 2:
                        turn(n - 2)
                    if n >= 3:
                        mix(n - 3)

            @block.scalar
            def _(act):
                for n in range(1, len(proj), 2):
                    take(n, act, qkv_s, False)
                for n in range(NU + 2):
                    if n < NU:
                        t, h = n // H, n % H
                        act.wait_ge(bias, n + 1)
                        if n >= 3:
                            act.wait_ge(turned, 2 * (n - 2))
                        nc.scalar.activation(pr[:, n % 3, :], sc[:, n % 2, :], ACT.Exp, bias=nmx[:, t, h:h + 1],
                                             accum_out=den[:, t, h:h + 1]).then_inc(exped, 1)
                    if n >= 2:
                        take_turned(nc.scalar.copy, act, 2 * (n - 2) + 1, pT_s)

            @block.vector
            def _(dve):
                step = Chain(dve, vec)
                for n in range(0, len(proj), 2):
                    take(n, dve, qkv_v, True)

                def norm(t):
                    dve.wait_ge(summed, H * (t + 1))
                    step(nc.vector.reciprocal(rden[:, t, :], den[:, t, :]))
                    nc.vector.tensor_tensor(
                        L.mixed[:, t, :].rearrange("p (h d) -> p h d", d=HD),
                        bank_of(L, 6 + t % 2, D).rearrange("p (h d) -> p h d", d=HD),
                        rden[:, t, :].rearrange("p (h a) -> p h a", a=1).to_broadcast((P, H, HD)), ALU.mult).then_inc(normed, 1)

                for n in range(NU + 2):
                    if n < NU:
                        t, h = n // H, n % H
                        dve.wait_ge(scored, n + 1)
                        if h == 0:
                            dve.wait_ge(mask_done, t + 1)
                        if n >= 2:
                            dve.wait_ge(exped, n - 1)
                        pair = L.PS[:, (n % 2) * SC:(n % 2 + 1) * SC]
                        nc.vector.tensor_tensor_reduce(out=sc[:, n % 2, :], in0=pair, in1=mask[:, t, :], scale=1.0, scalar=LOWEST,
                                                       op0=ALU.add, op1=ALU.max, accum_out=mx[:, t, h:h + 1]).then_inc(masked, 1)
                        dve.wait_ge(masked, n + 1)
                        nc.vector.tensor_scalar(nmx[:, t, h:h + 1], mx[:, t, h:h + 1], -1.0, None, ALU.mult).then_inc(bias, 1)
                    if n >= 2:
                        take_turned(nc.vector.tensor_copy, dve, 2 * (n - 2), pT_v)
                    if n >= H + 4 and (n - 4) % H == 0:
                        norm((n - 4) // H - 1)
                norm(T - 1)


def experts(nc, a, L):
    PROD = ((0, 1), (1, 0), (0, 0))
    with Stage(nc, "moe") as st:
        def pair(name, shape):
            return [st.sb(f"{name}_{w}", shape, F32R) for w in ("hi", "lo")]
        x2 = pair("x", [P, KD, S])
        w1, w2 = st.sb("w1", [P, 2, KD, ED]), st.sb("w2", [P, 2, EM, D])
        w1p, w2p = pair("w1", [P, 2, KD, ED]), pair("w2", [P, 2, EM, D])
        full = st.sb("full", [P, 4, S])
        hp = pair("h", [P, 2, EM, S])
        logit, prob, rest, top8, cw = (st.sb(n, [P, T, E]) for n in ("logit", "prob", "rest", "top8", "cw"))
        lmax, lden = st.sb("lmax", [P, T]), st.sb("lden", [P, T])
        cwT = st.sb("cwT", [E, T, P])
        acc = L.mixed
        w_in = [st.sem("w_in0"), st.sem("w_in1")]
        names = ("x_hi", "x_lo", "w_hi", "w_lo", "routed", "shifted", "exped", "cw_done", "cw_turned", "cwT_done", "biased", "acc_done",
                 "made", "relued", "hi_done", "lo_done", "summed")
        (x_hi, x_lo, w_hi, w_lo, routed, shifted, exped, cw_done, cw_turned, cwT_done, biased, acc_done,
         made, relued, hi_done, lo_done, summed) = (st.sem(n) for n in names)
        tail = NormTail(nc, st, L, acc, turned_banks=None)

        with nc.Block("experts") as block:
            @block.sync
            def _(sp):
                for e in range(E):
                    if e >= 2:
                        sp.wait_ge(w_lo, 2 * (e - 1))
                    sp.dma_start(w1[:, e % 2, :, :], a["L1_ffn_W1"][e].rearrange("(k p) n -> p k n", p=P)).then_inc(w_in[e % 2], 16)
                    sp.dma_start(w2[:, e % 2, :, :], a["L1_ffn_W2"][e].rearrange("(k p) n -> p k n", p=P)).then_inc(w_in[e % 2], 16)

            @block.gpsimd
            def _(pool):
                nc.gpsimd.tensor_copy(x2[0][:, :, :], L.x_T[:, :, :]).then_inc(x_hi, 1)
                pool.wait_ge(x_hi, 1)
                nc.gpsimd.tensor_tensor(x2[1][:, :, :], L.x_T[:, :, :], x2[0][:, :, :].bitcast(F32), ALU.subtract).then_inc(x_lo, 1)
                for e in range(E):
                    pool.wait_ge(w_in[e % 2], 32 * (e // 2 + 1))
                    s = e % 2
                    for n, (w, wp) in enumerate(((w1, w1p), (w2, w2p))):
                        if e >= 2:
                            pool.wait_ge(summed if n else made, EM * (e - 1))
                        nc.gpsimd.tensor_copy(wp[0][:, s, :, :], w[:, s, :, :]).then_inc(w_hi, 1)
                        pool.wait_ge(w_hi, 2 * e + n + 1)
                        nc.gpsimd.tensor_tensor(wp[1][:, s, :, :], w[:, s, :, :], wp[0][:, s, :, :].bitcast(F32), ALU.subtract).then_inc(w_lo, 1)

            @block.tensor
            def _(pe):
                for t in range(T):
                    o = bank_of(L, 4)[:, t * E:(t + 1) * E]
                    nc.tensor.matmul(o, L.ones[:, :], L.br[:, :], start=True, stop=False)
                    for k in range(KD):
                        last = nc.tensor.matmul(o, L.x_T[:, k, t * P:(t + 1) * P], L.wr[:, k, :], start=False, stop=(k == KD - 1))
                    last.then_inc(routed, 1)

                def up(e):
                    pe.wait_ge(w_lo, 2 * e + 1)
                    for m in range(EM):
                        n = e * EM + m
                        if n >= 4:
                            pe.wait_ge(relued, n - 3)
                        for k in range(KD):
                            for i, (p, q) in enumerate(PROD):
                                last = nc.tensor.matmul(bank_of(L, n % 4), w1p[p][:, e % 2, k, m * P:(m + 1) * P], x2[q][:, k, :],
                                                        start=(k == 0 and i == 0), stop=(k == KD - 1 and i == 2))
                        last.then_inc(made, 1)

                def down(e):
                    pe.wait_ge(w_lo, 2 * e + 2)
                    for t in range(T):
                        n = e * T + t
                        if n >= 4:
                            pe.wait_ge(acc_done, T + n - 3)
                        for k in range(EM):
                            if t == 0:
                                pe.wait_ge(lo_done, e * EM + k + 1)
                            for i, (p, q) in enumerate(PROD):
                                last = nc.tensor.matmul(bank_of(L, 4 + n % 4, D), hp[p][:, e % 2, k, t * P:(t + 1) * P], w2p[q][:, e % 2, k, :],
                                                        start=(k == 0 and i == 0), stop=(k == EM - 1 and i == 2))
                        last.then_inc(summed, 1)

                pe.wait_ge(x_lo, 1)
                up(0)
                for t in range(T):
                    pe.wait_ge(cw_done, t + 1)
                    nc.tensor.transpose(bank_of(L, 5)[0:E, t * P:(t + 1) * P], cw[:, t, :], L.ident[:, :]).then_inc(cw_turned, 1)
                for t in range(T):
                    pe.wait_ge(cwT_done, 1)
                    nc.tensor.matmul(bank_of(L, 6 + t % 2)[:, (t // 2) * D:(t // 2 + 1) * D], cwT[:, t, :], L.b2[:, :], start=True, stop=True).then_inc(biased, 1)
                pe.wait_ge(acc_done, T)
                for e in range(1, E):
                    up(e)
                    down(e - 1)
                down(E - 1)

            @block.scalar
            def _(act):
                def relu(n):
                    act.wait_ge(made, n + 1)
                    if n >= 4:
                        act.wait_ge(lo_done, n - 3)
                    nc.scalar.activation(full[:, n % 4, :], bank_of(L, n % 4), ACT.Relu, bias=L.b1[:, n:n + 1]).then_inc(relued, 1)
                    act.wait_ge(relued, n + 1)
                    e, m = n // EM, n % EM
                    if e >= 2:
                        act.wait_ge(summed, T * (e - 1))
                    nc.scalar.copy(hp[0][:, e % 2, m, :], full[:, n % 4, :]).then_inc(hi_done, 1)

                for t in range(T):
                    act.wait_ge(shifted, t + 1)
                    nc.scalar.activation(prob[:, t, :], logit[:, t, :], ACT.Exp, accum_out=lden[:, t:t + 1]).then_inc(exped, 1)
                act.wait_ge(cw_turned, T)
                nc.scalar.copy(cwT[:, :, :], bank_of(L, 5)[0:E, :].rearrange("e (t p) -> e t p", p=P)).then_inc(cwT_done, 1)
                for n in range(E * EM):
                    relu(n)
                tail.finish(act, turned=False)

            @block.vector
            def _(dve):
                step = Chain(dve, tail.vec)
                dve.wait_ge(routed, T)
                step(nc.vector.tensor_copy(logit[:, :, :], bank_of(L, 4, T * E).rearrange("p (t e) -> p t e", e=E)))
                step(nc.vector.tensor_reduce(lmax[:, :], logit[:, :, :], AX.X, ALU.max))
                for t in range(T):
                    nc.vector.tensor_scalar(logit[:, t, :], logit[:, t, :], lmax[:, t:t + 1], None, ALU.subtract).then_inc(shifted, 1)
                dve.wait_ge(exped, T)
                step(nc.vector.reciprocal(lden[:, :], lden[:, :]))
                for t in range(T):
                    step(nc.vector.tensor_scalar(prob[:, t, :], prob[:, t, :], lden[:, t:t + 1], None, ALU.mult))
                    step(nc.vector.max(top8[:, t, :], prob[:, t, :]))
                    step(nc.vector.memset(top8[:, t, 2:E], -1.0))
                    step(nc.vector.match_replace(rest[:, t, :], top8[:, t, :], prob[:, t, :], 0.0))
                    nc.vector.tensor_tensor(cw[:, t, :], prob[:, t, :], rest[:, t, :], ALU.subtract).then_inc(cw_done, 1)
                for t in range(T):
                    dve.wait_ge(biased, t + 1)
                for t in range(T):
                    nc.vector.tensor_tensor(acc[:, t, :], bank_of(L, 6 + t % 2)[:, (t // 2) * D:(t // 2 + 1) * D], L.x_tok[:, t, :], ALU.add).then_inc(acc_done, 1)

                def low(n):
                    dve.wait_ge(hi_done, n + 1)
                    e, m = n // EM, n % EM
                    nc.vector.tensor_tensor(hp[1][:, e % 2, m, :], full[:, n % 4, :], hp[0][:, e % 2, m, :].bitcast(F32), ALU.subtract).then_inc(lo_done, 1)

                def add(n):
                    e, t = n // T, n % T
                    dve.wait_ge(summed, n + 1)
                    dve.wait_ge(acc_done, n + 1)
                    nc.vector.scalar_tensor_tensor(out=acc[:, t, :], in0=bank_of(L, 4 + n % 4, D), scalar=cw[:, t, e:e + 1], in1=acc[:, t, :],
                                                   op0=ALU.mult, op1=ALU.add).then_inc(acc_done, 1)

                for n in range(EM):
                    low(n)
                for e in range(1, E):
                    for m in range(EM):
                        low(e * EM + m)
                    for t in range(T):
                        add((e - 1) * T + t)
                for t in range(T):
                    add((E - 1) * T + t)
                for t in range(T):
                    dve.wait_ge(acc_done, E * T + t + 1)
                    tail.stats_of(step, t)
                    if t >= 1:
                        tail.norm(dve, t - 1)
                tail.norm(dve, T - 1)


_INS = ["x", "ctx_1024", "itok_BxS_0_511", "mask_SxS2_fk1",
        "L0_attn_Wq", "L0_attn_Wk", "L0_attn_Wv", "L0_attn_Wo", "L0_attn_bo",
        "L0_xattn_Wq", "L0_xattn_Wkv", "L0_xattn_Wo",
        "L0_ffn_k0", "L0_ffn_k1", "L0_ffn_k2", "L0_ffn_s0", "L0_ffn_s1", "L0_ffn_s2",
        "L1_attn_Wq", "L1_attn_Wk", "L1_attn_Wv", "L1_attn_Wo",
        "L1_attn_q_gamma", "L1_attn_q_beta", "L1_attn_k_gamma", "L1_attn_k_beta",
        "L1_xattn_Wq", "L1_xattn_bq", "L1_xattn_Wk", "L1_xattn_bk", "L1_xattn_Wv", "L1_xattn_bv",
        "L1_xattn_Wo", "L1_xattn_bo",
        "L1_ffn_Wr", "L1_ffn_br", "L1_ffn_W1", "L1_ffn_b1", "L1_ffn_W2", "L1_ffn_b2"]


def kernel(**inputs):
    import numpy as _np
    import concourse.bacc as _bacc
    from concourse import mybir as _mybir
    from concourse.bass_utils import run_bass_kernel_spmd as _run

    nc = _bacc.Bacc("TRN2", target_bir_lowering=False, num_devices=1)
    arrays, aps = {}, {}
    for name in _INS:
        v = _np.ascontiguousarray(inputs[name])
        v = v.view(_np.int32) if v.dtype == _np.bool_ else v
        v = v.reshape(1) if v.ndim == 0 else v
        arrays[f"in_{name}"] = v
        aps[name] = nc.dram_tensor(f"in_{name}", v.shape, _mybir.dt.from_np(v.dtype), kind="ExternalInput").ap()
    out = nc.dram_tensor("out_x", (B, S, D), _mybir.dt.float32, kind="ExternalOutput").ap()
    decoder(nc, aps, out)
    return _run(nc, [arrays], core_ids=[0]).results[0]["out_x"]
```

```python
from contextlib import ExitStack

import numpy as np

import concourse.bass as bass
from concourse import mybir

F32 = mybir.dt.float32
F32R = mybir.dt.float32r
I32 = mybir.dt.int32
U8 = mybir.dt.uint8
ALU = mybir.AluOpType
ACT = mybir.ActivationFunctionType
AX = mybir.AxisListType

P = 128
B, S, D = 4, 512, 256
SC = 1024
T, KD, CT = S // P, D // P, SC // P
H, HD = 16, D // 16
PADW = 32
WIN = 128
NOFF = 4
LH = 64
LD = H * LH
LM = LD // P
F = 1024
FM = F // P
E, ED = 8, 512
EM = ED // P
EPS = 1e-5
NEG = -1.0e9
LOWEST = float(np.finfo(np.float32).min)
FAR = -1.0e30


class Stage:

    def __init__(self, nc, name):
        self.nc, self.name, self.ctx, self.sems = nc, name, ExitStack(), []

    def __enter__(self):
        return self

    def sem(self, name):
        s = self.ctx.enter_context(self.nc.semaphore(f"{self.name}_{name}"))
        self.sems.append(s)
        return s

    def sb(self, name, shape, dt=F32):
        return self.ctx.enter_context(self.nc.sbuf_tensor(f"{self.name}_{name}", shape, dt))

    def __exit__(self, *exc):
        if exc[0] is None:
            nums = [s.num for s in self.sems]
            if nums:
                self.nc.all_engine_barrier(sems_to_clear=range(min(nums), max(nums) + 1))
        return self.ctx.__exit__(*exc)


class Chain:

    def __init__(self, eng, sem):
        self.eng, self.sem, self.n = eng, sem, 0

    def __call__(self, ins):
        self.n += 1
        ins.then_inc(self.sem, 1)
        self.eng.wait_ge(self.sem, self.n)


class Buffers:
    pass


def decoder(nc, a, out, n_batches=B, last_stage=99):
    top = ExitStack()

    def sb(name, shape, dt=F32):
        return top.enter_context(nc.sbuf_tensor(name, shape, dt))

    L = Buffers()
    L.kv_table = nc.dram_tensor("kv_table", [SC, 2 * D], F32).ap()

    L.PS = top.enter_context(nc.psum_tensor("PS", [P, 8 * 512], F32))

    L.ident = sb("ident", [P, P])
    L.ones = sb("ones", [1, P])
    L.eps = sb("eps", [P, 1])
    L.zero = sb("zero", [P, 1])
    L.sel = {n: sb(f"sel_{n}", [P, 4 * P], F32R) for n in ("q_hi", "q_lo", "k_hi", "k_lo")}
    L.window = sb("window", [P, 2 * P])
    L.causal = sb("causal", [P, S])
    L.head_mean = sb("head_mean", [P, P])
    L.a0q = sb("a0q", [P, KD, D])
    L.a0k = sb("a0k", [P, KD, D])
    L.a0v = sb("a0v", [P, KD, D])
    L.a0o = sb("a0o", [P, KD, D])
    L.a0bo = sb("a0bo", [1, D])
    L.x0q = sb("x0q", [P, KD, D])
    L.x0kv = sb("x0kv", [P, KD, 2 * D])
    L.x0o = sb("x0o", [P, KD, D])
    L.k0_words, L.k1_words, L.k2_words = (sb(n, [P, r, c // 4], I32) for n, r, c in (("k0", 2 * KD, F), ("k1", FM, F), ("k2", FM, D)))
    L.k0, L.k1, L.k2 = (w[:, :, :].bitcast(U8) for w in (L.k0_words, L.k1_words, L.k2_words))
    L.scales = sb("scales", [P, 4])
    L.a1q = sb("a1q", [P, KD, LD])
    L.a1k = sb("a1k", [P, KD, LD])
    L.a1v = sb("a1v", [P, KD, LD])
    L.a1o = sb("a1o", [P, LM, D])
    L.gains = sb("gains", [P, 4])
    L.x1q = sb("x1q", [P, KD, D])
    L.x1k = sb("x1k", [P, KD, D])
    L.x1v = sb("x1v", [P, KD, D])
    L.x1o = sb("x1o", [P, KD, D])
    L.x1bqk = sb("x1bqk", [P, 2, KD])
    L.x1bv = sb("x1bv", [1, D])
    L.x1bo = sb("x1bo", [1, D])
    L.wr = sb("wr", [P, KD, E])
    L.br = sb("br", [1, E])
    L.b1 = sb("b1", [P, E * EM])
    L.b2 = sb("b2", [E, D])
    L.x_tok = sb("x_tok", [P, T, D])
    L.x_T = sb("x_T", [P, KD, S])
    L.ctx_T = sb("ctx_T", [P, KD, SC])
    L.mixed = sb("mixed", [P, T, D])

    setup(nc, a, L)

    with nc.Fori(0, n_batches) as b:
        load_batch(nc, a, b, L)
        with Stage(nc, "gat") as gs:
            context_table(nc, a, b, gs, L)
            window_attention(nc, gs, L)
            if last_stage >= 1:
                project_norm(nc, "a0p", L, L.a0o, L.a0bo)
            if last_stage >= 3:
                gather_attention(nc, gs, L)
        if last_stage >= 3:
            project_norm(nc, "x0p", L, L.x0o, None)
        if last_stage >= 4:
            sign_ffn(nc, L)
        if last_stage >= 5:
            linear_attention(nc, L)
        if last_stage >= 6:
            cross_attention(nc, a, L)
            project_norm(nc, "x1p", L, L.x1o, L.x1bo)
        if last_stage >= 7:
            experts(nc, a, L)
        store_batch(nc, b, out, L.x_tok)
    top.close()


def setup(nc, a, L):
    with Stage(nc, "set") as st:
        loads = [0]
        loaded, memset, piece, sel_done = st.sem("loaded"), st.sem("memset"), st.sem("const"), st.sem("sel_done")
        turned, copied_v, copied_s = st.sem("turned"), st.sem("copied_v"), st.sem("copied_s")
        vec = st.sem("vec")
        raw = {}
        for n, rows in (("L0_xattn_Wq", 2), ("L0_xattn_Wkv", 4), ("L0_xattn_Wo", 2), ("L1_attn_Wq", 8),
                        ("L1_attn_Wk", 8), ("L1_attn_Wv", 8), ("L1_xattn_Wq", 2), ("L1_xattn_Wk", 2),
                        ("L1_xattn_Wv", 2), ("L1_xattn_Wo", 2)):
            raw[n] = st.sb(n, [P, rows, D])
        raw["L1_attn_Wo"] = st.sb("L1_attn_Wo", [P, KD, LD])
        sel = st.sb("sel", [P, 4 * P])
        mean = st.sb("mean", [P, KD * H])
        b1_rows = st.sb("b1_rows", [E * EM, P])

        jobs = []
        for n, dst in (("L0_xattn_Wq", L.x0q), ("L0_xattn_Wkv", L.x0kv),
                               ("L0_xattn_Wo", L.x0o), ("L1_attn_Wq", L.a1q), ("L1_attn_Wk", L.a1k),
                               ("L1_attn_Wv", L.a1v), ("L1_xattn_Wq", L.x1q), ("L1_xattn_Wk", L.x1k),
                               ("L1_xattn_Wv", L.x1v), ("L1_xattn_Wo", L.x1o)):
            for r in range(raw[n].shape[1]):
                pair = [raw[n][:, r, k * P:(k + 1) * P] for k in range(KD)]
                jobs.append((pair, dst[:, :, r * P:(r + 1) * P]))
        for r in range(KD):
            for c in range(0, LM, 2):
                pair = [raw["L1_attn_Wo"][:, r, (c + k) * P:(c + k + 1) * P] for k in range(2)]
                jobs.append((pair, L.a1o[:, c:c + 2, r * P:(r + 1) * P]))

        direct = [(raw[n][:, :, :], a[n].rearrange("(r p) n -> p r n", p=P)) for n in raw]
        direct += [
            (L.a0q[:, :, :], a["L0_attn_Wq"].rearrange("(k p) n -> p k n", p=P)),
            (L.a0k[:, :, :], a["L0_attn_Wk"].rearrange("(k p) n -> p k n", p=P)),
            (L.a0v[:, :, :], a["L0_attn_Wv"].rearrange("(k p) n -> p k n", p=P)),
            (L.a0o[:, :, :], a["L0_attn_Wo"].rearrange("(k p) n -> p k n", p=P)),
            (L.a0bo[:, :], a["L0_attn_bo"].rearrange("(a n) -> a n", a=1)),
            (L.k0_words[:, :, :], a["L0_ffn_k0"].rearrange("(k p) n -> p k n", p=P)),
            (L.k1_words[:, :, :], a["L0_ffn_k1"].rearrange("(k p) n -> p k n", p=P)),
            (L.k2_words[:, :, :], a["L0_ffn_k2"].rearrange("(k p) n -> p k n", p=P)),
            (L.x1bv[:, :], a["L1_xattn_bv"].rearrange("(a n) -> a n", a=1)),
            (L.x1bo[:, :], a["L1_xattn_bo"].rearrange("(a n) -> a n", a=1)),
            (L.wr[:, :, :], a["L1_ffn_Wr"].rearrange("(k p) n -> p k n", p=P)),
            (L.br[:, :], a["L1_ffn_br"].rearrange("(a n) -> a n", a=1)),
            (b1_rows[:, :], a["L1_ffn_b1"].rearrange("e (m p) -> (e m) p", p=P)),
            (L.b2[:, :], a["L1_ffn_b2"]),
        ]
        for i in range(3):
            direct.append((L.scales[:, i:i + 1], a[f"L0_ffn_s{i}"].rearrange("(a n) -> a n", a=1).to_broadcast((P, 1))))
        for i, n in enumerate(("q_gamma", "q_beta", "k_gamma", "k_beta")):
            for j in range(2):
                direct.append((L.gains[j * LH:(j + 1) * LH, i:i + 1], a[f"L1_attn_{n}"].rearrange("(n a) -> n a", a=1)))
        for i, n in enumerate(("L1_xattn_bq", "L1_xattn_bk")):
            direct.append((L.x1bqk[:, i, :], a[n].rearrange("(k p) -> p k", p=P)))

        small = nc.allow_non_contiguous_dma("biases and gains, a few hundred words each")
        with small, nc.Block("setup") as block:
            @block.sync
            def _(sp):
                for dst, src in direct[:len(direct) // 2]:
                    sp.dma_start(dst, src).then_inc(loaded, 16)
                sp.wait_ge(loaded, 16 * len(direct))

            @block.gpsimd
            def _(pool):
                nc.gpsimd.memset(L.ident[:, :], 0.0).then_inc(piece, 1)
                nc.gpsimd.memset(L.window[:, :], 0.0).then_inc(piece, 1)
                nc.gpsimd.memset(L.causal[:, :], 1.0).then_inc(piece, 1)
                nc.gpsimd.memset(L.ones[:, :], 1.0).then_inc(piece, 1)
                nc.gpsimd.memset(L.eps[:, :], EPS).then_inc(piece, 1)
                nc.gpsimd.memset(L.zero[:, :], 0.0).then_inc(piece, 1)
                nc.gpsimd.memset(sel[:, :], 0.0).then_inc(piece, 1)
                pool.wait_ge(piece, 7)
                nc.gpsimd.affine_select(out=L.ident[:, :], in_=L.ident[:, :], compare_op=ALU.not_equal, fill=1.0,
                                        base=0, pattern=[[-1, P]], channel_multiplier=1).then_inc(piece, 1)
                nc.gpsimd.affine_select(out=L.window[:, :], in_=L.window[:, :], compare_op=ALU.is_gt, fill=FAR,
                                        base=0, pattern=[[1, 2 * P]], channel_multiplier=-1).then_inc(piece, 1)
                nc.gpsimd.affine_select(out=L.causal[:, :], in_=L.causal[:, :], compare_op=ALU.is_ge, fill=0.0,
                                        base=0, pattern=[[1, S]], channel_multiplier=-1).then_inc(piece, 1)
                pool.wait_ge(piece, 10)
                nc.gpsimd.affine_select(out=L.window[:, :], in_=L.window[:, :], compare_op=ALU.is_ge, fill=FAR,
                                        base=P, pattern=[[-1, 2 * P]], channel_multiplier=1).then_inc(piece, 1)
                nc.gpsimd.affine_select(out=sel[:, :], in_=sel[:, :], compare_op=ALU.not_equal, fill=1.0, base=0,
                                        pattern=[[-2 * HD, 4], [-HD, 2], [0, 4], [-1, HD]], channel_multiplier=1).then_inc(sel_done, 1)
                pool.wait_ge(piece, 11)
                pool.wait_ge(sel_done, 1)

            @block.tensor
            def _(pe):
                pe.wait_ge(loaded, 16 * len(direct))
                pe.wait_ge(piece, 10)
                for n, (pair, _) in enumerate(jobs):
                    if n >= 4:
                        pe.wait_ge(copied_v if n % 2 == 0 else copied_s, (n - 4) // 2 + 1)
                    for k, src in enumerate(pair):
                        last = nc.tensor.transpose(bank_of(L, n % 4)[:, k * P:(k + 1) * P], src, L.ident[:, :])
                    last.then_inc(turned, 1)
                nc.tensor.transpose(bank_of(L, 4, E * EM), b1_rows[:, :], L.ident[0:E * EM, 0:E * EM]).then_inc(turned, 1)

            @block.scalar
            def _(act):
                for dst, src in direct[len(direct) // 2:]:
                    act.dma_start(dst, src).then_inc(loaded, 16)
                for n, (_, to) in enumerate(jobs):
                    if n % 2:
                        act.wait_ge(turned, n + 1)
                        src = bank_of(L, n % 4)[:, 0:2 * P].rearrange("p (k n) -> p k n", k=2)
                        nc.scalar.copy(to, src).then_inc(copied_s, 1)

            @block.vector
            def _(dve):
                step = Chain(dve, vec)
                nc.vector.memset(L.head_mean[:, :], 0.0).then_inc(memset, 1)
                for t in L.sel.values():
                    nc.vector.memset(t[:, :].bitcast(F32), 0.0).then_inc(memset, 1)
                dve.wait_ge(memset, 5)
                dve.wait_ge(sel_done, 1)
                copies = sel[:, :].rearrange("p (n c d) -> p n c d", c=4, d=HD)
                for n, rows in (("q_hi", (0, 1)), ("q_lo", (2, 3)), ("k_hi", (0, 2)), ("k_lo", (1, 3))):
                    for c in rows:
                        step(nc.vector.tensor_copy(L.sel[n][:, :].rearrange("p (n c d) -> p n c d", c=4, d=HD)[:, :, c, :], copies[:, :, c, :]))
                for j in range(2):
                    step(nc.vector.memset(L.head_mean[j * LH:(j + 1) * LH, j * LH:(j + 1) * LH], 1.0 / LH))
                dve.wait_ge(loaded, 16 * len(direct))
                step(nc.vector.tensor_scalar(L.a0q[:, :, :], L.a0q[:, :, :], HD ** -0.5, None, ALU.mult))
                step(nc.vector.tensor_scalar(L.scales[:, 0:2], L.scales[:, 0:2], 2.0, None, ALU.mult))
                step(nc.vector.tensor_scalar(L.x1bqk[:, 0, :], L.x1bqk[:, 0, :], HD ** -0.5, None, ALU.mult))
                for n, (_, to) in enumerate(jobs):
                    if n % 2 == 0:
                        dve.wait_ge(turned, n + 1)
                        src = bank_of(L, n % 4)[:, 0:2 * P].rearrange("p (k n) -> p k n", k=2)
                        nc.vector.tensor_copy(to, src).then_inc(copied_v, 1)
                dve.wait_ge(turned, len(jobs) + 1)
                step(nc.vector.tensor_copy(L.b1[:, :], bank_of(L, 4, E * EM)))
                dve.wait_ge(copied_v, (len(jobs) + 1) // 2)
                dve.wait_ge(copied_s, len(jobs) // 2)
                step(nc.vector.tensor_scalar(L.x1q[:, :, :], L.x1q[:, :, :], HD ** -0.5, None, ALU.mult))
                for w in (L.a1q, L.a1k):
                    heads = w[:, :, :].rearrange("p k (h d) -> p (k h) d", d=LH)
                    step(nc.vector.tensor_reduce(mean[:, :], heads, AX.X, ALU.add))
                    step(nc.vector.tensor_scalar(mean[:, :], mean[:, :], 1.0 / LH, None, ALU.mult))
                    step(nc.vector.tensor_tensor(heads, heads, mean[:, :].rearrange("p (h a) -> p h a", a=1).to_broadcast((P, KD * H, LH)), ALU.subtract))


def bank_of(L, i, n=512):
    return L.PS[:, i * 512:i * 512 + n]


def load_batch(nc, a, b, L):
    with Stage(nc, "load") as st:
        ctx = st.sb("ctx", [P, CT, D])
        x_in, ctx_in, turned, cv, cs = (st.sem(n) for n in ("x_in", "ctx_in", "turned", "copied_v", "copied_s"))
        jobs = [([L.x_tok[:, t, k * P:(k + 1) * P] for k in range(KD)], L.x_T[:, :, t * P:(t + 1) * P]) for t in range(T)]
        jobs += [([ctx[:, t, k * P:(k + 1) * P] for k in range(KD)], L.ctx_T[:, :, t * P:(t + 1) * P]) for t in range(CT)]
        with nc.Block("load_batch") as block:
            @block.sync
            def _(sp):
                sp.dma_start(L.x_tok[:, :, :], a["x"][bass.ds(b, 1), :, :].rearrange("a (t p) d -> p (a t) d", p=P)).then_inc(x_in, 16)

            @block.tensor
            def _(pe):
                pe.wait_ge(x_in, 16)
                for n, (pair, _) in enumerate(jobs):
                    if n == T:
                        pe.wait_ge(ctx_in, 16)
                    if n >= 4:
                        pe.wait_ge(cs if n % 2 else cv, (n - 4) // 2 + 1)
                    for k, src in enumerate(pair):
                        last = nc.tensor.transpose(bank_of(L, n % 4)[:, k * P:(k + 1) * P], src, L.ident[:, :])
                    last.then_inc(turned, 1)

            @block.scalar
            def _(act):
                act.dma_start(ctx[:, :, :], a["ctx_1024"][bass.ds(b, 1), :, :].rearrange("a (t p) d -> p (a t) d", p=P)).then_inc(ctx_in, 16)
                for n, (_, to) in enumerate(jobs):
                    if n % 2:
                        act.wait_ge(turned, n + 1)
                        nc.scalar.copy(to, bank_of(L, n % 4, 2 * P).rearrange("p (k n) -> p k n", k=2)).then_inc(cs, 1)

            @block.vector
            def _(dve):
                for n, (_, to) in enumerate(jobs):
                    if n % 2 == 0:
                        dve.wait_ge(turned, n + 1)
                        nc.vector.tensor_copy(to, bank_of(L, n % 4, 2 * P).rearrange("p (k n) -> p k n", k=2)).then_inc(cv, 1)


def store_batch(nc, b, out, x_tok):
    with Stage(nc, "store") as st:
        stored = st.sem("stored")
        with nc.Block("store_batch") as block:
            @block.sync
            def _(sp):
                sp.dma_start(out[bass.ds(b, 1), :, :].rearrange("a (t p) d -> p (a t) d", p=P), x_tok[:, :, :]).then_inc(stored, 16)
                sp.wait_ge(stored, 16)


def context_table(nc, a, b, gs, L):
    gs.selected = gs.sb("selected", [P, T, NOFF, 2 * D])
    gs.rows = gs.sb("rows", [P, NOFF, T], I32)
    gs.keep = gs.sb("keep", [P, T, NOFF])
    gs.lowest = gs.sb("lowest", [P, T, NOFF])
    gs.rows_done = gs.sem("rows_done")
    gs.gathered = [[gs.sem(f"gathered{t}_{o}") for o in range(NOFF)] for t in range(T)]
    with Stage(nc, "tab") as st:
        kv = st.sb("kv", [P, CT, 2 * D])
        tok = st.sb("tok", [P, T], I32)
        tokf = st.sb("tokf", [P, T])
        shifted = st.sb("shifted", [P, T, NOFF])
        tok_in, made, cv, cs, written, vec = (st.sem(n) for n in ("tok_in", "made", "copied_v", "copied_s", "written", "vec"))
        with nc.Block("table") as block:
            @block.sync
            def _(sp):
                with nc.allow_non_contiguous_dma("token numbers, 2 KB"):
                    sp.dma_start(tok[:, :], a["itok_BxS_0_511"][bass.ds(b, 1), :].rearrange("a (t p) -> p (a t)", p=P)).then_inc(tok_in, 16)
                for n in range(CT):
                    sp.wait_ge(cs if n % 2 else cv, n // 2 + 1)
                    sp.dma_start(L.kv_table[n * P:(n + 1) * P, :], kv[:, n, :]).then_inc(written, 16)
                sp.wait_ge(written, 16 * CT)

            @block.tensor
            def _(pe):
                for n in range(CT):
                    if n >= 4:
                        pe.wait_ge(cs if n % 2 else cv, (n - 4) // 2 + 1)
                    for k in range(KD):
                        last = nc.tensor.matmul(bank_of(L, n % 4), L.ctx_T[:, k, n * P:(n + 1) * P], L.x0kv[:, k, :],
                                                start=(k == 0), stop=(k == KD - 1))
                    last.then_inc(made, 1)

            @block.scalar
            def _(act):
                for n in range(1, CT, 2):
                    act.wait_ge(made, n + 1)
                    nc.scalar.copy(kv[:, n, :], bank_of(L, n % 4)).then_inc(cs, 1)

            @block.vector
            def _(dve):
                step = Chain(dve, vec)
                for n in range(0, CT, 2):
                    dve.wait_ge(made, n + 1)
                    nc.vector.tensor_copy(kv[:, n, :], bank_of(L, n % 4)).then_inc(cv, 1)
                dve.wait_ge(tok_in, 16)
                step(nc.vector.tensor_copy(tokf[:, :], tok[:, :]))
                for o in range(NOFF):
                    step(nc.vector.tensor_scalar(shifted[:, :, o], tokf[:, :], float(-o), None, ALU.add))
                step(nc.vector.tensor_scalar(gs.keep[:, :, :], shifted[:, :, :], 0.0, None, ALU.is_ge))
                step(nc.vector.tensor_scalar(gs.lowest[:, :, :], shifted[:, :, :], 0.0, LOWEST, ALU.is_lt, ALU.mult))
                nc.vector.tensor_scalar(gs.rows[:, :, :].rearrange("p o t -> p t o"), shifted[:, :, :], 0.0, float(SC - 1),
                                        ALU.max, ALU.min).then_inc(gs.rows_done, 1)


def project_heads(nc, st, L, name, q, k, v, sync=None, pool=None):
    plain = [(w, "qk"[w], m, c) for w in range(2) for m in range(KD) for c in range((q, k)[w][1].shape[2] // 512)]
    stack = [(w, "qk"[w], m, c) for w in range(2) for m in range(H // 2) for c in range((q, k)[w][1].shape[2] // 512)]
    NP, NS, NV = len(plain), len(stack), v[1].shape[2] // P
    with ExitStack() as tmp:
        parts = [[tmp.enter_context(nc.sbuf_tensor(f"{name}_{n}_{w}", [P, KD, x[1].shape[2]], F32R)) for w in ("hi", "lo")]
                 for n, x in (("q", q), ("k", k))]
        names = ("p_made", "hi_done", "lo_done", "v_made", "v_v", "v_s", "s_made", "s_v", "s_s")
        p_made, hi_done, lo_done, v_made, v_v, v_s, s_made, s_v, s_s = (st.sem(n) for n in names)

        def cols(c):
            return slice(c * 512, (c + 1) * 512)

        with nc.Block(name) as block:
            if sync is not None:
                block.sync(sync)
            if pool is not None:
                block.gpsimd(pool)

            @block.tensor
            def _(pe):
                for n, (w, _, m, c) in enumerate(plain):
                    if n >= 2:
                        pe.wait_ge(hi_done, n - 1)
                        pe.wait_ge(lo_done, n - 1)
                    weights, x = (q, k)[w][0:2]
                    for kt in range(KD):
                        last = nc.tensor.matmul(bank_of(L, n % 2), weights[:, kt, m * P:(m + 1) * P], x[:, kt, cols(c)], start=(kt == 0), stop=(kt == KD - 1))
                    last.then_inc(p_made, 1)
                for n in range(NV):
                    if n >= 2:
                        pe.wait_ge(v_s if n % 2 else v_v, (n - 2) // 2 + 1)
                    o = bank_of(L, 6 + n % 2, D)
                    if v[2] is not None:
                        nc.tensor.matmul(o, L.ones[:, :], v[2][:, :], start=True, stop=False)
                    for kt in range(KD):
                        last = nc.tensor.matmul(o, v[1][:, kt, n * P:(n + 1) * P], v[0][:, kt, :], start=(kt == 0 and v[2] is None), stop=(kt == KD - 1))
                    last.then_inc(v_made, 1)
                pe.wait_ge(hi_done, NP)
                pe.wait_ge(lo_done, NP)
                for n, (w, what, m, c) in enumerate(stack):
                    if n >= 4:
                        pe.wait_ge(s_s if n % 2 else s_v, (n - 4) // 2 + 1)
                    o = bank_of(L, 2 + n % 4)
                    at = slice((m % 4) * P, (m % 4 + 1) * P)
                    nc.tensor.matmul(o, L.sel[what + "_hi"][:, at], parts[w][0][:, m // 4, cols(c)], start=True, stop=False)
                    nc.tensor.matmul(o, L.sel[what + "_lo"][:, at], parts[w][1][:, m // 4, cols(c)], start=False, stop=True).then_inc(s_made, 1)

            @block.scalar
            def _(act):
                for n, (w, _, m, c) in enumerate(plain):
                    act.wait_ge(p_made, n + 1)
                    nc.scalar.activation(parts[w][0][:, m, cols(c)], bank_of(L, n % 2), ACT.Identity, bias=(q, k)[w][2](m)).then_inc(hi_done, 1)
                for n in range(1, NV, 2):
                    act.wait_ge(v_made, n + 1)
                    nc.scalar.copy(v[3][:, n, :], bank_of(L, 6 + n % 2, D)).then_inc(v_s, 1)
                for n, (w, _, m, c) in enumerate(stack):
                    if n % 2:
                        act.wait_ge(s_made, n + 1)
                        nc.scalar.copy((q, k)[w][3][:, m, cols(c)], bank_of(L, 2 + n % 4)).then_inc(s_s, 1)

            @block.vector
            def _(dve):
                for n, (w, _, m, c) in enumerate(plain):
                    dve.wait_ge(hi_done, n + 1)
                    nc.vector.scalar_tensor_tensor(out=parts[w][1][:, m, cols(c)], in0=bank_of(L, n % 2), scalar=(q, k)[w][2](m),
                                                   in1=parts[w][0][:, m, cols(c)].bitcast(F32), op0=ALU.add, op1=ALU.subtract).then_inc(lo_done, 1)
                for n in range(0, NV, 2):
                    dve.wait_ge(v_made, n + 1)
                    nc.vector.tensor_copy(v[3][:, n, :], bank_of(L, 6 + n % 2, D)).then_inc(v_v, 1)
                for n, (w, _, m, c) in enumerate(stack):
                    if n % 2 == 0:
                        dve.wait_ge(s_made, n + 1)
                        nc.vector.tensor_copy((q, k)[w][3][:, m, cols(c)], bank_of(L, 2 + n % 4)).then_inc(s_v, 1)


def attend(nc, st, L, name, qS, kS, v, sc, per_unit, keys, mask, slots, sync=None, pool=None, before=None):
    units = [(t, range(h, h + per_unit)) for t in range(T) for h in range(0, H, per_unit)]
    NU, UG = len(units), 4 // per_unit
    NG = NU // UG
    W = SC // per_unit
    pT = st.sb("pT", [P, slots, CT, P])
    oT = st.sb("oT", [P, 2, P])
    mx, nmx, den, rden = (st.sb(n, [P, T, H]) for n in ("mx", "nmx", "den", "rden"))
    names = ("cleared", "scored", "masked", "bias", "exped", "turned", "pT_v", "pT_s", "summed", "oT_done", "back", "normed", "vec")
    cleared, scored, masked, bias, exped, turned, pT_v, pT_s, summed, oT_done, back, normed, vec = (st.sem(n) for n in names)

    def width(t):
        return keys(t)[1] * P

    def column(i):
        return (i % 2 * (per_unit // 2) + i // 2) * W

    def blocks(t):
        every = [(i, c) for i in range(per_unit) for c in range(keys(t)[1])]
        return every[:len(every) // 2], every[len(every) // 2:]

    def copy_turned(copy, eng, n, done):
        u, half = n // 2, n % 2
        nb = len(blocks(units[u][0])[half])
        eng.wait_ge(turned, n + 1)
        if u >= slots:
            eng.wait_ge(summed, (u - slots) // UG + 1)
        copy(pT[:, u % slots, half * nb:(half + 1) * nb, :], bank_of(L, 4 + half, nb * P).rearrange("p (c n) -> p c n", n=P)).then_inc(done, 1)

    def groups_with_last(u):
        return [u // UG] if 0 <= u < NU and u % UG == UG - 1 else []

    with nc.Block(name) as block:
        if sync is not None:
            block.sync(lambda sp: sync(sp, masked))
        if pool is not None:
            block.gpsimd(pool)

        @block.tensor
        def _(pe):
            def scores(u):
                t, hs = units[u]
                if u >= 2:
                    pe.wait_ge(masked, per_unit * (u - 1))
                for i, h in enumerate(hs):
                    rows = slice((h % 2) * 64, (h % 2) * 64 + 64)
                    for c in range(0, width(t), 512):
                        n = min(512, width(t) - c)
                        at = 2 * (u % 2) * 512 + column(i) + c
                        k0 = keys(t)[0] * P + c
                        last = nc.tensor.matmul(L.PS[:, at:at + n], qS[rows, h // 2, t * P:(t + 1) * P], kS[rows, h // 2, k0:k0 + n], start=True, stop=True)
                last.then_inc(scored, 1)

            def turn(u):
                pe.wait_ge(exped, per_unit * (u + 1))
                for half, part in enumerate(blocks(units[u][0])):
                    if u >= 1:
                        pe.wait_ge(pT_s if half else pT_v, u)
                    for n, (i, c) in enumerate(part):
                        at = column(i) + c * P
                        last = nc.tensor.transpose(bank_of(L, 4 + half)[:, n * P:(n + 1) * P], sc[u % 4][:, at:at + P], L.ident[:, :])
                    last.then_inc(turned, 1)

            def mix(g):
                last_u = (g + 1) * UG - 1
                pe.wait_ge(pT_v, last_u + 1)
                pe.wait_ge(pT_s, last_u + 1)
                pe.wait_ge(cleared, 2)
                if g >= 2:
                    pe.wait_ge(normed, g - 1)
                t = units[last_u][0]
                first, nk = keys(t)
                for c in range(nk):
                    for j in range(4):
                        h = 4 * (g % (H // 4)) + j
                        slot = (g * UG + j // per_unit) % slots
                        last = nc.tensor.matmul(bank_of(L, 6 + g % 2)[j * PADW:j * PADW + HD, 0:P], v[:, first + c, h * HD:(h + 1) * HD],
                                                pT[:, slot, (j % per_unit) * nk + c, :], start=(c == 0), stop=(c == nk - 1))
                last.then_inc(summed, 1)

            def turn_back(g):
                pe.wait_ge(oT_done, g + 1)
                nc.tensor.transpose(bank_of(L, 6 + g % 2)[:, P:2 * P], oT[:, g % 2, :], L.ident[:, :]).then_inc(back, 1)

            for n in range(NU + 5):
                if n < NU:
                    scores(n)
                if 2 <= n < NU + 2:
                    turn(n - 2)
                for g in groups_with_last(n - 4):
                    turn_back(g)
                for g in groups_with_last(n - 3):
                    mix(g)

        @block.scalar
        def _(act):
            for n in range(NU + 5):
                for g in groups_with_last(n - 4):
                    act.wait_ge(summed, g + 1)
                    nc.scalar.copy(oT[:, g % 2, :], bank_of(L, 6 + g % 2, P)).then_inc(oT_done, 1)
                if n < NU:
                    t, hs = units[n]
                    act.wait_ge(bias, n + 1)
                    for i, h in enumerate(hs):
                        part = sc[n % 4][:, column(i):column(i) + width(t)]
                        nc.scalar.activation(part, part, ACT.Exp, bias=nmx[:, t, h:h + 1], accum_out=den[:, t, h:h + 1]).then_inc(exped, 1)
                if 2 <= n < NU + 2:
                    copy_turned(nc.scalar.copy, act, 2 * (n - 2) + 1, pT_s)

        @block.vector
        def _(dve):
            step = Chain(dve, vec)
            for i in range(2):
                nc.vector.memset(bank_of(L, 6 + i, P), 0.0).then_inc(cleared, 1)

            def normalise(g):
                t, h = g // (H // 4), 4 * (g % (H // 4))
                dve.wait_ge(back, g + 1)
                step(nc.vector.reciprocal(rden[:, t, h:h + 4], den[:, t, h:h + 4]))
                nc.vector.tensor_tensor(
                    L.mixed[:, t, h * HD:(h + 4) * HD].rearrange("p (j d) -> p j d", d=HD),
                    bank_of(L, 6 + g % 2)[:, P:2 * P].rearrange("p (j d) -> p j d", d=PADW)[:, :, 0:HD],
                    rden[:, t, h:h + 4].rearrange("p (j a) -> p j a", a=1).to_broadcast((P, 4, HD)), ALU.mult).then_inc(normed, 1)

            for n in range(NU + 5):
                for g in groups_with_last(n - 5):
                    normalise(g)
                if n < NU:
                    t, hs = units[n]
                    if before is not None:
                        before(dve, t, hs)
                    dve.wait_ge(scored, n + 1)
                    if n >= 4:
                        dve.wait_ge(turned, 2 * (n - 3))
                    for i, h in enumerate(hs):
                        at = 2 * (n % 2) * 512 + column(i)
                        nc.vector.tensor_tensor_reduce(out=sc[n % 4][:, column(i):column(i) + width(t)], in0=L.PS[:, at:at + width(t)], in1=mask(t),
                                                       scale=1.0, scalar=LOWEST, op0=ALU.add, op1=ALU.max, accum_out=mx[:, t, h:h + 1]).then_inc(masked, 1)
                    dve.wait_ge(masked, per_unit * (n + 1))
                    h = hs[0]
                    nc.vector.tensor_scalar(nmx[:, t, h:h + per_unit], mx[:, t, h:h + per_unit], -1.0, None, ALU.mult).then_inc(bias, 1)
                if 2 <= n < NU + 2:
                    copy_turned(nc.vector.tensor_copy, dve, 2 * (n - 2), pT_v)


def window_attention(nc, gs, L):
    with Stage(nc, "win") as st:
        qS, kS = st.sb("qS", [P, H // 2, S], F32R), st.sb("kS", [P, H // 2, S], F32R)
        v = st.sb("v", [P, T, D])

        def gather(pool):
            pool.wait_ge(gs.rows_done, 1)
            for t in range(T):
                for o in range(NOFF):
                    nc.gpsimd.indirect_dma_start(
                        out=gs.selected[:, t, o, :], out_offset=None, in_=L.kv_table,
                        in_offset=bass.IndirectOffsetOnAxis(ap=gs.rows[:, o, t:t + 1], axis=0)).then_inc(gs.gathered[t][o], 16)

        def keys(t):
            return max(t - 1, 0), min(t, 1) + 1

        def no_bias(m):
            return L.zero[:, :]

        project_heads(nc, st, L, "win_project", (L.a0q, L.x_T, no_bias, qS), (L.a0k, L.x_T, no_bias, kS), (L.a0v, L.x_T, None, v))
        sc = st.sb("sc", [P, 4, SC])
        attend(nc, st, L, "window", qS, kS, v, [sc[:, i, :] for i in range(4)], 4, keys, lambda t: L.window[:, 2 * P - P * keys(t)[1]:2 * P], 3, pool=gather)


def project_norm(nc, name, L, weight, bias):
    with Stage(nc, name) as st:
        mT = st.sb("mT", [P, T, KD, P])
        res = st.sb("res", [P, T, D])
        turned, mT_done, made = st.sem("turned"), st.sem("mT_done"), st.sem("made")
        tail = NormTail(nc, st, L, res, turned_banks=(6, 7))
        with nc.Block(name) as block:
            @block.tensor
            def _(pe):
                for t in range(T):
                    for k in range(KD):
                        last = nc.tensor.transpose(bank_of(L, t)[:, k * P:(k + 1) * P], L.mixed[:, t, k * P:(k + 1) * P], L.ident[:, :])
                    last.then_inc(turned, 1)
                for t in range(T):
                    pe.wait_ge(mT_done, t + 1)
                    o = bank_of(L, 4 + t % 2, D)
                    if t >= 2:
                        pe.wait_ge(tail.added, t - 1)
                    if bias is not None:
                        nc.tensor.matmul(o, L.ones[:, :], bias[:, :], start=True, stop=False)
                    for k in range(KD):
                        last = nc.tensor.matmul(o, mT[:, t, k, :], weight[:, k, :], start=(k == 0 and bias is None), stop=(k == KD - 1))
                    last.then_inc(made, 1)
                tail.turn(pe)

            @block.scalar
            def _(act):
                for t in range(T):
                    act.wait_ge(turned, t + 1)
                    nc.scalar.copy(mT[:, t, :, :], bank_of(L, t, KD * P).rearrange("p (k n) -> p k n", k=KD)).then_inc(mT_done, 1)
                tail.finish(act)

            @block.vector
            def _(dve):
                step = Chain(dve, tail.vec)
                for t in range(T):
                    dve.wait_ge(made, t + 1)
                    nc.vector.tensor_tensor(res[:, t, :], bank_of(L, 4 + t % 2, D), L.x_tok[:, t, :], ALU.add).then_inc(tail.added, 1)
                    dve.wait_ge(tail.added, t + 1)
                    tail.stats_of(step, t)
                    if t >= 1:
                        tail.norm(dve, t - 1)
                tail.norm(dve, T - 1)


class NormTail:

    def __init__(self, nc, st, L, res, turned_banks, turn_x=True):
        self.nc, self.L, self.res, self.banks = nc, L, res, turned_banks
        self.stats, self.mv = st.sb("stats", [P, T, 6]), st.sb("mv", [P, T, 2])
        self.std, self.rstd = st.sb("std", [P, T]), st.sb("rstd", [P, T])
        self.added, self.var_done, self.std_done, self.rstd_done, self.new_x, self.x_turned, self.xT_done, self.vec = (
            st.sem(n) for n in ("added", "var_done", "std_done", "rstd_done", "new_x", "x_turned", "xT_done", "vec"))

    def stats_of(self, step, t):
        step(self.nc.vector.bn_stats(self.stats[:, t, :], self.res[:, t, :]))
        self.nc.vector.bn_aggr(self.mv[:, t, :], self.stats[:, t, :]).then_inc(self.var_done, 1)

    def norm(self, dve, t):
        dve.wait_ge(self.std_done, t + 1)
        self.nc.vector.reciprocal(self.rstd[:, t:t + 1], self.std[:, t:t + 1]).then_inc(self.rstd_done, 1)
        dve.wait_ge(self.rstd_done, t + 1)
        self.nc.vector.tensor_scalar(self.L.x_tok[:, t, :], self.res[:, t, :], self.mv[:, t, 0:1], self.rstd[:, t:t + 1],
                                     ALU.subtract, ALU.mult).then_inc(self.new_x, 1)

    def turn(self, pe):
        for t in range(T):
            pe.wait_ge(self.new_x, t + 1)
            if t >= 2:
                pe.wait_ge(self.xT_done, t - 1)
            for k in range(KD):
                last = self.nc.tensor.transpose(bank_of(self.L, self.banks[t % 2])[:, k * P:(k + 1) * P],
                                                self.L.x_tok[:, t, k * P:(k + 1) * P], self.L.ident[:, :])
            last.then_inc(self.x_turned, 1)

    def finish(self, act, turned=True):
        def copy_turned(t):
            act.wait_ge(self.x_turned, t + 1)
            self.nc.scalar.copy(self.L.x_T[:, :, t * P:(t + 1) * P],
                                bank_of(self.L, self.banks[t % 2], KD * P).rearrange("p (k n) -> p k n", k=KD)).then_inc(self.xT_done, 1)

        for t in range(T):
            act.wait_ge(self.var_done, t + 1)
            self.nc.scalar.activation(self.std[:, t:t + 1], self.mv[:, t, 1:2], ACT.Sqrt, bias=self.L.eps[:, :]).then_inc(self.std_done, 1)
            if turned and t >= 1:
                copy_turned(t - 1)
        if turned:
            copy_turned(T - 1)


def gather_attention(nc, gs, L):
    with Stage(nc, "gatt") as st:
        q = st.sb("q", [P, 2, D])
        pk, pv = st.sb("pk", [P, 2, NOFF, D]), st.sb("pv", [P, 2, NOFF, D])
        s = st.sb("s", [P, T, NOFF, H])
        m, den, rden = (st.sb(n, [P, T, H]) for n in ("m", "den", "rden"))
        e = st.sb("e", [P, T, NOFF, H])
        made, q_done, centred, exped, weighted, summed, vec = (
            st.sem(n) for n in ("made", "q_done", "centred", "exped", "weighted", "summed", "vec"))

        def heads(ap):
            return ap.rearrange("p o (h d) -> p (o h) d", d=HD)

        with nc.Block("gather_attention") as block:
            @block.tensor
            def _(pe):
                for t in range(T):
                    if t >= 2:
                        pe.wait_ge(q_done, t - 1)
                    for k in range(KD):
                        last = nc.tensor.matmul(bank_of(L, t % 2, D), L.x_T[:, k, t * P:(t + 1) * P], L.x0q[:, k, :],
                                                start=(k == 0), stop=(k == KD - 1))
                    last.then_inc(made, 1)

            @block.scalar
            def _(act):
                for t in range(T):
                    act.wait_ge(made, t + 1)
                    if t >= 2:
                        act.wait_ge(centred, t - 1)
                    nc.scalar.mul(q[:, t % 2, :], bank_of(L, t % 2, D), HD ** -0.5).then_inc(q_done, 1)
                    if t >= 1:
                        act.wait_ge(centred, t)
                        nc.scalar.activation(e[:, t - 1, :, :], s[:, t - 1, :, :], ACT.Exp).then_inc(exped, 1)
                act.wait_ge(centred, T)
                nc.scalar.activation(e[:, T - 1, :, :], s[:, T - 1, :, :], ACT.Exp).then_inc(exped, 1)

            @block.gpsimd
            def _(pool):
                for t in range(T):
                    for o in range(NOFF):
                        pool.wait_ge(gs.gathered[t][o], 16)
                nc.gpsimd.dma_reset()
                for t in range(T):
                    pool.wait_ge(exped, t + 1)
                    if t >= 2:
                        pool.wait_ge(summed, t - 1)
                    nc.gpsimd.tensor_tensor(
                        pv[:, t % 2, :, :].rearrange("p o (h d) -> p o h d", d=HD), gs.selected[:, t, :, D:2 * D].rearrange("p o (h d) -> p o h d", d=HD),
                        e[:, t, :, :].rearrange("p o (h a) -> p o h a", a=1).to_broadcast((P, NOFF, H, HD)), ALU.mult).then_inc(weighted, 1)

            @block.vector
            def _(dve):
                step = Chain(dve, vec)

                def out(t):
                    dve.wait_ge(exped, t + 1)
                    step(nc.vector.tensor_reduce(den[:, t, :], e[:, t, :, :].rearrange("p o h -> p h o"), AX.X, ALU.add))
                    step(nc.vector.reciprocal(rden[:, t, :], den[:, t, :]))
                    dve.wait_ge(weighted, t + 1)
                    nc.vector.tensor_reduce(L.mixed[:, t, :], pv[:, t % 2, :, :].rearrange("p o n -> p n o"), AX.X, ALU.add).then_inc(summed, 1)
                    dve.wait_ge(summed, t + 1)
                    view = L.mixed[:, t, :].rearrange("p (h d) -> p h d", d=HD)
                    step(nc.vector.tensor_tensor(view, view, rden[:, t, :].rearrange("p (h a) -> p h a", a=1).to_broadcast((P, H, HD)), ALU.mult))

                for t in range(T):
                    dve.wait_ge(q_done, t + 1)
                    for o in range(NOFF):
                        dve.wait_ge(gs.gathered[t][o], 16)
                    step(nc.vector.tensor_tensor(pk[:, t % 2, :, :], gs.selected[:, t, :, 0:D],
                                                 q[:, t % 2, :].rearrange("p (a n) -> p a n", a=1).to_broadcast((P, NOFF, D)), ALU.mult))
                    step(nc.vector.tensor_reduce(s[:, t, :, :], heads(pk[:, t % 2, :, :]), AX.X, ALU.add))
                    for mask, op in ((gs.keep, ALU.mult), (gs.lowest, ALU.add)):
                        step(nc.vector.tensor_tensor(s[:, t, :, :], s[:, t, :, :],
                                                     mask[:, t, :].rearrange("p (o a) -> p o a", a=1).to_broadcast((P, NOFF, H)), op))
                    step(nc.vector.tensor_reduce(m[:, t, :], s[:, t, :, :].rearrange("p o h -> p h o"), AX.X, ALU.max))
                    nc.vector.tensor_tensor(s[:, t, :, :], s[:, t, :, :],
                                            m[:, t, :].rearrange("p (a h) -> p a h", a=1).to_broadcast((P, NOFF, H)), ALU.subtract).then_inc(centred, 1)
                    if t >= 1:
                        out(t - 1)
                out(T - 1)



def sign_ffn(nc, L):
    NR = 3
    with Stage(nc, "ffn") as st:
        def pair(name, shape):
            return [st.sb(f"{name}_{w}", shape, F32R) for w in ("hi", "lo")]
        h1, h2 = pair("h1", [P, FM, S]), pair("h2", [P, FM, S])
        x2 = [h[:, 0:KD, :] for h in h2]
        w0 = st.sb("w0", [P, KD, F], F32R)
        w1 = st.sb("w1", [P, NR, FM, P], F32R)
        w2 = st.sb("w2", [P, FM, D], F32R)
        full = st.sb("full", [P, 4, S])
        w0_half = L.mixed[:, 0:2, :].rearrange("p m (k n) -> p m k n", k=KD)
        res = L.mixed
        names = ("w0_done", "w1_done", "w2_done", "x_hi", "x_lo", "made", "relued", "hi_done", "lo_done", "summed")
        w0_done, w1_done, w2_done, x_hi, x_lo, made, relued, hi_done, lo_done, summed = (st.sem(n) for n in names)
        tail = NormTail(nc, st, L, res, turned_banks=(6, 7))
        NT = 2 * FM

        with nc.Block("sign_ffn") as block:
            @block.gpsimd
            def _(pool):
                nc.gpsimd.tensor_copy(x2[0][:, :, :], L.x_T[:, :, :]).then_inc(x_hi, 1)
                for n in range(FM):
                    if n >= NR:
                        pool.wait_ge(made, FM + n - NR + 1)
                    nc.gpsimd.tensor_scalar(w1[:, n % NR, :, :], L.k1[:, :, n * P:(n + 1) * P], 2.0, -1.0, ALU.mult, ALU.add).then_inc(w1_done, 1)
                for k in range(FM):
                    nc.gpsimd.tensor_scalar(w2[:, k, :], L.k2[:, k, :], 2.0, -1.0, ALU.mult, ALU.add).then_inc(w2_done, 1)

            @block.tensor
            def _(pe):
                pe.wait_ge(x_lo, 1)
                for n in range(NT):
                    layer, m = n // FM, n % FM
                    if n >= 4:
                        pe.wait_ge(relued, n - 3)
                    if layer == 0:
                        pe.wait_ge(w0_done, m + 1)
                    else:
                        pe.wait_ge(w1_done, m + 1)
                    ks = KD if layer == 0 else FM
                    for k in range(ks):
                        if layer == 1 and m == 0:
                            pe.wait_ge(lo_done, k + 1)
                        for part in range(2):
                            w = w0[:, k, m * P:(m + 1) * P] if layer == 0 else w1[:, m % NR, k, :]
                            x = (x2 if layer == 0 else h1)[part][:, k, :]
                            last = nc.tensor.matmul(bank_of(L, n % 4), w, x, start=(k == 0 and part == 0), stop=(k == ks - 1 and part == 1))
                    last.then_inc(made, 1)
                pe.wait_ge(lo_done, NT)
                pe.wait_ge(w2_done, FM)
                for t in range(T):
                    if t >= 2:
                        pe.wait_ge(tail.added, t - 1)
                    for k in range(FM):
                        for part in range(2):
                            last = nc.tensor.matmul(bank_of(L, 4 + t % 2, D), h2[part][:, k, t * P:(t + 1) * P], w2[:, k, :],
                                                    start=(k == 0 and part == 0), stop=(k == FM - 1 and part == 1))
                    last.then_inc(summed, 1)
                tail.turn(pe)

            @block.scalar
            def _(act):
                for n in range(NT):
                    act.wait_ge(made, n + 1)
                    if n >= 4:
                        act.wait_ge(lo_done, n - 3)
                    layer = n // FM
                    nc.scalar.activation(full[:, n % 4, :], bank_of(L, n % 4), ACT.Relu,
                                         scale=L.scales[:, layer:layer + 1]).then_inc(relued, 1)
                    act.wait_ge(relued, n + 1)
                    nc.scalar.copy((h1 if n < FM else h2)[0][:, n % FM, :], full[:, n % 4, :]).then_inc(hi_done, 1)
                tail.finish(act)

            @block.vector
            def _(dve):
                step = Chain(dve, tail.vec)
                dve.wait_ge(x_hi, 1)
                nc.vector.tensor_tensor(x2[1][:, :, :], L.x_T[:, :, :], x2[0][:, :, :].bitcast(F32), ALU.subtract).then_inc(x_lo, 1)
                for m in range(FM):
                    w = w0[:, :, m * P:(m + 1) * P]
                    cols = slice(m * P, (m + 1) * P)
                    tmp = w0_half[:, m % 2, :, :]
                    if m >= 2:
                        dve.wait_ge(w0_done, m - 1)
                    step(nc.vector.tensor_tensor(tmp, L.k0[:, 0:KD, cols], L.k0[:, KD:2 * KD, cols], ALU.subtract))
                    nc.vector.tensor_scalar(w, tmp, 2.0, None, ALU.mult).then_inc(w0_done, 1)
                for n in range(NT):
                    dve.wait_ge(hi_done, n + 1)
                    h = h1 if n < FM else h2
                    nc.vector.tensor_tensor(h[1][:, n % FM, :], full[:, n % 4, :], h[0][:, n % FM, :].bitcast(F32), ALU.subtract).then_inc(lo_done, 1)
                for t in range(T):
                    dve.wait_ge(summed, t + 1)
                    nc.vector.scalar_tensor_tensor(out=res[:, t, :], in0=bank_of(L, 4 + t % 2, D), scalar=L.scales[:, 2:3],
                                                   in1=L.x_tok[:, t, :], op0=ALU.mult, op1=ALU.add).then_inc(tail.added, 1)
                    dve.wait_ge(tail.added, t + 1)
                    tail.stats_of(step, t)
                    if t >= 1:
                        tail.norm(dve, t - 1)
                tail.norm(dve, T - 1)


def linear_attention(nc, L):
    NQK = 2 * LM
    NV = 2 * T
    units = [(m, i, j) for m in range(LM) for i in range(T) for j in range(2)]
    NU = len(units)
    with Stage(nc, "lin") as st:
        qk = [st.sb("qT", [P, LM, S]), st.sb("kT", [P, LM, S])]
        v = st.sb("v", [P, T, LD])
        oT = st.sb("oT", [P, LM, S])
        sq, std, normed = (st.sb(n, [P, 2, S]) for n in ("sq", "root", "normed"))
        aT = st.sb("aT", [P, 4, S])
        res = L.mixed
        names = ("made", "squared", "meaned", "rooted", "divided", "scaled", "v_made", "v_v", "v_s", "scored", "copied",
                 "ready_v", "ready_p", "mixed_in", "oT_v", "oT_s", "summed")
        (made, squared, meaned, rooted, divided, scaled, v_made, v_v, v_s, scored, copied,
         ready_v, ready_p, mixed_in, oT_v, oT_s, summed) = (st.sem(n) for n in names)
        tail = NormTail(nc, st, L, res, turned_banks=(2, 3))

        def width(i):
            return S - i * P

        with nc.Block("linear") as block:
            def take_oT(copy, eng, m, done):
                eng.wait_ge(mixed_in, 8 * (m + 1))
                copy(oT[:, m, :], bank_of(L, 6 + m % 2)).then_inc(done, 1)

            @block.tensor
            def _(pe):
                def mean_square(n):
                    pe.wait_ge(squared, n + 1)
                    if n >= 2:
                        pe.wait_ge(rooted, n - 1)
                    nc.tensor.matmul(bank_of(L, 4 + n % 2), L.head_mean[:, :], sq[:, n % 2, :], start=True, stop=True).then_inc(meaned, 1)

                for n in range(NQK):
                    if n >= 4:
                        pe.wait_ge(divided, n - 3)
                    w = L.a1q if n < LM else L.a1k
                    m = n % LM
                    for k in range(KD):
                        last = nc.tensor.matmul(bank_of(L, n % 4), w[:, k, m * P:(m + 1) * P], L.x_T[:, k, :], start=(k == 0), stop=(k == KD - 1))
                    last.then_inc(made, 1)
                    if n >= 1:
                        mean_square(n - 1)
                    if n < NV:
                        if n >= 2:
                            pe.wait_ge(v_s if n % 2 else v_v, (n - 2) // 2 + 1)
                        t, half = n // 2, n % 2
                        for k in range(KD):
                            last = nc.tensor.matmul(bank_of(L, 6 + n % 2), L.x_T[:, k, t * P:(t + 1) * P],
                                                    L.a1v[:, k, half * 512:(half + 1) * 512], start=(k == 0), stop=(k == KD - 1))
                        last.then_inc(v_made, 1)
                mean_square(NQK - 1)
                pe.wait_ge(divided, NQK)
                pe.wait_ge(v_v, NV // 2)
                pe.wait_ge(v_s, NV // 2)

                def scores(u):
                    m, i, j = units[u]
                    if i == 0 and j == 0:
                        pe.wait_ge(scaled, LM + m + 1)
                    if u >= 4:
                        pe.wait_ge(copied if j else ready_v, (u - 4) // 2 + 1)
                    rows = slice(j * LH, (j + 1) * LH)
                    nc.tensor.matmul(bank_of(L, u % 4, width(i)), qk[1][rows, m, i * P:(i + 1) * P], qk[0][rows, m, i * P:S],
                                     start=True, stop=True).then_inc(scored, 1)

                def mix(u):
                    m, i, j = units[u]
                    pe.wait_ge(ready_p if j else ready_v, u // 2 + 1)
                    if i == 0 and j == 0 and m >= 2:
                        pe.wait_ge(oT_s if m % 2 else oT_v, (m - 2) // 2 + 1)
                    h = 2 * m + j
                    nc.tensor.matmul(bank_of(L, 6 + m % 2)[j * LH:(j + 1) * LH, i * P:S], v[:, i, h * LH:(h + 1) * LH],
                                     aT[:, u % 4, 0:width(i)], start=(i == 0), stop=(i == T - 1)).then_inc(mixed_in, 1)

                for n in range(NU + 2):
                    if n < NU:
                        scores(n)
                    if n >= 2:
                        mix(n - 2)
                pe.wait_ge(oT_v, LM // 2)
                pe.wait_ge(oT_s, LM // 2)
                for t in range(T):
                    if t >= 2:
                        pe.wait_ge(tail.added, t - 1)
                    for k in range(LM):
                        last = nc.tensor.matmul(bank_of(L, 4 + t % 2, D), oT[:, k, t * P:(t + 1) * P], L.a1o[:, k, :], start=(k == 0), stop=(k == LM - 1))
                    last.then_inc(summed, 1)
                tail.turn(pe)

            @block.scalar
            def _(act):
                def root(n):
                    act.wait_ge(meaned, n + 1)
                    if n >= 2:
                        act.wait_ge(divided, n - 1)
                    nc.scalar.activation(std[:, n % 2, :], bank_of(L, 4 + n % 2), ACT.Sqrt, bias=L.eps[:, :]).then_inc(rooted, 1)

                for n in range(NQK):
                    act.wait_ge(made, n + 1)
                    if n >= 2:
                        act.wait_ge(meaned, n - 1)
                    nc.scalar.activation(sq[:, n % 2, :], bank_of(L, n % 4), ACT.Square).then_inc(squared, 1)
                    if n >= 1:
                        root(n - 1)
                    if n < NV and n % 2:
                        act.wait_ge(v_made, n + 1)
                        nc.scalar.copy(v[:, n // 2, 512:LD], bank_of(L, 6 + n % 2)).then_inc(v_s, 1)
                root(NQK - 1)
                for u in range(NU):
                    m, i, j = units[u]
                    if j:
                        act.wait_ge(scored, u + 1)
                        if u >= 4:
                            act.wait_ge(mixed_in, u - 3)
                        nc.scalar.copy(aT[:, u % 4, 0:width(i)], bank_of(L, u % 4, width(i))).then_inc(copied, 1)
                        if i == 1 and m >= 1 and (m - 1) % 2:
                            take_oT(nc.scalar.copy, act, m - 1, oT_s)
                take_oT(nc.scalar.copy, act, LM - 1, oT_s)
                tail.finish(act)

            @block.gpsimd
            def _(pool):
                for n in range(NQK):
                    pool.wait_ge(divided, n + 1)
                    i = 0 if n < LM else 2
                    nc.gpsimd.tensor_scalar(qk[n // LM][:, n % LM, :], normed[:, n % 2, :], L.gains[:, i:i + 1], L.gains[:, i + 1:i + 2],
                                            ALU.mult, ALU.add).then_inc(scaled, 1)
                for u in range(1, NU, 2):
                    pool.wait_ge(copied, u // 2 + 1)
                    nc.gpsimd.affine_select(out=aT[:, u % 4, 0:P], in_=aT[:, u % 4, 0:P], compare_op=ALU.is_ge, fill=0.0,
                                            base=0, pattern=[[1, P]], channel_multiplier=-1).then_inc(ready_p, 1)

            @block.vector
            def _(dve):
                step = Chain(dve, tail.vec)

                def divide(n):
                    dve.wait_ge(rooted, n + 1)
                    if n >= 2:
                        dve.wait_ge(scaled, n - 1)
                    step(nc.vector.reciprocal(std[:, n % 2, :], std[:, n % 2, :]))
                    nc.vector.tensor_tensor(normed[:, n % 2, :], bank_of(L, n % 4), std[:, n % 2, :], ALU.mult).then_inc(divided, 1)

                for n in range(NQK):
                    if n < NV and n % 2 == 0:
                        dve.wait_ge(v_made, n + 1)
                        nc.vector.tensor_copy(v[:, n // 2, 0:512], bank_of(L, 6 + n % 2)).then_inc(v_v, 1)
                    if n >= 1:
                        divide(n - 1)
                divide(NQK - 1)
                for u in range(NU):
                    m, i, j = units[u]
                    if j == 0:
                        dve.wait_ge(scored, u + 1)
                        if u >= 4:
                            dve.wait_ge(mixed_in, u - 3)
                        nc.vector.tensor_tensor(aT[:, u % 4, 0:width(i)], bank_of(L, u % 4, width(i)), L.causal[:, 0:width(i)], ALU.mult).then_inc(ready_v, 1)
                        if i == 1 and m >= 1 and (m - 1) % 2 == 0:
                            take_oT(nc.vector.tensor_copy, dve, m - 1, oT_v)
                for t in range(T):
                    dve.wait_ge(summed, t + 1)
                    nc.vector.tensor_tensor(res[:, t, :], bank_of(L, 4 + t % 2, D), L.x_tok[:, t, :], ALU.add).then_inc(tail.added, 1)
                    dve.wait_ge(tail.added, t + 1)
                    tail.stats_of(step, t)
                    if t >= 1:
                        tail.norm(dve, t - 1)
                tail.norm(dve, T - 1)


def cross_attention(nc, a, L):
    with Stage(nc, "cross") as st:
        qS, kS = st.sb("qS", [P, H // 2, S], F32R), st.sb("kS", [P, H // 2, SC], F32R)
        v = st.sb("v", [P, CT, D])

        def bias_of(i):
            return lambda m: L.x1bqk[:, i, m:m + 1]

        mask = st.sb("mask", [P, 2, SC])
        mask_in, mask_done = [st.sem("mask_in0"), st.sem("mask_in1")], st.sem("mask_done")

        def load(sp, t):
            sp.dma_start(mask[:, t % 2, :], a["mask_SxS2_fk1"][t * P:(t + 1) * P, :]).then_inc(mask_in[t % 2], 16)

        def load_first(sp):
            for t in range(2):
                load(sp, t)

        def load_rest(sp, masked):
            for t in range(2, T):
                sp.wait_ge(masked, H * (t - 1))
                load(sp, t)

        def scale(t):
            nc.gpsimd.wait_ge(mask_in[t % 2], 16 * (t // 2 + 1))
            nc.gpsimd.tensor_scalar(mask[:, t % 2, :], mask[:, t % 2, :], NEG, None, ALU.mult).then_inc(mask_done, 1)

        def mask_ready(dve, t, hs):
            if hs[0] == 0:
                dve.wait_ge(mask_done, t + 1)

        project_heads(nc, st, L, "cross_project", (L.x1q, L.x_T, bias_of(0), qS), (L.x1k, L.ctx_T, bias_of(1), kS),
                      (L.x1v, L.ctx_T, L.x1bv, v), sync=load_first, pool=lambda pool: [scale(t) for t in range(2)])
        rest = st.sb("sc", [P, 2, SC])
        sc = [L.ctx_T[:, 0, :], L.ctx_T[:, 1, :], rest[:, 0, :], rest[:, 1, :]]
        attend(nc, st, L, "cross", qS, kS, v, sc, 1, lambda t: (0, CT), lambda t: mask[:, t % 2, :], 6,
               sync=load_rest, pool=lambda pool: [scale(t) for t in range(2, T)], before=mask_ready)


def experts(nc, a, L):
    PROD = ((0, 1), (1, 0), (0, 0))
    with Stage(nc, "moe") as st:
        def pair(name, shape):
            return [st.sb(f"{name}_{w}", shape, F32R) for w in ("hi", "lo")]
        x2 = pair("x", [P, KD, S])
        w1, w2 = st.sb("w1", [P, 2, KD, ED]), st.sb("w2", [P, 2, EM, D])
        w1p, w2p = pair("w1", [P, 2, KD, ED]), pair("w2", [P, 2, EM, D])
        full = st.sb("full", [P, 4, S])
        hp = pair("h", [P, 2, EM, S])
        logit, prob, rest, top8, cw = (st.sb(n, [P, T, E]) for n in ("logit", "prob", "rest", "top8", "cw"))
        lmax, lden = st.sb("lmax", [P, T]), st.sb("lden", [P, T])
        cwT = st.sb("cwT", [E, T, P])
        acc = L.mixed
        w_in = [st.sem("w_in0"), st.sem("w_in1")]
        names = ("x_hi", "x_lo", "w_hi", "w_lo", "routed", "shifted", "exped", "cw_done", "cw_turned", "cwT_done", "biased", "acc_done",
                 "made", "relued", "hi_done", "lo_done", "summed")
        (x_hi, x_lo, w_hi, w_lo, routed, shifted, exped, cw_done, cw_turned, cwT_done, biased, acc_done,
         made, relued, hi_done, lo_done, summed) = (st.sem(n) for n in names)
        tail = NormTail(nc, st, L, acc, turned_banks=None)

        with nc.Block("experts") as block:
            @block.sync
            def _(sp):
                for e in range(E):
                    if e >= 2:
                        sp.wait_ge(w_lo, 2 * (e - 1))
                    sp.dma_start(w1[:, e % 2, :, :], a["L1_ffn_W1"][e].rearrange("(k p) n -> p k n", p=P)).then_inc(w_in[e % 2], 16)
                    sp.dma_start(w2[:, e % 2, :, :], a["L1_ffn_W2"][e].rearrange("(k p) n -> p k n", p=P)).then_inc(w_in[e % 2], 16)

            @block.gpsimd
            def _(pool):
                nc.gpsimd.tensor_copy(x2[0][:, :, :], L.x_T[:, :, :]).then_inc(x_hi, 1)
                pool.wait_ge(x_hi, 1)
                nc.gpsimd.tensor_tensor(x2[1][:, :, :], L.x_T[:, :, :], x2[0][:, :, :].bitcast(F32), ALU.subtract).then_inc(x_lo, 1)
                for e in range(E):
                    pool.wait_ge(w_in[e % 2], 32 * (e // 2 + 1))
                    s = e % 2
                    for n, (w, wp) in enumerate(((w1, w1p), (w2, w2p))):
                        if e >= 2:
                            pool.wait_ge(summed if n else made, EM * (e - 1))
                        nc.gpsimd.tensor_copy(wp[0][:, s, :, :], w[:, s, :, :]).then_inc(w_hi, 1)
                        pool.wait_ge(w_hi, 2 * e + n + 1)
                        nc.gpsimd.tensor_tensor(wp[1][:, s, :, :], w[:, s, :, :], wp[0][:, s, :, :].bitcast(F32), ALU.subtract).then_inc(w_lo, 1)

            @block.tensor
            def _(pe):
                for t in range(T):
                    o = bank_of(L, 4)[:, t * E:(t + 1) * E]
                    nc.tensor.matmul(o, L.ones[:, :], L.br[:, :], start=True, stop=False)
                    for k in range(KD):
                        last = nc.tensor.matmul(o, L.x_T[:, k, t * P:(t + 1) * P], L.wr[:, k, :], start=False, stop=(k == KD - 1))
                    last.then_inc(routed, 1)

                def up(e):
                    pe.wait_ge(w_lo, 2 * e + 1)
                    for m in range(EM):
                        n = e * EM + m
                        if n >= 4:
                            pe.wait_ge(relued, n - 3)
                        for k in range(KD):
                            for i, (p, q) in enumerate(PROD):
                                last = nc.tensor.matmul(bank_of(L, n % 4), w1p[p][:, e % 2, k, m * P:(m + 1) * P], x2[q][:, k, :],
                                                        start=(k == 0 and i == 0), stop=(k == KD - 1 and i == 2))
                        last.then_inc(made, 1)

                def down(e):
                    pe.wait_ge(w_lo, 2 * e + 2)
                    for t in range(T):
                        n = e * T + t
                        if n >= 4:
                            pe.wait_ge(acc_done, T + n - 3)
                        for k in range(EM):
                            if t == 0:
                                pe.wait_ge(lo_done, e * EM + k + 1)
                            for i, (p, q) in enumerate(PROD):
                                last = nc.tensor.matmul(bank_of(L, 4 + n % 4, D), hp[p][:, e % 2, k, t * P:(t + 1) * P], w2p[q][:, e % 2, k, :],
                                                        start=(k == 0 and i == 0), stop=(k == EM - 1 and i == 2))
                        last.then_inc(summed, 1)

                pe.wait_ge(x_lo, 1)
                up(0)
                for t in range(T):
                    pe.wait_ge(cw_done, t + 1)
                    nc.tensor.transpose(bank_of(L, 5)[0:E, t * P:(t + 1) * P], cw[:, t, :], L.ident[:, :]).then_inc(cw_turned, 1)
                for t in range(T):
                    pe.wait_ge(cwT_done, 1)
                    nc.tensor.matmul(bank_of(L, 6 + t % 2)[:, (t // 2) * D:(t // 2 + 1) * D], cwT[:, t, :], L.b2[:, :], start=True, stop=True).then_inc(biased, 1)
                pe.wait_ge(acc_done, T)
                for e in range(1, E):
                    up(e)
                    down(e - 1)
                down(E - 1)

            @block.scalar
            def _(act):
                def relu(n):
                    act.wait_ge(made, n + 1)
                    if n >= 4:
                        act.wait_ge(lo_done, n - 3)
                    nc.scalar.activation(full[:, n % 4, :], bank_of(L, n % 4), ACT.Relu, bias=L.b1[:, n:n + 1]).then_inc(relued, 1)
                    act.wait_ge(relued, n + 1)
                    e, m = n // EM, n % EM
                    if e >= 2:
                        act.wait_ge(summed, T * (e - 1))
                    nc.scalar.copy(hp[0][:, e % 2, m, :], full[:, n % 4, :]).then_inc(hi_done, 1)

                for t in range(T):
                    act.wait_ge(shifted, t + 1)
                    nc.scalar.activation(prob[:, t, :], logit[:, t, :], ACT.Exp, accum_out=lden[:, t:t + 1]).then_inc(exped, 1)
                act.wait_ge(cw_turned, T)
                nc.scalar.copy(cwT[:, :, :], bank_of(L, 5)[0:E, :].rearrange("e (t p) -> e t p", p=P)).then_inc(cwT_done, 1)
                for n in range(E * EM):
                    relu(n)
                tail.finish(act, turned=False)

            @block.vector
            def _(dve):
                step = Chain(dve, tail.vec)
                dve.wait_ge(routed, T)
                step(nc.vector.tensor_copy(logit[:, :, :], bank_of(L, 4, T * E).rearrange("p (t e) -> p t e", e=E)))
                step(nc.vector.tensor_reduce(lmax[:, :], logit[:, :, :], AX.X, ALU.max))
                for t in range(T):
                    nc.vector.tensor_scalar(logit[:, t, :], logit[:, t, :], lmax[:, t:t + 1], None, ALU.subtract).then_inc(shifted, 1)
                dve.wait_ge(exped, T)
                step(nc.vector.reciprocal(lden[:, :], lden[:, :]))
                for t in range(T):
                    step(nc.vector.tensor_scalar(prob[:, t, :], prob[:, t, :], lden[:, t:t + 1], None, ALU.mult))
                    step(nc.vector.max(top8[:, t, :], prob[:, t, :]))
                    step(nc.vector.memset(top8[:, t, 2:E], -1.0))
                    step(nc.vector.match_replace(rest[:, t, :], top8[:, t, :], prob[:, t, :], 0.0))
                    nc.vector.tensor_tensor(cw[:, t, :], prob[:, t, :], rest[:, t, :], ALU.subtract).then_inc(cw_done, 1)
                for t in range(T):
                    dve.wait_ge(biased, t + 1)
                for t in range(T):
                    nc.vector.tensor_tensor(acc[:, t, :], bank_of(L, 6 + t % 2)[:, (t // 2) * D:(t // 2 + 1) * D], L.x_tok[:, t, :], ALU.add).then_inc(acc_done, 1)

                def low(n):
                    dve.wait_ge(hi_done, n + 1)
                    e, m = n // EM, n % EM
                    nc.vector.tensor_tensor(hp[1][:, e % 2, m, :], full[:, n % 4, :], hp[0][:, e % 2, m, :].bitcast(F32), ALU.subtract).then_inc(lo_done, 1)

                def add(n):
                    e, t = n // T, n % T
                    dve.wait_ge(summed, n + 1)
                    dve.wait_ge(acc_done, n + 1)
                    nc.vector.scalar_tensor_tensor(out=acc[:, t, :], in0=bank_of(L, 4 + n % 4, D), scalar=cw[:, t, e:e + 1], in1=acc[:, t, :],
                                                   op0=ALU.mult, op1=ALU.add).then_inc(acc_done, 1)

                for n in range(EM):
                    low(n)
                for e in range(1, E):
                    for m in range(EM):
                        low(e * EM + m)
                    for t in range(T):
                        add((e - 1) * T + t)
                for t in range(T):
                    add((E - 1) * T + t)
                for t in range(T):
                    dve.wait_ge(acc_done, E * T + t + 1)
                    tail.stats_of(step, t)
                    if t >= 1:
                        tail.norm(dve, t - 1)
                tail.norm(dve, T - 1)


_INS = ["x", "ctx_1024", "itok_BxS_0_511", "mask_SxS2_fk1",
        "L0_attn_Wq", "L0_attn_Wk", "L0_attn_Wv", "L0_attn_Wo", "L0_attn_bo",
        "L0_xattn_Wq", "L0_xattn_Wkv", "L0_xattn_Wo",
        "L0_ffn_k0", "L0_ffn_k1", "L0_ffn_k2", "L0_ffn_s0", "L0_ffn_s1", "L0_ffn_s2",
        "L1_attn_Wq", "L1_attn_Wk", "L1_attn_Wv", "L1_attn_Wo",
        "L1_attn_q_gamma", "L1_attn_q_beta", "L1_attn_k_gamma", "L1_attn_k_beta",
        "L1_xattn_Wq", "L1_xattn_bq", "L1_xattn_Wk", "L1_xattn_bk", "L1_xattn_Wv", "L1_xattn_bv",
        "L1_xattn_Wo", "L1_xattn_bo",
        "L1_ffn_Wr", "L1_ffn_br", "L1_ffn_W1", "L1_ffn_b1", "L1_ffn_W2", "L1_ffn_b2"]


def kernel(**inputs):
    import numpy as _np
    import concourse.bacc as _bacc
    from concourse import mybir as _mybir
    from concourse.bass_utils import run_bass_kernel_spmd as _run

    nc = _bacc.Bacc("TRN2", target_bir_lowering=False, num_devices=1)
    arrays, aps = {}, {}
    for name in _INS:
        v = _np.ascontiguousarray(inputs[name])
        v = v.view(_np.int32) if v.dtype == _np.bool_ else v
        v = v.reshape(1) if v.ndim == 0 else v
        arrays[f"in_{name}"] = v
        aps[name] = nc.dram_tensor(f"in_{name}", v.shape, _mybir.dt.from_np(v.dtype), kind="ExternalInput").ap()
    out = nc.dram_tensor("out_x", (B, S, D), _mybir.dt.float32, kind="ExternalOutput").ap()
    decoder(nc, aps, out)
    return _run(nc, [arrays], core_ids=[0]).results[0]["out_x"]
```

```python
from contextlib import ExitStack

import numpy as np

import concourse.bass as bass
from concourse import mybir

F32 = mybir.dt.float32
F32R = mybir.dt.float32r
I32 = mybir.dt.int32
U8 = mybir.dt.uint8
ALU = mybir.AluOpType
ACT = mybir.ActivationFunctionType
AX = mybir.AxisListType

P = 128
B, S, D = 4, 512, 256
SC = 1024
T, KD, CT = S // P, D // P, SC // P
H, HD = 16, D // 16
PADW = 32
WIN = 128
NOFF = 4
LH = 64
LD = H * LH
LM = LD // P
F = 1024
FM = F // P
E, ED = 8, 512
EM = ED // P
EPS = 1e-5
NEG = -1.0e9
LOWEST = float(np.finfo(np.float32).min)
FAR = -1.0e30


class Stage:

    def __init__(self, nc, name, outer=None):
        self.nc, self.name, self.ctx, self.sems, self.outer = nc, name, ExitStack(), [], outer

    def __enter__(self):
        return self

    def sem(self, name):
        return self.sem_named(f"{self.name}_{name}")

    def sem_named(self, name):
        if self.outer is not None:
            return self.outer.sem_named(name)
        s = self.ctx.enter_context(self.nc.semaphore(name))
        self.sems.append(s)
        return s

    def sb(self, name, shape, dt=F32):
        return self.ctx.enter_context(self.nc.sbuf_tensor(f"{self.name}_{name}", shape, dt))

    def __exit__(self, *exc):
        if exc[0] is None:
            nums = [s.num for s in self.sems]
            if nums:
                self.nc.all_engine_barrier(sems_to_clear=range(min(nums), max(nums) + 1))
        return self.ctx.__exit__(*exc)


class Chain:

    def __init__(self, eng, sem):
        self.eng, self.sem, self.n = eng, sem, 0

    def __call__(self, ins):
        self.n += 1
        ins.then_inc(self.sem, 1)
        self.eng.wait_ge(self.sem, self.n)


class Buffers:
    pass


def decoder(nc, a, out):
    top = ExitStack()

    def sb(name, shape, dt=F32):
        return top.enter_context(nc.sbuf_tensor(name, shape, dt))

    L = Buffers()
    L.kv_table = nc.dram_tensor("kv_table", [SC, 2 * D], F32).ap()


    L.PS = top.enter_context(nc.psum_tensor("PS", [P, 8 * 512], F32))

    L.ident = sb("ident", [P, P])
    L.ones = sb("ones", [1, P])
    L.eps = sb("eps", [P, 1])
    L.zero = sb("zero", [P, 1])
    L.sel = {n: sb(f"sel_{n}", [P, 4 * P], F32R) for n in ("q_hi", "q_lo", "k_hi", "k_lo")}
    L.window = sb("window", [P, 2 * P])
    L.causal = sb("causal", [P, P])
    L.a0q = sb("a0q", [P, KD, D])
    L.a0k = sb("a0k", [P, KD, D])
    L.a0v = sb("a0v", [P, KD, D])
    L.a0o = sb("a0o", [P, KD, D])
    L.a0bo = sb("a0bo", [P, D])
    L.x0q = sb("x0q", [P, KD, D])
    L.x0kv = sb("x0kv", [P, KD, 2 * D])
    L.x0o = sb("x0o", [P, KD, D])
    L.k0_words, L.k1_words, L.k2_words = (sb(n, [P, r, c // 4], I32) for n, r, c in (("k0", 2 * KD, F), ("k1", FM, F), ("k2", FM, D)))
    L.k0, L.k1, L.k2 = (w[:, :, :].bitcast(U8) for w in (L.k0_words, L.k1_words, L.k2_words))
    L.scales = sb("scales", [P, 4])
    L.a1q = sb("a1q", [P, KD, LD])
    L.a1k = sb("a1k", [P, KD, LD])
    L.a1v = sb("a1v", [P, KD, LD])
    L.a1o = sb("a1o", [P, LM, D])
    L.gains = sb("gains", [P, 4])
    L.k_gains = sb("k_gains", [P, 2, LH])
    L.x1q = sb("x1q", [P, KD, D])
    L.x1k = sb("x1k", [P, KD, D])
    L.x1v = sb("x1v", [P, KD, D])
    L.x1o = sb("x1o", [P, KD, D])
    L.x1bqk = sb("x1bqk", [P, 2, KD])
    L.x1bv = sb("x1bv", [P, D])
    L.x1bo = sb("x1bo", [P, D])
    L.wr = sb("wr", [P, KD, E])
    L.br = sb("br", [1, E])
    L.b1 = sb("b1", [P, E * EM])
    L.b2 = sb("b2", [E, D])
    L.x_tok = sb("x_tok", [P, T, D])
    L.x_T = sb("x_T", [P, KD, S])
    L.ctx_T = sb("ctx_T", [P, KD, SC])
    L.mixed = sb("mixed", [P, T, D])

    setup(nc, a, L)

    with nc.Fori(0, B) as b:
        with Stage(nc, "layer0") as L.layer:
            with Stage(nc, "gat", L.layer) as gs:
                load_batch(nc, a, b, gs, L)
                window_attention(nc, gs, L)
                gather_attention(nc, gs, L)
            sign_ffn(nc, L)
        with Stage(nc, "layer1") as L.layer:
            linear_attention(nc, L)
            cross_attention(nc, a, L)
            experts(nc, a, b, out, L)
    top.close()


def setup(nc, a, L):
    with Stage(nc, "set") as st:
        loaded, memset, piece, sel_done = st.sem("loaded"), st.sem("memset"), st.sem("const"), st.sem("sel_done")
        turned, copied_v, copied_s = st.sem("turned"), st.sem("copied_v"), st.sem("copied_s")
        vec, centred = st.sem("vec"), st.sem("centred")
        raw = {}
        for n, rows in (("L0_xattn_Wq", 2), ("L0_xattn_Wkv", 4), ("L0_xattn_Wo", 2), ("L1_attn_Wq", 8),
                        ("L1_attn_Wk", 8), ("L1_attn_Wv", 8), ("L1_xattn_Wq", 2), ("L1_xattn_Wk", 2),
                        ("L1_xattn_Wv", 2), ("L1_xattn_Wo", 2)):
            raw[n] = st.sb(n, [P, rows, D])
        raw["L1_attn_Wo"] = st.sb("L1_attn_Wo", [P, KD, LD])
        sel = st.sb("sel", [P, 4 * P])
        centre = st.sb("centre", [P, P])
        b1_rows = st.sb("b1_rows", [E * EM, P])

        jobs = []
        for n, dst in (("L1_attn_Wv", L.a1v), ("L1_attn_Wq", L.a1q), ("L1_attn_Wk", L.a1k),
                       ("L0_xattn_Wq", L.x0q), ("L0_xattn_Wkv", L.x0kv), ("L0_xattn_Wo", L.x0o),
                       ("L1_xattn_Wq", L.x1q), ("L1_xattn_Wk", L.x1k), ("L1_xattn_Wv", L.x1v), ("L1_xattn_Wo", L.x1o)):
            for r in range(raw[n].shape[1]):
                pair = [raw[n][:, r, k * P:(k + 1) * P] for k in range(KD)]
                jobs.append((n, pair, dst[:, :, r * P:(r + 1) * P]))
        for r in range(KD):
            for c in range(0, LM, 2):
                pair = [raw["L1_attn_Wo"][:, r, (c + k) * P:(c + k + 1) * P] for k in range(2)]
                jobs.append(("L1_attn_Wo", pair, L.a1o[:, c:c + 2, r * P:(r + 1) * P]))
        order = list(dict.fromkeys(n for n, _, _ in jobs))
        weight_in = {n: st.sem(n) for n in order}

        direct = [
            (L.a0q[:, :, :], a["L0_attn_Wq"].rearrange("(k p) n -> p k n", p=P)),
            (L.a0k[:, :, :], a["L0_attn_Wk"].rearrange("(k p) n -> p k n", p=P)),
            (L.a0v[:, :, :], a["L0_attn_Wv"].rearrange("(k p) n -> p k n", p=P)),
            (L.a0o[:, :, :], a["L0_attn_Wo"].rearrange("(k p) n -> p k n", p=P)),
            (L.a0bo[:, :], a["L0_attn_bo"].rearrange("(a n) -> a n", a=1).to_broadcast((P, D))),
            (L.k0_words[:, :, :], a["L0_ffn_k0"].rearrange("(k p) n -> p k n", p=P)),
            (L.k1_words[:, :, :], a["L0_ffn_k1"].rearrange("(k p) n -> p k n", p=P)),
            (L.k2_words[:, :, :], a["L0_ffn_k2"].rearrange("(k p) n -> p k n", p=P)),
            (L.x1bv[:, :], a["L1_xattn_bv"].rearrange("(a n) -> a n", a=1).to_broadcast((P, D))),
            (L.x1bo[:, :], a["L1_xattn_bo"].rearrange("(a n) -> a n", a=1).to_broadcast((P, D))),
            (L.wr[:, :, :], a["L1_ffn_Wr"].rearrange("(k p) n -> p k n", p=P)),
            (L.br[:, :], a["L1_ffn_br"].rearrange("(a n) -> a n", a=1)),
            (b1_rows[:, :], a["L1_ffn_b1"].rearrange("e (m p) -> (e m) p", p=P)),
            (L.b2[:, :], a["L1_ffn_b2"]),
        ]
        for i in range(3):
            direct.append((L.scales[:, i:i + 1], a[f"L0_ffn_s{i}"].rearrange("(a n) -> a n", a=1).to_broadcast((P, 1))))
        for i, n in enumerate(("q_gamma", "q_beta", "k_gamma", "k_beta")):
            for j in range(2):
                direct.append((L.gains[j * LH:(j + 1) * LH, i:i + 1], a[f"L1_attn_{n}"].rearrange("(n a) -> n a", a=1)))
        for i, n in enumerate(("k_gamma", "k_beta")):
            direct.append((L.k_gains[:, i, :], a[f"L1_attn_{n}"].rearrange("(a n) -> a n", a=1).to_broadcast((P, LH))))
        for i, n in enumerate(("L1_xattn_bq", "L1_xattn_bk")):
            direct.append((L.x1bqk[:, i, :], a[n].rearrange("(k p) -> p k", p=P)))

        small = nc.allow_non_contiguous_dma("biases and gains, a few hundred words each")
        with small, nc.Block("setup") as block:
            @block.sync
            def _(sp):
                for n in order[::2]:
                    sp.dma_start(raw[n][:, :, :], a[n].rearrange("(r p) n -> p r n", p=P)).then_inc(weight_in[n], 16)
                for dst, src in direct[:len(direct) // 2]:
                    sp.dma_start(dst, src).then_inc(loaded, 16)
                sp.wait_ge(loaded, 16 * len(direct))

            @block.gpsimd
            def _(pool):
                nc.gpsimd.memset(L.ident[:, :], 0.0).then_inc(piece, 1)
                nc.gpsimd.memset(L.window[:, :], 0.0).then_inc(piece, 1)
                nc.gpsimd.memset(L.causal[:, :], 1.0).then_inc(piece, 1)
                nc.gpsimd.memset(L.ones[:, :], 1.0).then_inc(piece, 1)
                nc.gpsimd.memset(L.eps[:, :], EPS).then_inc(piece, 1)
                nc.gpsimd.memset(L.zero[:, :], 0.0).then_inc(piece, 1)
                nc.gpsimd.memset(sel[:, :], 0.0).then_inc(piece, 1)
                pool.wait_ge(piece, 7)
                nc.gpsimd.affine_select(out=L.ident[:, :], in_=L.ident[:, :], compare_op=ALU.not_equal, fill=1.0,
                                        base=0, pattern=[[-1, P]], channel_multiplier=1).then_inc(piece, 1)
                nc.gpsimd.affine_select(out=L.window[:, :], in_=L.window[:, :], compare_op=ALU.is_gt, fill=FAR,
                                        base=0, pattern=[[1, 2 * P]], channel_multiplier=-1).then_inc(piece, 1)
                nc.gpsimd.affine_select(out=L.causal[:, :], in_=L.causal[:, :], compare_op=ALU.is_ge, fill=0.0,
                                        base=0, pattern=[[1, P]], channel_multiplier=-1).then_inc(piece, 1)
                pool.wait_ge(piece, 10)
                nc.gpsimd.affine_select(out=L.window[:, :], in_=L.window[:, :], compare_op=ALU.is_ge, fill=FAR,
                                        base=P, pattern=[[-1, 2 * P]], channel_multiplier=1).then_inc(piece, 1)
                nc.gpsimd.affine_select(out=sel[:, :], in_=sel[:, :], compare_op=ALU.not_equal, fill=1.0, base=0,
                                        pattern=[[-2 * HD, 4], [-HD, 2], [0, 4], [-1, HD]], channel_multiplier=1).then_inc(sel_done, 1)
                pool.wait_ge(piece, 11)
                pool.wait_ge(sel_done, 1)

            @block.tensor
            def _(pe):
                pe.wait_ge(piece, 10)
                pe.wait_ge(centred, 4)
                for n, (name, pair, _) in enumerate(jobs):
                    pe.wait_ge(weight_in[name], 16)
                    if n >= 4:
                        pe.wait_ge(copied_v if n % 2 == 0 else copied_s, (n - 4) // 2 + 1)
                    for k, src in enumerate(pair):
                        o = bank_of(L, n % 4)[:, k * P:(k + 1) * P]
                        if name in ("L1_attn_Wq", "L1_attn_Wk"):
                            last = nc.tensor.matmul(o, src, centre[:, :], start=True, stop=True)
                        else:
                            last = nc.tensor.transpose(o, src, L.ident[:, :])
                    last.then_inc(turned, 1)
                pe.wait_ge(loaded, 16 * len(direct))
                nc.tensor.transpose(bank_of(L, 4, E * EM), b1_rows[:, :], L.ident[0:E * EM, 0:E * EM]).then_inc(turned, 1)

            @block.scalar
            def _(act):
                for n in order[1::2]:
                    act.dma_start(raw[n][:, :, :], a[n].rearrange("(r p) n -> p r n", p=P)).then_inc(weight_in[n], 16)
                for dst, src in direct[len(direct) // 2:]:
                    act.dma_start(dst, src).then_inc(loaded, 16)
                for n, (_, _, to) in enumerate(jobs):
                    if n % 2:
                        act.wait_ge(turned, n + 1)
                        src = bank_of(L, n % 4)[:, 0:2 * P].rearrange("p (k n) -> p k n", k=2)
                        nc.scalar.copy(to, src).then_inc(copied_s, 1)

            @block.vector
            def _(dve):
                step = Chain(dve, vec)
                for t in L.sel.values():
                    nc.vector.memset(t[:, :].bitcast(F32), 0.0).then_inc(memset, 1)
                dve.wait_ge(memset, 4)
                dve.wait_ge(sel_done, 1)
                copies = sel[:, :].rearrange("p (n c d) -> p n c d", c=4, d=HD)
                for n, rows in (("q_hi", (0, 1)), ("q_lo", (2, 3)), ("k_hi", (0, 2)), ("k_lo", (1, 3))):
                    for c in rows:
                        step(nc.vector.tensor_copy(L.sel[n][:, :].rearrange("p (n c d) -> p n c d", c=4, d=HD)[:, :, c, :], copies[:, :, c, :]))
                dve.wait_ge(piece, 10)
                for r in range(2):
                    half = slice(r * LH, (r + 1) * LH)
                    other = slice((1 - r) * LH, (2 - r) * LH)
                    nc.vector.tensor_scalar(centre[half, half], L.ident[half, half], -1.0 / LH, None, ALU.add).then_inc(centred, 1)
                    nc.vector.memset(centre[half, other], 0.0).then_inc(centred, 1)
                for n, (_, _, to) in enumerate(jobs):
                    if n % 2 == 0:
                        dve.wait_ge(turned, n + 1)
                        src = bank_of(L, n % 4)[:, 0:2 * P].rearrange("p (k n) -> p k n", k=2)
                        nc.vector.tensor_copy(to, src).then_inc(copied_v, 1)
                dve.wait_ge(loaded, 16 * len(direct))
                step(nc.vector.tensor_scalar(L.a0q[:, :, :], L.a0q[:, :, :], HD ** -0.5, None, ALU.mult))
                step(nc.vector.tensor_scalar(L.scales[:, 0:2], L.scales[:, 0:2], 2.0, None, ALU.mult))
                step(nc.vector.tensor_scalar(L.x1bqk[:, 0, :], L.x1bqk[:, 0, :], HD ** -0.5, None, ALU.mult))
                dve.wait_ge(turned, len(jobs) + 1)
                step(nc.vector.tensor_copy(L.b1[:, :], bank_of(L, 4, E * EM)))
                dve.wait_ge(copied_v, (len(jobs) + 1) // 2)
                dve.wait_ge(copied_s, len(jobs) // 2)
                step(nc.vector.tensor_scalar(L.x1q[:, :, :], L.x1q[:, :, :], HD ** -0.5, None, ALU.mult))


def bank_of(L, i, n=512):
    return L.PS[:, i * 512:i * 512 + n]


def load_batch(nc, a, b, gs, L):
    gs.selected = gs.sb("selected", [P, T, NOFF, 2 * D])
    gs.tok = gs.sb("tok", [P, T], I32)
    gs.rows = gs.sb("rows", [P, NOFF, T], I32)
    gs.keep = gs.sb("keep", [P, T, NOFF])
    gs.lowest = gs.sb("lowest", [P, T, NOFF])
    gs.ctx_in, gs.tok_in = gs.sem("ctx_in"), gs.sem("tok_in")
    gs.context = gs.selected[:, 2, :, :].rearrange("p o n -> p (o n)").rearrange("p (t d) -> p t d", d=D)
    gs.kv = gs.selected[:, 0:2, :, :].rearrange("p t o n -> p (t o) n")
    with Stage(nc, "load", L.layer) as st:
        x_in, turned, cv, cs = (st.sem(n) for n in ("x_in", "turned", "copied_v", "copied_s"))
        with nc.Block("load_batch") as block:
            @block.sync
            def _(sp):
                sp.dma_start(L.x_tok[:, :, :], a["x"][bass.ds(b, 1), :, :].rearrange("a (t p) d -> p (a t) d", p=P)).then_inc(x_in, 16)
                sp.dma_start(gs.context, a["ctx_1024"][bass.ds(b, 1), :, :].rearrange("a (t p) d -> p (a t) d", p=P)).then_inc(gs.ctx_in, 16)
                with nc.allow_non_contiguous_dma("token numbers, 2 KB"):
                    sp.dma_start(gs.tok[:, :], a["itok_BxS_0_511"][bass.ds(b, 1), :].rearrange("a (t p) -> p (a t)", p=P)).then_inc(gs.tok_in, 16)

            @block.tensor
            def _(pe):
                pe.wait_ge(x_in, 16)
                for t in range(T):
                    for k in range(KD):
                        last = nc.tensor.transpose(bank_of(L, t)[:, k * P:(k + 1) * P], L.x_tok[:, t, k * P:(k + 1) * P], L.ident[:, :])
                    last.then_inc(turned, 1)

            def take(copy, eng, t, done):
                eng.wait_ge(turned, t + 1)
                copy(L.x_T[:, :, t * P:(t + 1) * P], bank_of(L, t, 2 * P).rearrange("p (k n) -> p k n", k=KD)).then_inc(done, 1)

            @block.scalar
            def _(act):
                for t in range(1, T, 2):
                    take(nc.scalar.copy, act, t, cs)

            @block.vector
            def _(dve):
                for t in range(0, T, 2):
                    take(nc.vector.tensor_copy, dve, t, cv)


def context_table(nc, gs, L):
    gs.rows_done, gs.written = gs.sem("rows_done"), gs.sem("written")
    gs.gathered = [[gs.sem(f"gathered{t}_{o}") for o in range(NOFF)] for t in range(T)]
    with Stage(nc, "tab", L.layer) as st:
        tokf = st.sb("tokf", [P, T])
        shifted = st.sb("shifted", [P, T, NOFF])
        turned, cT_done, made, kv_done, vec = (st.sem(n) for n in ("turned", "cT_done", "made", "kv_done", "vec"))
        with nc.Block("table") as block:
            @block.sync
            def _(sp):
                for n in range(CT):
                    sp.wait_ge(kv_done, n + 1)
                    sp.dma_start(L.kv_table[n * P:(n + 1) * P, :], gs.kv[:, n, :]).then_inc(gs.written, 16)

            @block.tensor
            def _(pe):
                def turn(n):
                    if n >= 4:
                        pe.wait_ge(cT_done, n - 3)
                    for k in range(KD):
                        last = nc.tensor.transpose(bank_of(L, 4 + n % 4)[:, k * P:(k + 1) * P], gs.context[:, n, k * P:(k + 1) * P], L.ident[:, :])
                    last.then_inc(turned, 1)

                pe.wait_ge(gs.ctx_in, 16)
                turn(0)
                for n in range(CT):
                    if n + 1 < CT:
                        turn(n + 1)
                    pe.wait_ge(cT_done, n + 1)
                    if n >= 4:
                        pe.wait_ge(kv_done, n - 3)
                    for k in range(KD):
                        last = nc.tensor.matmul(bank_of(L, n % 4), L.ctx_T[:, k, n * P:(n + 1) * P], L.x0kv[:, k, :],
                                                start=(k == 0), stop=(k == KD - 1))
                    last.then_inc(made, 1)

            @block.scalar
            def _(act):
                for n in range(CT):
                    act.wait_ge(turned, n + 1)
                    nc.scalar.copy(L.ctx_T[:, :, n * P:(n + 1) * P], bank_of(L, 4 + n % 4, 2 * P).rearrange("p (k n) -> p k n", k=KD)).then_inc(cT_done, 1)

            @block.vector
            def _(dve):
                step = Chain(dve, vec)
                dve.wait_ge(gs.tok_in, 16)
                step(nc.vector.tensor_copy(tokf[:, :], gs.tok[:, :]))
                for o in range(NOFF):
                    step(nc.vector.tensor_scalar(shifted[:, :, o], tokf[:, :], float(-o), None, ALU.add))
                step(nc.vector.tensor_scalar(gs.keep[:, :, :], shifted[:, :, :], 0.0, None, ALU.is_ge))
                step(nc.vector.tensor_scalar(gs.lowest[:, :, :], shifted[:, :, :], 0.0, LOWEST, ALU.is_lt, ALU.mult))
                nc.vector.tensor_scalar(gs.rows[:, :, :].rearrange("p o t -> p t o"), shifted[:, :, :], 0.0, float(SC - 1),
                                        ALU.max, ALU.min).then_inc(gs.rows_done, 1)
                for n in range(CT):
                    dve.wait_ge(made, n + 1)
                    nc.vector.tensor_copy(gs.kv[:, n, :], bank_of(L, n % 4)).then_inc(kv_done, 1)


def project_heads(nc, st, L, name, q, k, v, sync=None, pool=None):
    plain = [(w, "qk"[w], m, c) for w in range(2) for m in range(KD) for c in range((q, k)[w][1].shape[2] // 512)]
    stack = [(w, "qk"[w], m, c) for w in range(2) for m in range(H // 2) for c in range((q, k)[w][1].shape[2] // 512)]
    NP, NS, NV = len(plain), len(stack), v[1].shape[2] // P
    with ExitStack() as tmp:
        parts = [[tmp.enter_context(nc.sbuf_tensor(f"{name}_{n}_{w}", [P, KD, x[1].shape[2]], F32R)) for w in ("hi", "lo")]
                 for n, x in (("q", q), ("k", k))]
        names = ("p_made", "hi_done", "lo_done", "v_made", "v_done", "s_made", "s_v", "s_s")
        p_made, hi_done, lo_done, v_made, v_done, s_made, s_v, s_s = (st.sem(n) for n in names)

        def cols(c):
            return slice(c * 512, (c + 1) * 512)

        def by_head(ap):
            return ap.rearrange("p (h d) -> p h d", d=HD)

        with nc.Block(name) as block:
            if sync is not None:
                block.sync(sync)
            if pool is not None:
                block.gpsimd(pool)

            @block.tensor
            def _(pe):
                for n, (w, _, m, c) in enumerate(plain):
                    if n >= 2:
                        pe.wait_ge(hi_done, n - 1)
                        pe.wait_ge(lo_done, n - 1)
                    weights, x = (q, k)[w][0:2]
                    for kt in range(KD):
                        last = nc.tensor.matmul(bank_of(L, n % 2), weights[:, kt, m * P:(m + 1) * P], x[:, kt, cols(c)], start=(kt == 0), stop=(kt == KD - 1))
                    last.then_inc(p_made, 1)
                for n in range(NV):
                    if n >= 2:
                        pe.wait_ge(v_done, n - 1)
                    o = bank_of(L, 6 + n % 2, D)
                    for kt in range(KD):
                        last = nc.tensor.matmul(o, v[1][:, kt, n * P:(n + 1) * P], v[0][:, kt, :], start=(kt == 0), stop=(kt == KD - 1))
                    last.then_inc(v_made, 1)
                pe.wait_ge(hi_done, NP)
                pe.wait_ge(lo_done, NP)
                for n, (w, what, m, c) in enumerate(stack):
                    if n >= 4:
                        pe.wait_ge(s_s if n % 2 else s_v, (n - 4) // 2 + 1)
                    o = bank_of(L, 2 + n % 4)
                    at = slice((m % 4) * P, (m % 4 + 1) * P)
                    nc.tensor.matmul(o, L.sel[what + "_hi"][:, at], parts[w][0][:, m // 4, cols(c)], start=True, stop=False)
                    nc.tensor.matmul(o, L.sel[what + "_lo"][:, at], parts[w][1][:, m // 4, cols(c)], start=False, stop=True).then_inc(s_made, 1)

            @block.scalar
            def _(act):
                for n, (w, _, m, c) in enumerate(plain):
                    act.wait_ge(p_made, n + 1)
                    nc.scalar.activation(parts[w][0][:, m, cols(c)], bank_of(L, n % 2), ACT.Identity, bias=(q, k)[w][2](m)).then_inc(hi_done, 1)
                for n in range(NV if v[2] is None else 0):
                    act.wait_ge(v_made, n + 1)
                    nc.scalar.copy(v[3][:, n, :, 0:HD], by_head(bank_of(L, 6 + n % 2, D))).then_inc(v_done, 1)
                for n, (w, _, m, c) in enumerate(stack):
                    if n % 2:
                        act.wait_ge(s_made, n + 1)
                        nc.scalar.copy((q, k)[w][3][:, m, cols(c)], bank_of(L, 2 + n % 4)).then_inc(s_s, 1)

            @block.vector
            def _(dve):
                for n, (w, _, m, c) in enumerate(plain):
                    dve.wait_ge(hi_done, n + 1)
                    nc.vector.scalar_tensor_tensor(out=parts[w][1][:, m, cols(c)], in0=bank_of(L, n % 2), scalar=(q, k)[w][2](m),
                                                   in1=parts[w][0][:, m, cols(c)].bitcast(F32), op0=ALU.add, op1=ALU.subtract).then_inc(lo_done, 1)
                for n in range(NV if v[2] is not None else 0):
                    dve.wait_ge(v_made, n + 1)
                    nc.vector.tensor_tensor(v[3][:, n, :, 0:HD], by_head(bank_of(L, 6 + n % 2, D)), by_head(v[2][:, :]), ALU.add).then_inc(v_done, 1)
                for n, (w, _, m, c) in enumerate(stack):
                    if n % 2 == 0:
                        dve.wait_ge(s_made, n + 1)
                        nc.vector.tensor_copy((q, k)[w][3][:, m, cols(c)], bank_of(L, 2 + n % 4)).then_inc(s_v, 1)


def attend(nc, st, L, name, qS, kS, v, sc, per_unit, keys, mask, slots, sync=None, pool=None, before=None, between=None):
    units = [(t, range(h, h + per_unit)) for t in range(T) for h in range(0, H, per_unit)]
    NU, UG = len(units), 4 // per_unit
    PARTS = 4 if UG > 1 else 1
    END = NU + 4 + PARTS
    W = SC // per_unit
    pT = st.sb("pT", [P, slots, CT, P])
    oT = st.sb("oT", [P, 2, P])
    mx, nmx, rden = (st.sb(n, [P, T, H]) for n in ("mx", "nmx", "rden"))
    names = ("cleared", "scored", "masked", "bias", "exped", "turned", "pT_v", "pT_s", "summed", "oT_done", "back", "normed", "vec")
    cleared, scored, masked, bias, exped, turned, pT_v, pT_s, summed, oT_done, back, normed, vec = (st.sem(n) for n in names)

    def width(t):
        return keys(t)[1] * P

    def column(i):
        return (i % 2 * (per_unit // 2) + i // 2) * W

    def blocks(t):
        every = [(i, c) for i in range(per_unit) for c in range(keys(t)[1])]
        return every[:len(every) // 2], every[len(every) // 2:]

    def copy_turned(copy, eng, n, done):
        u, half = n // 2, n % 2
        nb = len(blocks(units[u][0])[half])
        eng.wait_ge(turned, n + 1)
        if u >= slots:
            eng.wait_ge(summed, (u - slots) // UG + 1)
        copy(pT[:, u % slots, half * nb:(half + 1) * nb, :], bank_of(L, 4 + half, nb * P).rearrange("p (c n) -> p c n", n=P)).then_inc(done, 1)

    def groups_with_last(u):
        return [u // UG] if 0 <= u < NU and u % UG == UG - 1 else []

    def negate(eng, u):
        t, hs = units[u]
        eng.wait_ge(masked, per_unit * (u + 1))
        eng.tensor_scalar(nmx[:, t, hs[0]:hs[0] + per_unit], mx[:, t, hs[0]:hs[0] + per_unit], -1.0, None, ALU.mult).then_inc(bias, 1)

    with nc.Block(name) as block:
        if sync is not None:
            block.sync(lambda sp: sync(sp, masked))
        if pool is not None:
            block.gpsimd(pool)
        else:
            @block.gpsimd
            def _(pool):
                for u in range(NU):
                    negate(nc.gpsimd, u)
                    if between is not None:
                        between(pool, u)

        @block.tensor
        def _(pe):
            def scores(u):
                t, hs = units[u]
                if u >= 2:
                    pe.wait_ge(masked, per_unit * (u - 1))
                for i, h in enumerate(hs):
                    rows = slice((h % 2) * 64, (h % 2) * 64 + 64)
                    for c in range(0, width(t), 512):
                        n = min(512, width(t) - c)
                        at = 2 * (u % 2) * 512 + column(i) + c
                        k0 = keys(t)[0] * P + c
                        last = nc.tensor.matmul(L.PS[:, at:at + n], qS[rows, h // 2, t * P:(t + 1) * P], kS[rows, h // 2, k0:k0 + n], start=True, stop=True)
                last.then_inc(scored, 1)

            def turn(u, half):
                if half == 0:
                    pe.wait_ge(exped, per_unit * (u + 1))
                if u >= 1:
                    pe.wait_ge(pT_s if half else pT_v, u)
                for n, (i, c) in enumerate(blocks(units[u][0])[half]):
                    at = column(i) + c * P
                    last = nc.tensor.transpose(bank_of(L, 4 + half)[:, n * P:(n + 1) * P], sc[u % 4][:, at:at + P], L.ident[:, :])
                last.then_inc(turned, 1)

            def mix(g, part):
                last_u = (g + 1) * UG - 1
                if part == 0:
                    pe.wait_ge(pT_v, last_u + 1)
                    pe.wait_ge(pT_s, last_u + 1)
                    pe.wait_ge(cleared, 3)
                    if g >= 2:
                        pe.wait_ge(normed, g - 1)
                t = units[last_u][0]
                first, nk = keys(t)
                for c in range(part * nk // PARTS, (part + 1) * nk // PARTS):
                    for j in range(4):
                        h = 4 * (g % (H // 4)) + j
                        slot = (g * UG + j // per_unit) % slots
                        last = nc.tensor.matmul(bank_of(L, 6 + g % 2)[j * PADW:j * PADW + HD + 1, 0:P], v[:, first + c, h, :],
                                                pT[:, slot, (j % per_unit) * nk + c, :], start=(c == 0), stop=(c == nk - 1))
                if part == PARTS - 1:
                    last.then_inc(summed, 1)

            def turn_back(g):
                pe.wait_ge(oT_done, g + 1)
                nc.tensor.transpose(bank_of(L, 6 + g % 2)[:, P:2 * P], oT[:, g % 2, :], L.ident[:, :]).then_inc(back, 1)

            scores(0)
            for n in range(END):
                if 2 <= n < NU + 2:
                    turn(n - 2, 0)
                if n + 1 < NU:
                    scores(n + 1)
                for g in groups_with_last(n - 3 - PARTS):
                    turn_back(g)
                for part in range(PARTS):
                    for g in groups_with_last(n - 3 - part):
                        mix(g, part)
                if 2 <= n < NU + 2:
                    turn(n - 2, 1)

        @block.scalar
        def _(act):
            for n in range(END):
                for g in groups_with_last(n - 3 - PARTS):
                    act.wait_ge(summed, g + 1)
                    nc.scalar.copy(oT[:, g % 2, :], bank_of(L, 6 + g % 2, P)).then_inc(oT_done, 1)
                if n < NU:
                    t, hs = units[n]
                    act.wait_ge(bias, n + 1)
                    for i, h in enumerate(hs):
                        part = sc[n % 4][:, column(i):column(i) + width(t)]
                        nc.scalar.activation(part, part, ACT.Exp, bias=nmx[:, t, h:h + 1]).then_inc(exped, 1)
                if 2 <= n < NU + 2:
                    copy_turned(nc.scalar.copy, act, 2 * (n - 2) + 1, pT_s)

        @block.vector
        def _(dve):
            step = Chain(dve, vec)
            for i in range(2):
                nc.vector.memset(bank_of(L, 6 + i, P), 0.0).then_inc(cleared, 1)
            nc.vector.memset(v[:, :, :, HD:HD + 1], 1.0).then_inc(cleared, 1)

            def normalise(g):
                t, h = g // (H // 4), 4 * (g % (H // 4))
                dve.wait_ge(back, g + 1)
                out = bank_of(L, 6 + g % 2)[:, P:2 * P].rearrange("p (j d) -> p j d", d=PADW)
                step(nc.vector.reciprocal(rden[:, t, h:h + 4].rearrange("p (j a) -> p j a", a=1), out[:, :, HD:HD + 1]))
                nc.vector.tensor_tensor(
                    L.mixed[:, t, h * HD:(h + 4) * HD].rearrange("p (j d) -> p j d", d=HD),
                    out[:, :, 0:HD],
                    rden[:, t, h:h + 4].rearrange("p (j a) -> p j a", a=1).to_broadcast((P, 4, HD)), ALU.mult).then_inc(normed, 1)

            for n in range(END):
                for g in groups_with_last(n - 4 - PARTS):
                    normalise(g)
                if n < NU:
                    t, hs = units[n]
                    if before is not None:
                        before(dve, t, hs)
                    dve.wait_ge(scored, n + 1)
                    if n >= 4:
                        dve.wait_ge(turned, 2 * (n - 3))
                    for i, h in enumerate(hs):
                        at = 2 * (n % 2) * 512 + column(i)
                        nc.vector.tensor_tensor_reduce(out=sc[n % 4][:, column(i):column(i) + width(t)], in0=L.PS[:, at:at + width(t)], in1=mask(t),
                                                       scale=1.0, scalar=LOWEST, op0=ALU.add, op1=ALU.max, accum_out=mx[:, t, h:h + 1]).then_inc(masked, 1)
                    if pool is not None:
                        negate(nc.vector, n)
                if 2 <= n < NU + 2:
                    copy_turned(nc.vector.tensor_copy, dve, 2 * (n - 2), pT_v)


def window_attention(nc, gs, L):
    with Stage(nc, "win", L.layer) as st:
        qS, kS = st.sb("qS", [P, H // 2, S], F32R), st.sb("kS", [P, H // 2, S], F32R)
        v = st.sb("v", [P, T, H, HD + 1])

        def gather(pool):
            pool.wait_ge(gs.rows_done, 1)
            pool.wait_ge(gs.written, 16 * CT)
            for t in range(T):
                for o in range(NOFF):
                    nc.gpsimd.indirect_dma_start(
                        out=gs.selected[:, t, o, :], out_offset=None, in_=L.kv_table,
                        in_offset=bass.IndirectOffsetOnAxis(ap=gs.rows[:, o, t:t + 1], axis=0)).then_inc(gs.gathered[t][o], 16)

        def keys(t):
            return max(t - 1, 0), min(t, 1) + 1

        def no_bias(m):
            return L.zero[:, :]

        project_heads(nc, st, L, "win_project", (L.a0q, L.x_T, no_bias, qS), (L.a0k, L.x_T, no_bias, kS), (L.a0v, L.x_T, None, v))
        context_table(nc, gs, L)
        sc = st.sb("sc", [P, 4, SC])
        attend(nc, st, L, "window", qS, kS, v, [sc[:, i, :] for i in range(4)], 4, keys, lambda t: L.window[:, 2 * P - P * keys(t)[1]:2 * P], 3, pool=gather)


def project_norm(nc, name, L, weight, bias, sync=None, scalar=None, pool=None):
    with Stage(nc, name, L.layer) as st:
        proj = Projection(nc, st, L, weight, bias)
        with nc.Block(name) as block:
            if sync is not None:
                block.sync(sync)
            @block.gpsimd
            def _(engine):
                proj.on_gpsimd(engine)
                if pool is not None:
                    pool(engine)

            block.tensor(proj.on_tensor)

            @block.scalar
            def _(engine):
                proj.on_scalar(engine, after=scalar)

            block.vector(proj.on_vector)


class Projection:

    def __init__(self, nc, st, L, weight, bias):
        self.nc, self.L, self.weight, self.bias = nc, L, weight, bias
        self.mT = st.sb("mT", [P, T, KD, P])
        self.res = st.sb("res", [P, T, D])
        self.turned, self.mT_done, self.made, self.biased = (st.sem(n) for n in ("turned", "mT_done", "made", "biased"))
        self.tail = NormTail(nc, st, L, self.res, turned_banks=(6, 7))

    def on_tensor(self, pe, after=None):
        nc, L = self.nc, self.L
        for t in range(T):
            for k in range(KD):
                last = nc.tensor.transpose(bank_of(L, t)[:, k * P:(k + 1) * P], L.mixed[:, t, k * P:(k + 1) * P], L.ident[:, :])
            last.then_inc(self.turned, 1)
        for t in range(T):
            pe.wait_ge(self.mT_done, t + 1)
            o = bank_of(L, 4 + t % 2, D)
            if t >= 2:
                pe.wait_ge(self.tail.added, t - 1)
            for k in range(KD):
                last = nc.tensor.matmul(o, self.mT[:, t, k, :], self.weight[:, k, :], start=(k == 0), stop=(k == KD - 1))
            last.then_inc(self.made, 1)
        self.tail.turn(pe, after)

    def on_scalar(self, act, after=None):
        for t in range(T):
            act.wait_ge(self.turned, t + 1)
            self.nc.scalar.copy(self.mT[:, t, :, :], bank_of(self.L, t, KD * P).rearrange("p (k n) -> p k n", k=KD)).then_inc(self.mT_done, 1)
        self.tail.finish(act, after=after)

    def on_gpsimd(self, pool):
        for t in range(T):
            x = self.L.x_tok[:, t, :]
            self.nc.gpsimd.tensor_tensor(x, x, self.bias[:, :], ALU.add).then_inc(self.biased, 1)

    def on_vector(self, dve):
        step = Chain(dve, self.tail.vec)
        for t in range(T):
            dve.wait_ge(self.made, t + 1)
            dve.wait_ge(self.biased, t + 1)
            self.nc.vector.tensor_tensor(self.res[:, t, :], bank_of(self.L, 4 + t % 2, D), self.L.x_tok[:, t, :], ALU.add).then_inc(self.tail.added, 1)
            dve.wait_ge(self.tail.added, t + 1)
            self.tail.stats_of(step, t)
            if t >= 1:
                self.tail.norm(dve, t - 1)
        self.tail.norm(dve, T - 1)


class NormTail:

    def __init__(self, nc, st, L, res, turned_banks, turn_x=True):
        self.nc, self.L, self.res, self.banks = nc, L, res, turned_banks
        self.stats, self.mv = st.sb("stats", [P, T, 6]), st.sb("mv", [P, T, 2])
        self.std, self.rstd = st.sb("std", [P, T]), st.sb("rstd", [P, T])
        self.added, self.var_done, self.std_done, self.rstd_done, self.new_x, self.x_turned, self.xT_done, self.vec = (
            st.sem(n) for n in ("added", "var_done", "std_done", "rstd_done", "new_x", "x_turned", "xT_done", "vec"))

    def stats_of(self, step, t):
        step(self.nc.vector.bn_stats(self.stats[:, t, :], self.res[:, t, :]))
        self.nc.vector.bn_aggr(self.mv[:, t, :], self.stats[:, t, :]).then_inc(self.var_done, 1)

    def norm(self, dve, t):
        dve.wait_ge(self.std_done, t + 1)
        self.nc.vector.reciprocal(self.rstd[:, t:t + 1], self.std[:, t:t + 1]).then_inc(self.rstd_done, 1)
        dve.wait_ge(self.rstd_done, t + 1)
        self.nc.vector.tensor_scalar(self.L.x_tok[:, t, :], self.res[:, t, :], self.mv[:, t, 0:1], self.rstd[:, t:t + 1],
                                     ALU.subtract, ALU.mult).then_inc(self.new_x, 1)

    def turn_tile(self, pe, t, bank):
        pe.wait_ge(self.new_x, t + 1)
        for k in range(KD):
            last = self.nc.tensor.transpose(bank_of(self.L, bank)[:, k * P:(k + 1) * P],
                                            self.L.x_tok[:, t, k * P:(k + 1) * P], self.L.ident[:, :])
        last.then_inc(self.x_turned, 1)

    def root(self, act, t):
        act.wait_ge(self.var_done, t + 1)
        self.nc.scalar.activation(self.std[:, t:t + 1], self.mv[:, t, 1:2], ACT.Sqrt, bias=self.L.eps[:, :]).then_inc(self.std_done, 1)

    def copy_turned(self, act, t, bank):
        act.wait_ge(self.x_turned, t + 1)
        self.nc.scalar.copy(self.L.x_T[:, :, t * P:(t + 1) * P],
                            bank_of(self.L, bank, KD * P).rearrange("p (k n) -> p k n", k=KD)).then_inc(self.xT_done, 1)

    def turn(self, pe, after=None):
        for t in range(T):
            if t >= 2:
                pe.wait_ge(self.xT_done, t - 1)
            self.turn_tile(pe, t, self.banks[t % 2])
            if after is not None and t >= 1:
                after(t - 1)
        if after is not None:
            after(T - 1)

    def finish(self, act, turned=True, after=None):
        for t in range(T):
            self.root(act, t)
            if turned and t >= 1:
                self.copy_turned(act, t - 1, self.banks[(t - 1) % 2])
                if after is not None and t >= 2:
                    after(t - 2)
        if turned:
            self.copy_turned(act, T - 1, self.banks[(T - 1) % 2])
        if after is not None:
            for t in range(T - 2, T):
                after(t)


def gather_attention(nc, gs, L):
    with Stage(nc, "a0p", L.layer) as before, Stage(nc, "gatt", L.layer) as st:
        proj = Projection(nc, before, L, L.a0o, L.a0bo)
        q = st.sb("q", [P, T, D])
        pk, pv = st.sb("pk", [P, 2, NOFF, D]), st.sb("pv", [P, 2, NOFF, D])
        s, e = (st.sb(n, [P, T, NOFF, H]) for n in ("s", "e"))
        m, den, rden = (st.sb(n, [P, T, H]) for n in ("m", "den", "rden"))
        mT = st.sb("mT", [P, T, KD, P])
        res = st.sb("res", [P, T, D])
        made, q_done, centred, exped, shares, weighted, mixed_in, mT_done, summed = (
            st.sem(n) for n in ("made", "q_done", "centred", "exped", "shares", "weighted", "mixed_in", "mT_done", "summed"))
        tail = NormTail(nc, st, L, res, turned_banks=None)

        def heads(ap):
            return ap.rearrange("p o (h d) -> p (o h) d", d=HD)

        with nc.Block("gather_attention") as block:
            @block.tensor
            def _(pe):
                def query(t):
                    pe.wait_ge(proj.tail.xT_done, t + 1)
                    for k in range(KD):
                        last = nc.tensor.matmul(bank_of(L, t, D), L.x_T[:, k, t * P:(t + 1) * P], L.x0q[:, k, :],
                                                start=(k == 0), stop=(k == KD - 1))
                    last.then_inc(made, 1)

                proj.on_tensor(pe, after=query)

                def mix(t):
                    pe.wait_ge(weighted, t + 1)
                    if t >= 2:
                        pe.wait_ge(mT_done, t - 1)
                    for k in range(KD):
                        for o in range(NOFF):
                            last = nc.tensor.matmul(bank_of(L, 4 + t % 2)[:, k * P:(k + 1) * P], pv[:, t % 2, o, k * P:(k + 1) * P], L.ident[:, :],
                                                    start=(o == 0), stop=(o == NOFF - 1))
                    last.then_inc(mixed_in, 1)

                def output(t):
                    pe.wait_ge(mT_done, t + 1)
                    if t >= 2:
                        pe.wait_ge(tail.added, t - 1)
                    for k in range(KD):
                        last = nc.tensor.matmul(bank_of(L, 6 + t % 2, D), mT[:, t, k, :], L.x0o[:, k, :], start=(k == 0), stop=(k == KD - 1))
                    last.then_inc(summed, 1)

                for t in range(T):
                    mix(t)
                    output(t)
                for t in range(T):
                    tail.turn_tile(pe, t, t)

            @block.scalar
            def _(act):
                def take_query(t):
                    act.wait_ge(made, t + 1)
                    nc.scalar.mul(q[:, t, :], bank_of(L, t, D), HD ** -0.5).then_inc(q_done, 1)

                proj.on_scalar(act, after=take_query)
                for n in range(T + 1):
                    if n < T:
                        act.wait_ge(centred, n + 1)
                        nc.scalar.activation(e[:, n, :, :], s[:, n, :, :], ACT.Exp).then_inc(exped, 1)
                    if n >= 1:
                        act.wait_ge(mixed_in, n)
                        nc.scalar.copy(mT[:, n - 1, :, :], bank_of(L, 4 + (n - 1) % 2, KD * P).rearrange("p (k n) -> p k n", k=KD)).then_inc(mT_done, 1)
                for n in range(T + 1):
                    if n < T:
                        tail.root(act, n)
                    if n >= 1:
                        tail.copy_turned(act, n - 1, n - 1)

            @block.gpsimd
            def _(pool):
                proj.on_gpsimd(pool)
                for t in range(T):
                    for o in range(NOFF):
                        pool.wait_ge(gs.gathered[t][o], 16)
                nc.gpsimd.dma_reset()
                for t in range(T):
                    pool.wait_ge(shares, t + 1)
                    if t >= 2:
                        pool.wait_ge(mixed_in, t - 1)
                    nc.gpsimd.tensor_tensor(
                        pv[:, t % 2, :, :].rearrange("p o (h d) -> p o h d", d=HD), gs.selected[:, t, :, D:2 * D].rearrange("p o (h d) -> p o h d", d=HD),
                        e[:, t, :, :].rearrange("p o (h a) -> p o h a", a=1).to_broadcast((P, NOFF, H, HD)), ALU.mult).then_inc(weighted, 1)

            @block.vector
            def _(dve):
                proj.on_vector(dve)
                step = Chain(dve, tail.vec)

                def over_rows(ap):
                    return ap.rearrange("p (a h) -> p a h", a=1).to_broadcast((P, NOFF, H))

                def share(t):
                    dve.wait_ge(exped, t + 1)
                    step(nc.vector.tensor_reduce(den[:, t, :], e[:, t, :, :].rearrange("p o h -> p h o"), AX.X, ALU.add))
                    step(nc.vector.reciprocal(rden[:, t, :], den[:, t, :]))
                    nc.vector.tensor_tensor(e[:, t, :, :], e[:, t, :, :], over_rows(rden[:, t, :]), ALU.mult).then_inc(shares, 1)

                for n in range(T + 2):
                    if n < T:
                        dve.wait_ge(q_done, n + 1)
                        for o in range(NOFF):
                            dve.wait_ge(gs.gathered[n][o], 16)
                        step(nc.vector.tensor_tensor(pk[:, n % 2, :, :], gs.selected[:, n, :, 0:D],
                                                     q[:, n, :].rearrange("p (a n) -> p a n", a=1).to_broadcast((P, NOFF, D)), ALU.mult))
                    if 1 <= n <= T:
                        share(n - 1)
                    if n < T:
                        step(nc.vector.tensor_reduce(s[:, n, :, :], heads(pk[:, n % 2, :, :]), AX.X, ALU.add))
                        for mask, op in ((gs.keep, ALU.mult), (gs.lowest, ALU.add)):
                            step(nc.vector.tensor_tensor(s[:, n, :, :], s[:, n, :, :],
                                                         mask[:, n, :].rearrange("p (o a) -> p o a", a=1).to_broadcast((P, NOFF, H)), op))
                        step(nc.vector.tensor_reduce(m[:, n, :], s[:, n, :, :].rearrange("p o h -> p h o"), AX.X, ALU.max))
                        nc.vector.tensor_tensor(s[:, n, :, :], s[:, n, :, :], over_rows(m[:, n, :]), ALU.subtract).then_inc(centred, 1)
                    if 2 <= n <= T + 1:
                        t = n - 2
                        dve.wait_ge(summed, t + 1)
                        nc.vector.tensor_tensor(res[:, t, :], bank_of(L, 6 + t % 2, D), L.x_tok[:, t, :], ALU.add).then_inc(tail.added, 1)
                        dve.wait_ge(tail.added, t + 1)
                        tail.stats_of(step, t)
                    if n >= T:
                        for t in range(2 * (n - T), 2 * (n - T) + 2):
                            tail.norm(dve, t)


def sign_ffn(nc, L):
    NR = 3
    with Stage(nc, "ffn", L.layer) as st:
        def pair(name, shape):
            return [st.sb(f"{name}_{w}", shape, F32R) for w in ("hi", "lo")]
        h1, h2 = pair("h1", [P, FM, S]), pair("h2", [P, FM, S])
        x2 = [h[:, 0:KD, :] for h in h2]
        w0 = st.sb("w0", [P, KD, F], F32R)
        w1 = st.sb("w1", [P, NR, FM, P], F32R)
        w2 = st.sb("w2", [P, FM, D], F32R)
        full = st.sb("full", [P, 4, S])
        w0_half = L.mixed[:, 0:2, :].rearrange("p m (k n) -> p m k n", k=KD)
        res = L.mixed
        names = ("w0_done", "w1_done", "w2_done", "x_hi", "x_lo", "made", "relued", "hi_done", "lo_done", "summed")
        w0_done, w1_done, w2_done, x_hi, x_lo, made, relued, hi_done, lo_done, summed = (st.sem(n) for n in names)
        tail = NormTail(nc, st, L, res, turned_banks=(6, 7))
        NT = 2 * FM

        with nc.Block("sign_ffn") as block:
            @block.gpsimd
            def _(pool):
                for n in range(FM):
                    if n >= NR:
                        pool.wait_ge(made, FM + n - NR + 1)
                    nc.gpsimd.tensor_scalar(w1[:, n % NR, :, :], L.k1[:, :, n * P:(n + 1) * P], 2.0, -1.0, ALU.mult, ALU.add).then_inc(w1_done, 1)
                for k in range(FM):
                    nc.gpsimd.tensor_scalar(w2[:, k, :], L.k2[:, k, :], 2.0, -1.0, ALU.mult, ALU.add).then_inc(w2_done, 1)

            @block.tensor
            def _(pe):
                pe.wait_ge(x_lo, 1)
                for n in range(NT):
                    layer, m = n // FM, n % FM
                    if n >= 4:
                        pe.wait_ge(relued, n - 3)
                    if layer == 0:
                        pe.wait_ge(w0_done, m + 1)
                    else:
                        pe.wait_ge(w1_done, m + 1)
                    ks = KD if layer == 0 else FM
                    for k in range(ks):
                        if layer == 1 and m == 0:
                            pe.wait_ge(lo_done, k + 1)
                        for part in range(2):
                            w = w0[:, k, m * P:(m + 1) * P] if layer == 0 else w1[:, m % NR, k, :]
                            x = (x2 if layer == 0 else h1)[part][:, k, :]
                            last = nc.tensor.matmul(bank_of(L, n % 4), w, x, start=(k == 0 and part == 0), stop=(k == ks - 1 and part == 1))
                    last.then_inc(made, 1)
                for t in range(T):
                    if t >= 2:
                        pe.wait_ge(tail.added, t - 1)
                    for k in range(FM):
                        if t == 0:
                            pe.wait_ge(lo_done, FM + k + 1)
                            pe.wait_ge(w2_done, k + 1)
                        for part in range(2):
                            last = nc.tensor.matmul(bank_of(L, 4 + t % 2, D), h2[part][:, k, t * P:(t + 1) * P], w2[:, k, :],
                                                    start=(k == 0 and part == 0), stop=(k == FM - 1 and part == 1))
                    last.then_inc(summed, 1)
                tail.turn(pe)

            @block.scalar
            def _(act):
                nc.scalar.copy(x2[0][:, :, :], L.x_T[:, :, :]).then_inc(x_hi, 1)
                for n in range(NT):
                    act.wait_ge(made, n + 1)
                    if n >= 4:
                        act.wait_ge(lo_done, n - 3)
                    layer = n // FM
                    nc.scalar.activation(full[:, n % 4, :], bank_of(L, n % 4), ACT.Relu,
                                         scale=L.scales[:, layer:layer + 1]).then_inc(relued, 1)
                    act.wait_ge(relued, n + 1)
                    nc.scalar.copy((h1 if n < FM else h2)[0][:, n % FM, :], full[:, n % 4, :]).then_inc(hi_done, 1)
                tail.finish(act)

            @block.vector
            def _(dve):
                step = Chain(dve, tail.vec)
                dve.wait_ge(x_hi, 1)
                nc.vector.tensor_tensor(x2[1][:, :, :], L.x_T[:, :, :], x2[0][:, :, :].bitcast(F32), ALU.subtract).then_inc(x_lo, 1)
                for m in range(FM):
                    w = w0[:, :, m * P:(m + 1) * P]
                    cols = slice(m * P, (m + 1) * P)
                    tmp = w0_half[:, m % 2, :, :]
                    if m >= 2:
                        dve.wait_ge(w0_done, m - 1)
                    step(nc.vector.tensor_tensor(tmp, L.k0[:, 0:KD, cols], L.k0[:, KD:2 * KD, cols], ALU.subtract))
                    nc.vector.tensor_scalar(w, tmp, 2.0, None, ALU.mult).then_inc(w0_done, 1)
                for n in range(NT):
                    dve.wait_ge(hi_done, n + 1)
                    h = h1 if n < FM else h2
                    nc.vector.tensor_tensor(h[1][:, n % FM, :], full[:, n % 4, :], h[0][:, n % FM, :].bitcast(F32), ALU.subtract).then_inc(lo_done, 1)
                for t in range(T):
                    dve.wait_ge(summed, t + 1)
                    nc.vector.scalar_tensor_tensor(out=res[:, t, :], in0=bank_of(L, 4 + t % 2, D), scalar=L.scales[:, 2:3],
                                                   in1=L.x_tok[:, t, :], op0=ALU.mult, op1=ALU.add).then_inc(tail.added, 1)
                    dve.wait_ge(tail.added, t + 1)
                    tail.stats_of(step, t)
                    if t >= 1:
                        tail.norm(dve, t - 1)
                tail.norm(dve, T - 1)


def linear_attention(nc, L):
    HM = LM // 2
    HW = LD // 2
    with Stage(nc, "lin", L.layer) as st:
        tok = st.sb("tok", [P, 2, 2, LD])
        kg = st.sb("kg", [P, 2, LD])
        v = st.sb("v", [P, 2, LD])
        qkT = st.sb("qkT", [P, 2, LM, P])
        aT = st.sb("aT", [P, 2, 2, HM, P])
        oT = st.sb("oT", [P, LM, P])
        state = st.sb("state", [P, LM, P])
        sq = st.sb("sq", [P, 2, HW])
        ssum, std, rstd = (st.sb(n, [P, 4 * T, HW // LH]) for n in ("ssum", "root", "rroot"))
        res = L.mixed
        names = ("made", "squared", "sum_done", "rooted", "normed", "v_done", "kg_half", "kg_done", "turned", "T_s", "T_v",
                 "scored", "masked", "mixed_in", "oT_done", "cleared", "stated", "state_done", "summed")
        (made, squared, sum_done, rooted, normed, v_done, kg_half, kg_done, turned, T_s, T_v,
         scored, masked, mixed_in, oT_done, cleared, stated, state_done, summed) = (st.sem(n) for n in names)
        tail = NormTail(nc, st, L, res, turned_banks=None)

        def heads(ap):
            return ap.rearrange("p (h d) -> p h d", d=LH)

        def projected(t, what, half):
            return bank_of(L, half + (2 + 2 * what if t == 0 and what >= 1 else 0))

        with nc.Block("linear") as block:
            @block.tensor
            def _(pe):
                def project(t, what, halves=(0, 1)):
                    w = (L.a1q, L.a1k, L.a1v)[what]
                    for half in halves:
                        if what == 0 and t == 1:
                            pe.wait_ge(normed, half + 1)
                        if what == 0 and t >= 2:
                            pe.wait_ge(v_done, 2 * t - 1 + half)
                        if what >= 1 and t >= 1:
                            pe.wait_ge(normed, 4 * t + 2 * what - 1 + half)
                        for k in range(KD):
                            last = nc.tensor.matmul(projected(t, what, half), L.x_T[:, k, t * P:(t + 1) * P], w[:, k, half * HW:(half + 1) * HW],
                                                    start=(k == 0), stop=(k == KD - 1))
                        last.then_inc(made, 1)

                def turn(t, what):
                    for half in range(2):
                        if what == 1:
                            pe.wait_ge(T_v if half else T_s, 2 * t + 1)
                        elif half == 0 and t >= 1:
                            pe.wait_ge(state_done, 4 * (t - 1) + 2)
                        elif half == 1 and t == 1:
                            pe.wait_ge(state_done, 4)
                        elif half == 1 and t >= 2:
                            pe.wait_ge(tail.xT_done, t - 1)
                        pe.wait_ge(normed, 4 * t + 2 * what + half + 1)
                        for i in range(HM):
                            m = half * HM + i
                            last = nc.tensor.transpose(bank_of(L, 2 + half)[:, i * P:(i + 1) * P], tok[:, t % 2, what, m * P:(m + 1) * P], L.ident[:, :])
                        last.then_inc(turned, 1)

                def scores(t):
                    for half in range(2):
                        pe.wait_ge(T_v if half else T_s, 2 * t + 2)
                        for j in range(2):
                            n = 4 * t + 2 * half + j
                            if n >= 2:
                                pe.wait_ge(masked, n - 1)
                            if t >= 1 and half == 0 and j == 0:
                                pe.wait_ge(tail.added, t)
                            rows = slice(j * LH, (j + 1) * LH)
                            for i in range(HM):
                                m = half * HM + i
                                last = nc.tensor.matmul(bank_of(L, 4 + j)[:, i * P:(i + 1) * P], qkT[rows, 1, m, :], qkT[rows, 0, m, :], start=True, stop=True)
                            last.then_inc(scored, 1)

                def mix(t):
                    for half in range(2):
                        pe.wait_ge(v_done, 2 * t + half + 1)
                        pe.wait_ge(masked, 4 * t + 2 * half + 2)
                        if t >= 1:
                            pe.wait_ge(state_done, 4 * (t - 1) + 2 * half + 2)
                            pe.wait_ge(oT_done, 2 * (t - 1) + half + 1)
                        for i in range(HM):
                            m = half * HM + i
                            o = bank_of(L, 6 + half)[:, i * P:(i + 1) * P]
                            if t >= 1:
                                nc.tensor.matmul(o, state[:, m, :], qkT[:, 0, m, :], start=True, stop=False)
                            for j in range(2):
                                h = 2 * m + j
                                last = nc.tensor.matmul(o[j * LH:(j + 1) * LH, :], v[:, t % 2, h * LH:(h + 1) * LH], aT[:, half, j, i, :],
                                                        start=(t == 0), stop=True)
                        last.then_inc(mixed_in, 1)

                def update(t):
                    for half in range(2):
                        pe.wait_ge(kg_done, 2 * t + half + 1)
                        pe.wait_ge(T_v if half else T_s, 2 * t + 2)
                        for i in range(HM):
                            cols = slice((half * HM + i) * P, (half * HM + i + 1) * P)
                            last = nc.tensor.matmul(bank_of(L, 2 + half)[:, i * P:(i + 1) * P], kg[:, t % 2, cols], v[:, t % 2, cols], start=True, stop=True)
                        last.then_inc(stated, 1)

                def output(t):
                    pe.wait_ge(oT_done, 2 * t + 2)
                    pe.wait_ge(masked, 4 * t + 3)
                    for m in range(LM):
                        last = nc.tensor.matmul(bank_of(L, 4, D), oT[:, m, :], L.a1o[:, m, :], start=(m == 0), stop=(m == LM - 1))
                    last.then_inc(summed, 1)

                for what in range(3):
                    project(0, what)
                for t in range(T):
                    turn(t, 0)
                    if t + 1 < T:
                        project(t + 1, 0, (0,))
                    turn(t, 1)
                    if t + 1 < T:
                        project(t + 1, 0, (1,))
                    scores(t)
                    if t + 1 < T:
                        project(t + 1, 1)
                    mix(t)
                    if t + 1 < T:
                        project(t + 1, 2)
                        update(t)
                    if t >= 1:
                        if t + 1 < T:
                            pe.wait_ge(state_done, 4 * t + 4)
                        tail.turn_tile(pe, t - 1, 3)
                    output(t)
                tail.turn_tile(pe, T - 1, 2)

            @block.scalar
            def _(act):
                def square(t, what, half):
                    n = 4 * t + 2 * what + half
                    act.wait_ge(made, 6 * t + 2 * what + half + 1)
                    if n >= 2:
                        act.wait_ge(sum_done, n - 1)
                    nc.scalar.activation(sq[:, n % 2, :], projected(t, what, half), ACT.Square).then_inc(squared, 1)

                def root(t, what):
                    for half in range(2):
                        n = 4 * t + 2 * what + half
                        act.wait_ge(sum_done, n + 1)
                        nc.scalar.activation(std[:, n, :], ssum[:, n, :], ACT.Sqrt, scale=1.0 / LH, bias=L.eps[:, :]).then_inc(rooted, 1)

                def norm(t, what):
                    for half in range(2):
                        square(t, what, half)
                    root(t, what)

                def take_v(t):
                    for half in range(2):
                        act.wait_ge(made, 6 * t + 5 + half)
                        if t >= 2 and half == 0:
                            act.wait_ge(stated, 2 * (t - 1))
                        nc.scalar.copy(v[:, t % 2, half * HW:(half + 1) * HW], projected(t, 2, half)).then_inc(v_done, 1)

                norm(0, 0)
                norm(0, 1)
                take_v(0)
                for t in range(T):
                    for what in range(2):
                        act.wait_ge(turned, 4 * t + 2 * what + 1)
                        nc.scalar.activation(qkT[:, what, 0:HM, :], bank_of(L, 2).rearrange("p (m n) -> p m n", n=P), ACT.Identity,
                                             scale=L.gains[:, 2 * what:2 * what + 1], bias=L.gains[:, 2 * what + 1:2 * what + 2]).then_inc(T_s, 1)
                        if t + 1 < T:
                            square(t + 1, 0, what)
                    if t + 1 < T:
                        root(t + 1, 0)
                    if t >= 1:
                        tail.root(act, t - 1)
                    if t + 1 < T:
                        norm(t + 1, 1)
                    for half in range(2):
                        act.wait_ge(mixed_in, 2 * t + half + 1)
                        nc.scalar.copy(oT[:, half * HM:(half + 1) * HM, :], bank_of(L, 6 + half).rearrange("p (m n) -> p m n", n=P)).then_inc(oT_done, 1)
                    if t + 1 < T:
                        take_v(t + 1)
                    if t >= 1:
                        tail.copy_turned(act, t - 1, 3)
                tail.root(act, T - 1)
                tail.copy_turned(act, T - 1, 2)

            @block.gpsimd
            def _(pool):
                nc.gpsimd.memset(state[:, :, :], 0.0).then_inc(cleared, 1)
                for t in range(T - 1):
                    for half in range(2):
                        n = 2 * t + half
                        cols = slice(half * HW, (half + 1) * HW)
                        pool.wait_ge(normed, 4 * t + 3 + half)
                        if t >= 2 and half == 0:
                            pool.wait_ge(stated, 2 * (t - 1))
                        gamma, beta = (L.k_gains[:, i:i + 1, :].to_broadcast((P, HW // LH, LH)) for i in range(2))
                        nc.gpsimd.tensor_tensor(heads(kg[:, t % 2, cols]), heads(tok[:, t % 2, 1, cols]), gamma, ALU.mult).then_inc(kg_half, 1)
                        pool.wait_ge(kg_half, n + 1)
                        nc.gpsimd.tensor_tensor(heads(kg[:, t % 2, cols]), heads(kg[:, t % 2, cols]), beta, ALU.add).then_inc(kg_done, 1)

            @block.vector
            def _(dve):
                step = Chain(dve, tail.vec)

                def squares(t, what, half):
                    n = 4 * t + 2 * what + half
                    dve.wait_ge(squared, n + 1)
                    nc.vector.tensor_reduce(ssum[:, n, :], heads(sq[:, n % 2, :]), AX.X, ALU.add).then_inc(sum_done, 1)

                def divide(t, what):
                    for half in range(2):
                        n = 4 * t + 2 * what + half
                        dve.wait_ge(rooted, n + 1)
                        step(nc.vector.reciprocal(rstd[:, n, :], std[:, n, :]))
                        if t >= 2:
                            dve.wait_ge(turned, 4 * (t - 1))
                            dve.wait_ge(kg_done, 2 * (t - 1))
                        nc.vector.tensor_tensor(heads(tok[:, t % 2, what, half * HW:(half + 1) * HW]), heads(projected(t, what, half)),
                                                rstd[:, n, :].rearrange("p (h a) -> p h a", a=1).to_broadcast((P, HW // LH, LH)), ALU.mult).then_inc(normed, 1)

                for what in range(2):
                    for half in range(2):
                        squares(0, what, half)
                    divide(0, what)
                for t in range(T):
                    for what in range(2):
                        dve.wait_ge(turned, 4 * t + 2 * what + 2)
                        nc.vector.tensor_scalar(qkT[:, what, HM:LM, :], bank_of(L, 3).rearrange("p (m n) -> p m n", n=P),
                                                L.gains[:, 2 * what:2 * what + 1], L.gains[:, 2 * what + 1:2 * what + 2], ALU.mult, ALU.add).then_inc(T_v, 1)
                        if t + 1 < T:
                            squares(t + 1, 0, what)
                    for n in range(4):
                        dve.wait_ge(scored, 4 * t + n + 1)
                        nc.vector.tensor_tensor(aT[:, n // 2, n % 2, :, :], bank_of(L, 4 + n % 2).rearrange("p (m n) -> p m n", n=P),
                                                L.causal[:, :].rearrange("p (a n) -> p a n", a=1).to_broadcast((P, HM, P)), ALU.mult).then_inc(masked, 1)
                        if n == 1 and t + 1 < T:
                            divide(t + 1, 0)
                    if t + 1 < T:
                        for half in range(2):
                            squares(t + 1, 1, half)
                        divide(t + 1, 1)
                    if t >= 1:
                        tail.norm(dve, t - 1)
                    if t + 1 < T:
                        for half in range(2):
                            dve.wait_ge(stated, 2 * t + half + 1)
                            for j in range(2):
                                rows = slice(j * LH, (j + 1) * LH)
                                new = bank_of(L, 2 + half)[rows, :].rearrange("p (m n) -> p m n", n=P)[:, :, rows]
                                old = state[rows, half * HM:(half + 1) * HM, rows]
                                if t == 0:
                                    dve.wait_ge(cleared, 1)
                                    nc.vector.tensor_copy(old, new).then_inc(state_done, 1)
                                else:
                                    nc.vector.tensor_tensor(old, old, new, ALU.add).then_inc(state_done, 1)
                    dve.wait_ge(summed, t + 1)
                    nc.vector.tensor_tensor(res[:, t, :], bank_of(L, 4, D), L.x_tok[:, t, :], ALU.add).then_inc(tail.added, 1)
                    dve.wait_ge(tail.added, t + 1)
                    tail.stats_of(step, t)
                tail.norm(dve, T - 1)


def cross_attention(nc, a, L):
    with Stage(nc, "cross", L.layer) as st:
        qS, kS = st.sb("qS", [P, H // 2, S], F32R), st.sb("kS", [P, H // 2, SC], F32R)
        v = st.sb("v", [P, CT, H, HD + 1])

        def bias_of(i):
            return lambda m: L.x1bqk[:, i, m:m + 1]

        mask = [st.sb("mask", [P, SC])[:, :], L.x_T[:, :, :].rearrange("p k n -> p (k n)")]
        mask_in, mask_done = [st.sem("mask_in0"), st.sem("mask_in1")], st.sem("mask_done")
        CHUNKS = 4

        def load(sp, t):
            sp.dma_start(mask[t % 2], a["mask_SxS2_fk1"][t * P:(t + 1) * P, :]).then_inc(mask_in[t % 2], 16)

        def load_rest(sp, masked):
            for t in range(1, T):
                if t >= 2:
                    sp.wait_ge(masked, H * (t - 1))
                load(sp, t)

        def scale(pool, t, c):
            pool.wait_ge(mask_in[t % 2], 16 * (t // 2 + 1))
            part = mask[t % 2][:, c * SC // CHUNKS:(c + 1) * SC // CHUNKS]
            nc.gpsimd.tensor_scalar(part, part, NEG, None, ALU.mult).then_inc(mask_done, 1)

        def scale_rest(pool, u):
            t, c = u // H + 1, u % H - H // 2
            if 1 <= t < T and 0 <= c < CHUNKS:
                scale(pool, t, c)

        def mask_ready(dve, t, hs):
            if hs[0] == 0:
                dve.wait_ge(mask_done, CHUNKS * (t + 1))

        project_heads(nc, st, L, "cross_project", (L.x1q, L.x_T, bias_of(0), qS), (L.x1k, L.ctx_T, bias_of(1), kS),
                      (L.x1v, L.ctx_T, L.x1bv, v), sync=lambda sp: load(sp, 0), pool=lambda pool: [scale(pool, 0, c) for c in range(CHUNKS)])
        rest = st.sb("sc", [P, 2, SC])
        sc = [L.ctx_T[:, 0, :], L.ctx_T[:, 1, :], rest[:, 0, :], rest[:, 1, :]]
        attend(nc, st, L, "cross", qS, kS, v, sc, 1, lambda t: (0, CT), lambda t: mask[t % 2], 8,
               sync=load_rest, before=mask_ready, between=scale_rest)


def experts(nc, a, b, out, L):
    PROD = ((0, 0), (1, 0), (0, 1))
    with Stage(nc, "moe", L.layer) as st:
        def pair(name, shape):
            return [st.sb(f"{name}_{w}", shape, F32R) for w in ("hi", "lo")]
        w1, w2 = st.sb("w1", [P, 2, KD, ED]), st.sb("w2", [P, 2, EM, D])
        w1p, w2p = pair("w1", [P, 2, KD, ED]), pair("w2", [P, 2, EM, D])
        w_in = [st.sem("w_in0"), st.sem("w_in1")]
        w1_hi, w2_hi, w1_lo, w2_lo = (st.sem(n) for n in ("w1_hi", "w2_hi", "w1_lo", "w2_lo"))

        def load(sp, e):
            sp.dma_start(w1[:, e % 2, :, :], a["L1_ffn_W1"][e].rearrange("(k p) n -> p k n", p=P)).then_inc(w_in[e % 2], 16)
            sp.dma_start(w2[:, e % 2, :, :], a["L1_ffn_W2"][e].rearrange("(k p) n -> p k n", p=P)).then_inc(w_in[e % 2], 16)

        def high_w1(act, e):
            act.wait_ge(w_in[e % 2], 32 * (e // 2 + 1))
            nc.scalar.copy(w1p[0][:, e % 2, :, :], w1[:, e % 2, :, :]).then_inc(w1_hi, 1)

        def low_w1(pool, e):
            pool.wait_ge(w1_hi, e + 1)
            nc.gpsimd.tensor_tensor(w1p[1][:, e % 2, :, :], w1[:, e % 2, :, :], w1p[0][:, e % 2, :, :].bitcast(F32), ALU.subtract).then_inc(w1_lo, 1)

        def high_first(t):
            if t == 0:
                high_w1(nc.scalar, 0)

        def load_first(sp):
            for e in range(2):
                load(sp, e)

        project_norm(nc, "x1p", L, L.x1o, L.x1bo, sync=load_first, scalar=high_first, pool=lambda pool: low_w1(pool, 0))

        x2 = pair("x", [P, KD, S])
        full = st.sb("full", [P, 4, S])
        hp = pair("h", [P, 2, EM, S])
        logit, prob, rest, top8, cw = (st.sb(n, [P, T, E]) for n in ("logit", "prob", "rest", "top8", "cw"))
        lmax, lden = st.sb("lmax", [P, T]), st.sb("lden", [P, T])
        cwT = st.sb("cwT", [E, T, P])
        acc = L.mixed
        names = ("x_hi", "x_lo", "routed", "shifted", "exped", "cw_done", "cw_turned", "cwT_done", "biased", "acc_done",
                 "made", "relued", "hi_done", "lo_done", "summed")
        (x_hi, x_lo, routed, shifted, exped, cw_done, cw_turned, cwT_done, biased, acc_done,
         made, relued, hi_done, lo_done, summed) = (st.sem(n) for n in names)
        tail = NormTail(nc, st, L, acc, turned_banks=None)
        stored = st.sem("stored")

        def place(e, t):
            return (e + (e > 0)) * T + t

        with nc.Block("experts") as block:
            @block.sync
            def _(sp):
                for e in range(2, E):
                    sp.wait_ge(w1_lo, e - 1)
                    sp.wait_ge(w2_lo, e - 1)
                    load(sp, e)
                for t in range(T):
                    sp.wait_ge(tail.new_x, t + 1)
                    sp.dma_start(out[bass.ds(b, 1), t * P:(t + 1) * P, :].rearrange("a p d -> p (a d)"), L.x_tok[:, t, :]).then_inc(stored, 16)
                sp.wait_ge(stored, 16 * T)

            @block.gpsimd
            def _(pool):
                for e in range(E):
                    if e + 1 < E:
                        low_w1(pool, e + 1)
                    pool.wait_ge(w2_hi, e + 1)
                    nc.gpsimd.tensor_tensor(w2p[1][:, e % 2, :, :], w2[:, e % 2, :, :], w2p[0][:, e % 2, :, :].bitcast(F32), ALU.subtract).then_inc(w2_lo, 1)

            @block.tensor
            def _(pe):
                def up(e):
                    pe.wait_ge(w1_lo, e + 1)
                    for m in range(EM):
                        n = e * EM + m
                        if n >= 4:
                            pe.wait_ge(relued, n - 3)
                        for k in range(KD):
                            for i, (p, q) in enumerate(PROD):
                                if n == 0 and i == 2:
                                    pe.wait_ge(x_lo, 1)
                                last = nc.tensor.matmul(bank_of(L, n % 4), w1p[p][:, e % 2, k, m * P:(m + 1) * P], x2[q][:, k, :],
                                                        start=(k == 0 and i == 0), stop=(k == KD - 1 and i == 2))
                        last.then_inc(made, 1)

                def down(e):
                    pe.wait_ge(w2_lo, e + 1)
                    for t in range(T):
                        n = place(e, t)
                        if n >= 4:
                            pe.wait_ge(acc_done, n - 3)
                        for k in range(EM):
                            if t == 0:
                                pe.wait_ge(lo_done, e * EM + k + 1)
                            for i, (p, q) in enumerate(PROD):
                                last = nc.tensor.matmul(bank_of(L, 4 + n % 4, D), hp[p][:, e % 2, k, t * P:(t + 1) * P], w2p[q][:, e % 2, k, :],
                                                        start=(k == 0 and i == 0), stop=(k == EM - 1 and i == 2))
                        last.then_inc(summed, 1)

                pe.wait_ge(x_hi, 1)
                up(0)
                for t in range(T):
                    o = bank_of(L, 4)[:, t * E:(t + 1) * E]
                    nc.tensor.matmul(o, L.ones[:, :], L.br[:, :], start=True, stop=False)
                    for k in range(KD):
                        last = nc.tensor.matmul(o, L.x_T[:, k, t * P:(t + 1) * P], L.wr[:, k, :], start=False, stop=(k == KD - 1))
                    last.then_inc(routed, 1)
                up(1)
                pe.wait_ge(shifted, T)
                down(0)
                pe.wait_ge(acc_done, 1)
                for t in range(T):
                    pe.wait_ge(cw_done, t + 1)
                    nc.tensor.transpose(bank_of(L, 4)[0:E, t * P:(t + 1) * P], cw[:, t, :], L.ident[:, :]).then_inc(cw_turned, 1)
                up(2)
                pe.wait_ge(cwT_done, 1)
                for t in range(T):
                    pe.wait_ge(acc_done, t + 1)
                    nc.tensor.matmul(bank_of(L, 4 + t, D), cwT[:, t, :], L.b2[:, :], start=True, stop=True).then_inc(biased, 1)
                down(1)
                for e in range(3, E):
                    up(e)
                    down(e - 1)
                down(E - 1)

            @block.scalar
            def _(act):
                def relu(n):
                    act.wait_ge(made, n + 1)
                    if n >= 4:
                        act.wait_ge(lo_done, n - 3)
                    nc.scalar.activation(full[:, n % 4, :], bank_of(L, n % 4), ACT.Relu, bias=L.b1[:, n:n + 1]).then_inc(relued, 1)
                    act.wait_ge(relued, n + 1)
                    e, m = n // EM, n % EM
                    if e >= 2:
                        act.wait_ge(summed, T * (e - 1))
                    nc.scalar.copy(hp[0][:, e % 2, m, :], full[:, n % 4, :]).then_inc(hi_done, 1)

                nc.scalar.copy(x2[0][:, :, :], L.x_T[:, :, :]).then_inc(x_hi, 1)
                high_w1(act, 1)
                for e in range(E):
                    if e == 2:
                        act.wait_ge(cw_turned, T)
                        nc.scalar.copy(cwT[:, :, :], bank_of(L, 4)[0:E, :].rearrange("e (t p) -> e t p", p=P)).then_inc(cwT_done, 1)
                    for m in range(EM):
                        relu(e * EM + m)
                    if e == 0:
                        for t in range(T):
                            act.wait_ge(shifted, t + 1)
                            nc.scalar.activation(prob[:, t, :], logit[:, t, :], ACT.Exp, accum_out=lden[:, t:t + 1]).then_inc(exped, 1)
                    if 1 <= e < E - 1:
                        act.wait_ge(made, EM * e)
                        high_w1(act, e + 1)
                tail.finish(act, turned=False)

            @block.vector
            def _(dve):
                step = Chain(dve, tail.vec)
                dve.wait_ge(x_hi, 1)
                nc.vector.tensor_tensor(x2[1][:, :, :], L.x_T[:, :, :], x2[0][:, :, :].bitcast(F32), ALU.subtract).then_inc(x_lo, 1)
                def low(n):
                    dve.wait_ge(hi_done, n + 1)
                    e, m = n // EM, n % EM
                    nc.vector.tensor_tensor(hp[1][:, e % 2, m, :], full[:, n % 4, :], hp[0][:, e % 2, m, :].bitcast(F32), ALU.subtract).then_inc(lo_done, 1)

                def add(e, t):
                    n = place(e, t)
                    dve.wait_ge(summed, e * T + t + 1)
                    if n >= 1:
                        dve.wait_ge(acc_done, n)
                    nc.vector.scalar_tensor_tensor(out=acc[:, t, :], in0=bank_of(L, 4 + n % 4, D), scalar=cw[:, t, e:e + 1],
                                                   in1=L.x_tok[:, t, :] if e == 0 else acc[:, t, :],
                                                   op0=ALU.mult, op1=ALU.add).then_inc(acc_done, 1)

                def high_w2(e):
                    dve.wait_ge(w_in[e % 2], 32 * (e // 2 + 1))
                    if e >= 2:
                        dve.wait_ge(summed, T * (e - 1))
                    nc.vector.tensor_copy(w2p[0][:, e % 2, :, :], w2[:, e % 2, :, :]).then_inc(w2_hi, 1)

                high_w2(0)
                for n in range(EM):
                    low(n)
                dve.wait_ge(routed, T)
                step(nc.vector.tensor_copy(logit[:, :, :], bank_of(L, 4, T * E).rearrange("p (t e) -> p t e", e=E)))
                step(nc.vector.tensor_reduce(lmax[:, :], logit[:, :, :], AX.X, ALU.max))
                for t in range(T):
                    nc.vector.tensor_scalar(logit[:, t, :], logit[:, t, :], lmax[:, t:t + 1], None, ALU.subtract).then_inc(shifted, 1)
                dve.wait_ge(exped, T)
                step(nc.vector.reciprocal(lden[:, :], lden[:, :]))
                for t in range(T):
                    step(nc.vector.tensor_scalar(prob[:, t, :], prob[:, t, :], lden[:, t:t + 1], None, ALU.mult))
                    step(nc.vector.max(top8[:, t, :], prob[:, t, :]))
                    step(nc.vector.memset(top8[:, t, 2:E], -1.0))
                    step(nc.vector.match_replace(rest[:, t, :], top8[:, t, :], prob[:, t, :], 0.0))
                    nc.vector.tensor_tensor(cw[:, t, :], prob[:, t, :], rest[:, t, :], ALU.subtract).then_inc(cw_done, 1)
                high_w2(1)
                for n in range(EM, 2 * EM):
                    low(n)
                for t in range(T):
                    add(0, t)
                for e in range(2, E):
                    high_w2(e)
                    for m in range(EM):
                        low(e * EM + m)
                    if e == 2:
                        for t in range(T):
                            dve.wait_ge(biased, t + 1)
                            dve.wait_ge(acc_done, T + t)
                            nc.vector.tensor_tensor(acc[:, t, :], bank_of(L, 4 + t, D), acc[:, t, :], ALU.add).then_inc(acc_done, 1)
                    for t in range(T):
                        add(e - 1, t)
                for t in range(T):
                    add(E - 1, t)
                    dve.wait_ge(acc_done, E * T + t + 1)
                    tail.stats_of(step, t)
                    if t >= 1:
                        tail.norm(dve, t - 1)
                tail.norm(dve, T - 1)


_INS = ["x", "ctx_1024", "itok_BxS_0_511", "mask_SxS2_fk1",
        "L0_attn_Wq", "L0_attn_Wk", "L0_attn_Wv", "L0_attn_Wo", "L0_attn_bo",
        "L0_xattn_Wq", "L0_xattn_Wkv", "L0_xattn_Wo",
        "L0_ffn_k0", "L0_ffn_k1", "L0_ffn_k2", "L0_ffn_s0", "L0_ffn_s1", "L0_ffn_s2",
        "L1_attn_Wq", "L1_attn_Wk", "L1_attn_Wv", "L1_attn_Wo",
        "L1_attn_q_gamma", "L1_attn_q_beta", "L1_attn_k_gamma", "L1_attn_k_beta",
        "L1_xattn_Wq", "L1_xattn_bq", "L1_xattn_Wk", "L1_xattn_bk", "L1_xattn_Wv", "L1_xattn_bv",
        "L1_xattn_Wo", "L1_xattn_bo",
        "L1_ffn_Wr", "L1_ffn_br", "L1_ffn_W1", "L1_ffn_b1", "L1_ffn_W2", "L1_ffn_b2"]


def kernel(**inputs):
    import numpy as _np
    import concourse.bacc as _bacc
    from concourse import mybir as _mybir
    from concourse.bass_utils import run_bass_kernel_spmd as _run

    nc = _bacc.Bacc("TRN2", target_bir_lowering=False, num_devices=1)
    arrays, aps = {}, {}
    for name in _INS:
        v = _np.ascontiguousarray(inputs[name])
        v = v.view(_np.int32) if v.dtype == _np.bool_ else v
        v = v.reshape(1) if v.ndim == 0 else v
        arrays[f"in_{name}"] = v
        aps[name] = nc.dram_tensor(f"in_{name}", v.shape, _mybir.dt.from_np(v.dtype), kind="ExternalInput").ap()
    out = nc.dram_tensor("out_x", (B, S, D), _mybir.dt.float32, kind="ExternalOutput").ap()
    decoder(nc, aps, out)
    return _run(nc, [arrays], core_ids=[0]).results[0]["out_x"]
```
